# Optimizing a Trainium2 kernel written in Bass

```python
import numpy as np
import jax
import jax.numpy as jnp

def _softmax(x, axis=-1):
    return jax.nn.softmax(x, axis=axis)

def _gelu(x):
    return jax.nn.gelu(x, approximate=True)

def _silu(x):
    return jax.nn.silu(x)

def _sigmoid(x):
    return jax.nn.sigmoid(x)

def _layernorm(x, axis=-1, eps=1e-05):
    m = jnp.mean(x, axis=axis, keepdims=True)
    v = jnp.var(x, axis=axis, keepdims=True)
    return (x - m) / jnp.sqrt(v + eps)

def _scatter_add(tgt, idx, src, axis=0):
    return tgt.at[idx].add(src)

def _segment_sum(src, seg, n):
    return jax.ops.segment_sum(src, seg, n)
kernel_name = 'mk_perceiver_d2_seqx_r4_a29689'

def setup_inputs(seed: int=0):
    np.random.seed(seed)
    _w = jnp.asarray

    def _rec_inputs():
        import jax
        import jax.numpy as jnp
        _rk = jax.random.key(seed)
        x = 7.22e-05 + 1 * jax.random.normal(jax.random.fold_in(_rk, 1), (2, 256, 256), jnp.float32)
        _lenS = 256 - jax.random.randint(jax.random.fold_in(_rk, 7), (2,), 0, max(1, 256 // 4) + 1, jnp.int32)
        _lenS2 = 4096 - jax.random.randint(jax.random.fold_in(_rk, 8), (2,), 0, max(1, 4096 // 4) + 1, jnp.int32)
        _ctx_768P = jax.random.normal(jax.random.fold_in(_rk, 11), (2, 16, 192), jnp.float32)
        _ctx_768c = jax.random.dirichlet(jax.random.fold_in(_rk, 511), 0.3 * jnp.ones((16,), jnp.float32), (2, 4096))
        _ctx_768t = jnp.einsum('bsk,bkd->bsd', _ctx_768c, _ctx_768P)
        _ctx_768t = _ctx_768t * jax.lax.rsqrt(jnp.mean(jnp.square(_ctx_768t)) + 1e-12) * 0.953939
        ctx_768 = -0.000191848 + 0.999787 * (_ctx_768t + 0.3 * jax.random.normal(jax.random.fold_in(_rk, 611), (2, 4096, 192), jnp.float32))
        _validS = jnp.arange(256)[None, :] < _lenS[:, None]
        _validS2 = jnp.arange(4096)[None, :] < _lenS2[:, None]
        _causal = jnp.tril(jnp.ones((256, 256), dtype=bool))
        mask_BxS_bf1 = jnp.ones((2, 256), dtype=bool)
        mask_BxS2_bf1 = jnp.ones((2, 4096), dtype=bool)
        return (x, ctx_768, mask_BxS_bf1, mask_BxS2_bf1)
    x, ctx_768, mask_BxS_bf1, mask_BxS2_bf1 = _rec_inputs()

    def _L0_xattn_setup():
        import jax, jax.numpy as jnp
        import numpy as np
        NUM_HEADS = 16
        CLAMP = 10000.0
        key = jax.random.key(seed)
        ks = jax.random.split(key, 8)
        B, Nq, Nkv, Cq, Ckv = (4, 512, 512, 256, 192)
        s_q = 1.0 / np.sqrt(Cq)
        s_kv = 1.0 / np.sqrt(Ckv)
        return {'query': jax.random.normal(ks[0], (B, Nq, Cq), jnp.float32), 'key_value': jax.random.normal(ks[1], (B, Nkv, Ckv), jnp.float32), 'Wq': jax.random.normal(ks[2], (Cq, Cq), jnp.float32) * s_q, 'bq': jnp.zeros((Cq,), jnp.float32), 'Wk': jax.random.normal(ks[3], (Ckv, Cq), jnp.float32) * s_kv, 'bk': jnp.zeros((Cq,), jnp.float32), 'Wv': jax.random.normal(ks[4], (Ckv, Cq), jnp.float32) * s_kv, 'bv': jnp.zeros((Cq,), jnp.float32), 'Wo': jax.random.normal(ks[5], (Cq, Cq), jnp.float32) * s_q, 'bo': jnp.zeros((Cq,), jnp.float32)}
    _L0_xattn_all = _L0_xattn_setup()
    _L0_xattn_in = {k: v for k, v in _L0_xattn_all.items() if k in ('Wq', 'bq', 'Wk', 'bk', 'Wv', 'bv', 'Wo', 'bo')}
    del _L0_xattn_all

    def _L0_attn_setup():
        import jax, jax.numpy as jnp
        import numpy as np
        B, S, D, H, R = (8, 256, 256, 8, 32)
        DH = D // H

        def _lowrank(xh, U, V, b):
            t = jnp.einsum('bshd,hrd->bshr', xh, V)
            return jnp.einsum('bshr,hdr->bshd', t, U) + b
        key = jax.random.key(seed)
        ks = jax.random.split(key, 10)
        p = lambda k, shape: jax.random.normal(k, shape, dtype=jnp.float32) * 0.02
        return {'x': jax.random.normal(ks[0], (B, S, D), dtype=jnp.float32), 'Uq': p(ks[1], (H, DH, R)), 'Vq': p(ks[2], (H, R, DH)), 'bq': p(ks[3], (H, DH)), 'Uk': p(ks[4], (H, DH, R)), 'Vk': p(ks[5], (H, R, DH)), 'bk': p(ks[6], (H, DH)), 'Uv': p(ks[7], (H, DH, R)), 'Vv': p(ks[8], (H, R, DH)), 'bv': p(ks[9], (H, DH))}
    _L0_attn_all = _L0_attn_setup()
    _L0_attn_in = {k: v for k, v in _L0_attn_all.items() if k in ('Uq', 'Vq', 'bq', 'Uk', 'Vk', 'bk', 'Uv', 'Vv', 'bv')}
    del _L0_attn_all

    def _L0_ffn_setup():
        import jax, jax.numpy as jnp
        import numpy as np
        N_EXPERTS = 16
        TOP_K = 4
        HIDDEN = 256
        INTER = 128
        B, S = (2, 256)
        key = jax.random.key(seed)
        k1, k2, k3, k4, k5 = jax.random.split(key, 5)
        return {'hidden_states': jax.random.normal(k1, (B, S, HIDDEN), dtype=jnp.float32), 'gate_w': jax.random.normal(k2, (N_EXPERTS, HIDDEN), dtype=jnp.float32) * 0.02, 'w1': jax.random.normal(k3, (N_EXPERTS, HIDDEN, INTER), dtype=jnp.float32) * 0.02, 'w3': jax.random.normal(k4, (N_EXPERTS, HIDDEN, INTER), dtype=jnp.float32) * 0.02, 'w2': jax.random.normal(k5, (N_EXPERTS, INTER, HIDDEN), dtype=jnp.float32) * 0.02}
    _L0_ffn_all = _L0_ffn_setup()
    _L0_ffn_in = {k: v for k, v in _L0_ffn_all.items() if k in ('gate_w', 'w1', 'w3', 'w2')}
    del _L0_ffn_all

    def _L1_xattn_setup():
        import jax, jax.numpy as jnp
        import numpy as np
        B, T, DT, G, DV = (16, 128, 256, 144, 192)
        H, DH = (4, 32)
        INNER = H * DH
        HID = 4 * DT
        N_STATE = 64
        K_TOP = 32

        def layernorm(x, g, b, eps=1e-05):
            m = x.mean(-1, keepdims=True)
            v = x.var(-1, keepdims=True)
            return (x - m) * jax.lax.rsqrt(v + eps) * g + b

        def s4d(x, log_dt, A_re, A_im, C_re, C_im, D_skip):
            Bb, L, D = x.shape
            dt = jnp.exp(log_dt)
            A = A_re + 1j * A_im
            C = C_re + 1j * C_im
            dtA = dt[:, None] * A
            dC = C * (jnp.exp(dtA) - 1.0) / A
            powers = jnp.exp(dtA[:, :, None] * jnp.arange(L))
            K = 2.0 * jnp.einsum('dn,dnl->dl', dC, powers).real
            n = 2 * L
            Kf = jnp.fft.rfft(K, n=n, axis=-1)
            xf = jnp.fft.rfft(x, n=n, axis=1)
            y = jnp.fft.irfft(xf * Kf.T[None], n=n, axis=1)[:, :L]
            return y + x * D_skip
        key = jax.random.key(seed)
        ks = jax.random.split(key, 16)
        s = 0.02
        inp = {'x_text': jax.random.normal(ks[0], (B, T, DT), jnp.float32), 'x_vision': jax.random.normal(ks[1], (B, G, DV), jnp.float32), 'text_mask': jnp.ones((B, T), bool), 'vision_mask': jnp.ones((B, G), bool), 'Wq': jax.random.normal(ks[2], (DT, INNER), jnp.float32) * s, 'Wk': jax.random.normal(ks[3], (DV, INNER), jnp.float32) * s, 'Wv': jax.random.normal(ks[4], (DV, DT), jnp.float32) * s, 'W_film_in': jax.random.normal(ks[5], (DT, 2 * DT), jnp.float32) * s, 'b_film_in': jnp.zeros((2 * DT,), jnp.float32), 'W_film_out': jax.random.normal(ks[6], (DT, 2 * DT), jnp.float32) * s, 'b_film_out': jnp.zeros((2 * DT,), jnp.float32), 'g_norm_in': jnp.ones((DT,), jnp.float32), 'b_norm_in': jnp.zeros((DT,), jnp.float32), 'g_norm_out': jnp.ones((DT,), jnp.float32), 'b_norm_out': jnp.zeros((DT,), jnp.float32), 'g_ffn': jnp.ones((DT,), jnp.float32), 'b_ffn': jnp.zeros((DT,), jnp.float32), 'W1': jax.random.normal(ks[7], (DT, HID), jnp.float32) * s, 'b1': jnp.zeros((HID,), jnp.float32), 'W2': jax.random.normal(ks[8], (HID, DT), jnp.float32) * s, 'b2': jnp.zeros((DT,), jnp.float32), 'log_dt': jnp.log(0.001) + jax.random.uniform(ks[9], (DT,), jnp.float32) * (jnp.log(0.1) - jnp.log(0.001)), 'A_re': -0.5 * jnp.ones((DT, N_STATE), jnp.float32), 'A_im': jnp.tile(jnp.pi * jnp.arange(N_STATE, dtype=jnp.float32), (DT, 1)), 'C_re': jax.random.normal(ks[10], (DT, N_STATE), jnp.float32) * 0.5 ** 0.5, 'C_im': jax.random.normal(ks[11], (DT, N_STATE), jnp.float32) * 0.5 ** 0.5, 'D_skip': jax.random.normal(ks[12], (DT,), jnp.float32), 'mod_gate': jnp.array(0.5, jnp.float32)}
        return inp
    _L1_xattn_all = _L1_xattn_setup()
    _L1_xattn_in = {k: v for k, v in _L1_xattn_all.items() if k in ('Wq', 'Wk', 'Wv', 'W_film_in', 'b_film_in', 'W_film_out', 'b_film_out', 'g_norm_in', 'b_norm_in', 'g_norm_out', 'b_norm_out', 'g_ffn', 'b_ffn', 'W1', 'b1', 'W2', 'b2', 'log_dt', 'A_re', 'A_im', 'C_re', 'C_im', 'D_skip', 'mod_gate')}
    del _L1_xattn_all

    def _L1_attn_setup():
        import math
        import jax, jax.numpy as jnp
        import numpy as np
        B, L, DIM, HEADS = (4, 512, 256, 8)
        HEAD = DIM // HEADS
        SCALE_BASE = 512.0
        EPS = 1e-05

        def _xpos(x, downscale=False):
            l, dh = (x.shape[-2], x.shape[-1])
            half = dh // 2
            pos = jnp.arange(l, dtype=x.dtype)
            base = (jnp.arange(0, dh, 2, dtype=x.dtype) + 0.4 * dh) / (1.4 * dh)
            scale = base[None, :] ** (pos[:, None] / SCALE_BASE)
            inv_freq = 1.0 / 10000.0 ** (jnp.arange(half, dtype=x.dtype) / half)
            sinusoid = pos[:, None] * inv_freq[None, :]
            sin, cos = (jnp.sin(sinusoid), jnp.cos(sinusoid))
            if downscale:
                scale = 1.0 / scale
            s = jnp.repeat(sin * scale, 2, axis=-1)
            c = jnp.repeat(cos * scale, 2, axis=-1)
            x1, x2 = (x[..., ::2], x[..., 1::2])
            rot = jnp.stack([-x2, x1], axis=-1).reshape(x.shape)
            return x * c + rot * s

        def _decay_mask(l, gammas):
            n = jnp.arange(l)[:, None]
            m = jnp.arange(l)[None, :]
            lg = jnp.log(gammas)
            expo = (n - m).astype(jnp.float32)[None, :, :] * lg[:, None, None]
            return jnp.where((n >= m)[None], jnp.exp(expo), 0.0)
        key = jax.random.key(seed)
        ks = jax.random.split(key, 6)
        d = DIM
        return {'X': jax.random.normal(ks[0], (B, L, DIM), dtype=jnp.float32), 'W_Q': jax.random.normal(ks[1], (HEADS, DIM, HEAD), dtype=jnp.float32) / d, 'W_K': jax.random.normal(ks[2], (HEADS, DIM, HEAD), dtype=jnp.float32) / d, 'W_V': jax.random.normal(ks[3], (HEADS, DIM, HEAD), dtype=jnp.float32) / d, 'W_G': jax.random.normal(ks[4], (DIM, DIM), dtype=jnp.float32) / d, 'W_O': jax.random.normal(ks[5], (DIM, DIM), dtype=jnp.float32) / d, 'gn_weight': jnp.ones((DIM,), dtype=jnp.float32), 'gn_bias': jnp.zeros((DIM,), dtype=jnp.float32)}
    _L1_attn_all = _L1_attn_setup()
    _L1_attn_in = {k: v for k, v in _L1_attn_all.items() if k in ('W_Q', 'W_K', 'W_V', 'W_G', 'W_O', 'gn_weight', 'gn_bias')}
    del _L1_attn_all

    def _L1_ffn_setup():
        import jax, jax.numpy as jnp
        import numpy as np
        key = jax.random.key(seed)
        k_x, k_W, k_b, k_ids, k_w = jax.random.split(key, 5)
        N_ADAPTERS, D_OUT, D_IN = (32, 256, 256)
        B, S = (2, 512)
        K = 8
        x = jax.random.normal(k_x, (B, S, D_IN), dtype=jnp.float32)
        W = jax.random.normal(k_W, (N_ADAPTERS, D_OUT, D_IN), dtype=jnp.float32)
        b = jax.random.normal(k_b, (N_ADAPTERS, D_OUT), dtype=jnp.float32)
        ids = jax.random.randint(k_ids, (K,), 0, N_ADAPTERS, dtype=jnp.int64)
        weights = jax.random.uniform(k_w, (K,), dtype=jnp.float32)
        return {'x': x, 'W': W, 'b': b, 'ids': ids, 'weights': weights}
    _L1_ffn_all = _L1_ffn_setup()
    _L1_ffn_in = {k: v for k, v in _L1_ffn_all.items() if k in ('W', 'b', 'ids', 'weights')}
    del _L1_ffn_all
    return {'x': x, 'ctx_768': ctx_768, 'mask_BxS_bf1': mask_BxS_bf1, 'mask_BxS2_bf1': mask_BxS2_bf1, 'L0_xattn_Wq': _L0_xattn_in['Wq'], 'L0_xattn_bq': _L0_xattn_in['bq'], 'L0_xattn_Wk': _L0_xattn_in['Wk'], 'L0_xattn_bk': _L0_xattn_in['bk'], 'L0_xattn_Wv': _L0_xattn_in['Wv'], 'L0_xattn_bv': _L0_xattn_in['bv'], 'L0_xattn_Wo': _L0_xattn_in['Wo'], 'L0_xattn_bo': _L0_xattn_in['bo'], 'L0_attn_Uq': _L0_attn_in['Uq'], 'L0_attn_Vq': _L0_attn_in['Vq'], 'L0_attn_bq': _L0_attn_in['bq'], 'L0_attn_Uk': _L0_attn_in['Uk'], 'L0_attn_Vk': _L0_attn_in['Vk'], 'L0_attn_bk': _L0_attn_in['bk'], 'L0_attn_Uv': _L0_attn_in['Uv'], 'L0_attn_Vv': _L0_attn_in['Vv'], 'L0_attn_bv': _L0_attn_in['bv'], 'L0_ffn_gate_w': _L0_ffn_in['gate_w'], 'L0_ffn_w1': _L0_ffn_in['w1'], 'L0_ffn_w3': _L0_ffn_in['w3'], 'L0_ffn_w2': _L0_ffn_in['w2'], 'L1_xattn_Wq': _L1_xattn_in['Wq'], 'L1_xattn_Wk': _L1_xattn_in['Wk'], 'L1_xattn_Wv': _L1_xattn_in['Wv'], 'L1_xattn_W_film_in': _L1_xattn_in['W_film_in'], 'L1_xattn_b_film_in': _L1_xattn_in['b_film_in'], 'L1_xattn_W_film_out': _L1_xattn_in['W_film_out'], 'L1_xattn_b_film_out': _L1_xattn_in['b_film_out'], 'L1_xattn_g_norm_in': _L1_xattn_in['g_norm_in'], 'L1_xattn_b_norm_in': _L1_xattn_in['b_norm_in'], 'L1_xattn_g_norm_out': _L1_xattn_in['g_norm_out'], 'L1_xattn_b_norm_out': _L1_xattn_in['b_norm_out'], 'L1_xattn_g_ffn': _L1_xattn_in['g_ffn'], 'L1_xattn_b_ffn': _L1_xattn_in['b_ffn'], 'L1_xattn_W1': _L1_xattn_in['W1'], 'L1_xattn_b1': _L1_xattn_in['b1'], 'L1_xattn_W2': _L1_xattn_in['W2'], 'L1_xattn_b2': _L1_xattn_in['b2'], 'L1_xattn_log_dt': _L1_xattn_in['log_dt'], 'L1_xattn_A_re': _L1_xattn_in['A_re'], 'L1_xattn_A_im': _L1_xattn_in['A_im'], 'L1_xattn_C_re': _L1_xattn_in['C_re'], 'L1_xattn_C_im': _L1_xattn_in['C_im'], 'L1_xattn_D_skip': _L1_xattn_in['D_skip'], 'L1_xattn_mod_gate': _L1_xattn_in['mod_gate'], 'L1_attn_W_Q': _L1_attn_in['W_Q'], 'L1_attn_W_K': _L1_attn_in['W_K'], 'L1_attn_W_V': _L1_attn_in['W_V'], 'L1_attn_W_G': _L1_attn_in['W_G'], 'L1_attn_W_O': _L1_attn_in['W_O'], 'L1_attn_gn_weight': _L1_attn_in['gn_weight'], 'L1_attn_gn_bias': _L1_attn_in['gn_bias'], 'L1_ffn_W': _L1_ffn_in['W'], 'L1_ffn_b': _L1_ffn_in['b'], 'L1_ffn_ids': _L1_ffn_in['ids'], 'L1_ffn_weights': _L1_ffn_in['weights']}

def reference(x, ctx_768, mask_BxS_bf1, mask_BxS2_bf1, L0_xattn_Wq, L0_xattn_bq, L0_xattn_Wk, L0_xattn_bk, L0_xattn_Wv, L0_xattn_bv, L0_xattn_Wo, L0_xattn_bo, L0_attn_Uq, L0_attn_Vq, L0_attn_bq, L0_attn_Uk, L0_attn_Vk, L0_attn_bk, L0_attn_Uv, L0_attn_Vv, L0_attn_bv, L0_ffn_gate_w, L0_ffn_w1, L0_ffn_w3, L0_ffn_w2, L1_xattn_Wq, L1_xattn_Wk, L1_xattn_Wv, L1_xattn_W_film_in, L1_xattn_b_film_in, L1_xattn_W_film_out, L1_xattn_b_film_out, L1_xattn_g_norm_in, L1_xattn_b_norm_in, L1_xattn_g_norm_out, L1_xattn_b_norm_out, L1_xattn_g_ffn, L1_xattn_b_ffn, L1_xattn_W1, L1_xattn_b1, L1_xattn_W2, L1_xattn_b2, L1_xattn_log_dt, L1_xattn_A_re, L1_xattn_A_im, L1_xattn_C_re, L1_xattn_C_im, L1_xattn_D_skip, L1_xattn_mod_gate, L1_attn_W_Q, L1_attn_W_K, L1_attn_W_V, L1_attn_W_G, L1_attn_W_O, L1_attn_gn_weight, L1_attn_gn_bias, L1_ffn_W, L1_ffn_b, L1_ffn_ids, L1_ffn_weights):
    import jax
    import jax.numpy as jnp

    def _L0_xattn_ref(query, key_value, Wq, bq, Wk, bk, Wv, bv, Wo, bo):
        import jax, jax.numpy as jnp
        import numpy as np
        NUM_HEADS = 16
        CLAMP = 10000.0
        B, Nq, Cq = query.shape
        Nkv = key_value.shape[1]
        H = NUM_HEADS
        D = Cq // H
        scale = D ** (-0.5)
        q = (query @ Wq + bq).reshape(B, Nq, H, D).transpose(0, 2, 1, 3)
        k = (key_value @ Wk + bk).reshape(B, Nkv, H, D).transpose(0, 2, 1, 3)
        v = (key_value @ Wv + bv).reshape(B, Nkv, H, D).transpose(0, 2, 1, 3)
        attn = jnp.einsum('bhqd,bhkd->bhqk', q, k) * scale
        attn = jnp.clip(attn, -CLAMP, CLAMP)
        attn = jax.nn.softmax(attn, axis=-1)
        attn = jnp.where(jnp.any(jnp.isnan(attn)), jnp.asarray(1.0 / Nkv, attn.dtype), attn)
        x = jnp.einsum('bhqk,bhkd->bqhd', attn, v).reshape(B, Nq, Cq)
        return x @ Wo + bo

    def _L0_attn_ref(x, Uq, Vq, bq, Uk, Vk, bk, Uv, Vv, bv):
        import jax, jax.numpy as jnp
        import numpy as np
        B, S, D, H, R = (8, 256, 256, 8, 32)
        DH = D // H

        def _lowrank(xh, U, V, b):
            t = jnp.einsum('bshd,hrd->bshr', xh, V)
            return jnp.einsum('bshr,hdr->bshd', t, U) + b
        b_, s_, _ = x.shape
        xh = x.reshape(b_, s_, H, DH)
        q = _lowrank(xh, Uq, Vq, bq)
        k = _lowrank(xh, Uk, Vk, bk)
        v = _lowrank(xh, Uv, Vv, bv)
        scores = jnp.einsum('bqhd,bkhd->bhqk', q, k) / DH ** 0.5
        attn = jax.nn.softmax(scores, axis=-1)
        out = jnp.einsum('bhqk,bkhd->bqhd', attn, v)
        return out.reshape(b_, s_, D)

    def _L0_ffn_ref(hidden_states, gate_w, w1, w3, w2):
        import jax, jax.numpy as jnp
        import numpy as np
        N_EXPERTS = 16
        TOP_K = 4
        HIDDEN = 256
        INTER = 128
        B, S = (2, 256)
        'DeepseekV3 MoE adapter forward: router -> sparse scores -> expert GLU MLP -> combine.'
        b, s, h = hidden_states.shape
        x = hidden_states.reshape(-1, h)
        logits = jnp.einsum('th,eh->te', x, gate_w)
        probs = jax.nn.softmax(logits, axis=-1)
        topk_w, topk_idx = jax.lax.top_k(probs, TOP_K)
        topk_w = topk_w / jnp.sum(topk_w, axis=-1, keepdims=True)
        one_hot = (topk_idx[..., None] == jnp.arange(N_EXPERTS)).astype(topk_w.dtype)
        scores = jnp.einsum('tk,tke->te', topk_w, one_hot)
        g = jnp.einsum('th,ehi->tei', x, w1)
        u = jnp.einsum('th,ehi->tei', x, w3)
        act = jax.nn.silu(g) * u
        expert_out = jnp.einsum('tei,eih->teh', act, w2)
        out = jnp.einsum('teh,te->th', expert_out, scores)
        return out.reshape(b, s, h)

    def _L1_xattn_ref(x_text, x_vision, text_mask, vision_mask, Wq, Wk, Wv, W_film_in, b_film_in, W_film_out, b_film_out, g_norm_in, b_norm_in, g_norm_out, b_norm_out, g_ffn, b_ffn, W1, b1, W2, b2, log_dt, A_re, A_im, C_re, C_im, D_skip, mod_gate):
        import jax, jax.numpy as jnp
        import numpy as np
        B, T, DT, G, DV = (16, 128, 256, 144, 192)
        H, DH = (4, 32)
        INNER = H * DH
        HID = 4 * DT
        N_STATE = 64
        K_TOP = 32

        def layernorm(x, g, b, eps=1e-05):
            m = x.mean(-1, keepdims=True)
            v = x.var(-1, keepdims=True)
            return (x - m) * jax.lax.rsqrt(v + eps) * g + b

        def s4d(x, log_dt, A_re, A_im, C_re, C_im, D_skip):
            Bb, L, D = x.shape
            dt = jnp.exp(log_dt)
            A = A_re + 1j * A_im
            C = C_re + 1j * C_im
            dtA = dt[:, None] * A
            dC = C * (jnp.exp(dtA) - 1.0) / A
            powers = jnp.exp(dtA[:, :, None] * jnp.arange(L))
            K = 2.0 * jnp.einsum('dn,dnl->dl', dC, powers).real
            n = 2 * L
            Kf = jnp.fft.rfft(K, n=n, axis=-1)
            xf = jnp.fft.rfft(x, n=n, axis=1)
            y = jnp.fft.irfft(xf * Kf.T[None], n=n, axis=1)[:, :L]
            return y + x * D_skip
        Bb, Tt, D = x_text.shape
        Gg = x_vision.shape[1]
        Q = (x_text @ Wq).reshape(Bb, Tt, H, DH)
        K = (x_vision @ Wk).reshape(Bb, Gg, H, DH)
        scores = jnp.einsum('bthd,bghd->bhtg', Q, K) / np.sqrt(DH).astype(np.float32)
        scores = jnp.where(vision_mask[:, None, None, :], scores, -jnp.inf)
        topv, topi = jax.lax.top_k(scores, K_TOP)
        probs = jax.nn.softmax(topv, axis=-1)
        bi = jnp.arange(Bb)[:, None, None, None]
        hi = jnp.arange(H)[None, :, None, None]
        ti = jnp.arange(Tt)[None, None, :, None]
        attn = jnp.zeros_like(scores).at[bi, hi, ti, topi].set(probs)
        attn_mean = attn.mean(axis=1)
        V = x_vision @ Wv
        c_t = jnp.einsum('btg,bgd->btd', attn_mean, V)
        c_t = c_t * text_mask[..., None]
        x = layernorm(x_text, g_norm_in, b_norm_in)
        scale_in, shift_in = jnp.split(c_t @ W_film_in + b_film_in, 2, axis=-1)
        x = x * (1.0 + mod_gate * scale_in) + mod_gate * shift_in
        y = s4d(x, log_dt, A_re, A_im, C_re, C_im, D_skip)
        scale_out, shift_out = jnp.split(c_t @ W_film_out + b_film_out, 2, axis=-1)
        y = y * (1.0 + mod_gate * scale_out) + mod_gate * shift_out
        xt = x_text + y
        h = layernorm(xt, g_ffn, b_ffn)
        h = jax.nn.gelu(h @ W1 + b1, approximate=False) @ W2 + b2
        xt = xt + h
        return layernorm(xt, g_norm_out, b_norm_out)

    def _L1_attn_ref(X, W_Q, W_K, W_V, W_G, W_O, gn_weight, gn_bias):
        import math
        import jax, jax.numpy as jnp
        import numpy as np
        B, L, DIM, HEADS = (4, 512, 256, 8)
        HEAD = DIM // HEADS
        SCALE_BASE = 512.0
        EPS = 1e-05

        def _xpos(x, downscale=False):
            l, dh = (x.shape[-2], x.shape[-1])
            half = dh // 2
            pos = jnp.arange(l, dtype=x.dtype)
            base = (jnp.arange(0, dh, 2, dtype=x.dtype) + 0.4 * dh) / (1.4 * dh)
            scale = base[None, :] ** (pos[:, None] / SCALE_BASE)
            inv_freq = 1.0 / 10000.0 ** (jnp.arange(half, dtype=x.dtype) / half)
            sinusoid = pos[:, None] * inv_freq[None, :]
            sin, cos = (jnp.sin(sinusoid), jnp.cos(sinusoid))
            if downscale:
                scale = 1.0 / scale
            s = jnp.repeat(sin * scale, 2, axis=-1)
            c = jnp.repeat(cos * scale, 2, axis=-1)
            x1, x2 = (x[..., ::2], x[..., 1::2])
            rot = jnp.stack([-x2, x1], axis=-1).reshape(x.shape)
            return x * c + rot * s

        def _decay_mask(l, gammas):
            n = jnp.arange(l)[:, None]
            m = jnp.arange(l)[None, :]
            lg = jnp.log(gammas)
            expo = (n - m).astype(jnp.float32)[None, :, :] * lg[:, None, None]
            return jnp.where((n >= m)[None], jnp.exp(expo), 0.0)
        b, l, d = X.shape
        h = W_Q.shape[0]
        gammas = 1.0 - jnp.exp(jnp.linspace(math.log(1.0 / 32.0), math.log(1.0 / 512.0), h)).astype(jnp.float32)
        Q = jnp.einsum('bld,hde->bhle', X, W_Q)
        K = jnp.einsum('bld,hde->bhle', X, W_K)
        V = jnp.einsum('bld,hdv->bhlv', X, W_V)
        Q = _xpos(Q)
        K = _xpos(K, downscale=True)
        D = _decay_mask(l, gammas).astype(X.dtype)
        scores = jnp.einsum('bhle,bhme->bhlm', Q, K) * D[None]
        Y = jnp.einsum('bhlm,bhmv->bhlv', scores, V)
        mean = Y.mean(axis=-1, keepdims=True)
        var = Y.var(axis=-1, keepdims=True)
        Yn = (Y - mean) * jax.lax.rsqrt(var + EPS)
        Yn = jnp.transpose(Yn, (0, 2, 1, 3)).reshape(b, l, -1)
        Yn = Yn * gn_weight + gn_bias
        G = X @ W_G
        out = G * jax.nn.sigmoid(G) * Yn @ W_O
        return out

    def _L1_ffn_ref(x, W, b, ids, weights):
        import jax, jax.numpy as jnp
        import numpy as np
        Wsel = W[ids]
        bsel = b[ids]
        out = jnp.einsum('k,kod,bsd->bso', weights, Wsel, x)
        out = out + jnp.einsum('k,ko->o', weights, bsel)
        return out
    x = x + _L0_xattn_ref(_layernorm(x, axis=-1), ctx_768, L0_xattn_Wq, L0_xattn_bq, L0_xattn_Wk, L0_xattn_bk, L0_xattn_Wv, L0_xattn_bv, L0_xattn_Wo, L0_xattn_bo)
    x = x + _L0_attn_ref(_layernorm(x, axis=-1), L0_attn_Uq, L0_attn_Vq, L0_attn_bq, L0_attn_Uk, L0_attn_Vk, L0_attn_bk, L0_attn_Uv, L0_attn_Vv, L0_attn_bv)
    x = x + _L0_ffn_ref(_layernorm(x, axis=-1), L0_ffn_gate_w, L0_ffn_w1, L0_ffn_w3, L0_ffn_w2)
    x = x + _L1_xattn_ref(_layernorm(x, axis=-1), ctx_768, mask_BxS_bf1, mask_BxS2_bf1, L1_xattn_Wq, L1_xattn_Wk, L1_xattn_Wv, L1_xattn_W_film_in, L1_xattn_b_film_in, L1_xattn_W_film_out, L1_xattn_b_film_out, L1_xattn_g_norm_in, L1_xattn_b_norm_in, L1_xattn_g_norm_out, L1_xattn_b_norm_out, L1_xattn_g_ffn, L1_xattn_b_ffn, L1_xattn_W1, L1_xattn_b1, L1_xattn_W2, L1_xattn_b2, L1_xattn_log_dt, L1_xattn_A_re, L1_xattn_A_im, L1_xattn_C_re, L1_xattn_C_im, L1_xattn_D_skip, L1_xattn_mod_gate)
    x = x + _L1_attn_ref(_layernorm(x, axis=-1), L1_attn_W_Q, L1_attn_W_K, L1_attn_W_V, L1_attn_W_G, L1_attn_W_O, L1_attn_gn_weight, L1_attn_gn_bias)
    x = x + _L1_ffn_ref(_layernorm(x, axis=-1), L1_ffn_W, L1_ffn_b, L1_ffn_ids, L1_ffn_weights)
    return x

_drawn_inputs = setup_inputs


def setup_inputs(seed=0):
    import zlib

    import numpy as np

    out = dict(_drawn_inputs(seed))
    spreads = {'L0_xattn_bq': (0.0, 0.404),
     'L0_xattn_bk': (0.0, 2.0),
     'L0_xattn_bv': (0.0, 0.1),
     'L0_xattn_bo': (0.0, 0.1),
     'L1_xattn_b_film_in': (0.0, 0.771),
     'L1_xattn_b_film_out': (0.0, 1.032),
     'L1_xattn_g_norm_in': (1.0, 0.6),
     'L1_xattn_b_norm_in': (0.0, 0.496),
     'L1_xattn_g_norm_out': (1.0, 0.538),
     'L1_xattn_b_norm_out': (0.0, 0.446),
     'L1_xattn_g_ffn': (1.0, 0.6),
     'L1_xattn_b_ffn': (0.0, 2.0),
     'L1_xattn_b1': (0.0, 2.0),
     'L1_xattn_b2': (0.0, 0.965),
     'L1_xattn_A_re': (-0.5, 0.6),
     'L1_attn_gn_weight': (1.0, 0.6),
     'L1_attn_gn_bias': (0.0, 2.0)}
    factors = {'L0_attn_Uq': 8.0,
     'L0_attn_Vq': 8.0,
     'L0_attn_bq': 8.0,
     'L0_attn_Uk': 8.0,
     'L0_attn_Vk': 8.0,
     'L0_attn_bk': 64.0,
     'L0_attn_Uv': 8.0,
     'L0_attn_Vv': 8.0,
     'L0_attn_bv': 3.021,
     'L0_ffn_gate_w': 8.0,
     'L0_ffn_w1': 8.0,
     'L0_ffn_w3': 8.0,
     'L0_ffn_w2': 8.0,
     'L1_xattn_Wq': 4.237,
     'L1_xattn_Wk': 4.359,
     'L1_xattn_Wv': 2.676,
     'L1_xattn_W_film_in': 3.426,
     'L1_xattn_W_film_out': 4.146,
     'L1_attn_W_Q': 8.0,
     'L1_attn_W_K': 8.0,
     'L1_attn_W_V': 8.0,
     'L1_attn_W_G': 8.0,
     'L1_attn_W_O': 8.0,
     'L1_xattn_W1': 3.05}
    for name, (base, spread) in spreads.items():
        noise = np.random.default_rng([zlib.crc32(name.encode()), seed]).standard_normal(out[name].shape)
        drawn = base * np.exp(spread * noise) if base else spread * noise
        out[name] = jnp.asarray(drawn.astype(out[name].dtype))
    for name, factor in factors.items():
        out[name] = (out[name] * factor).astype(out[name].dtype)
    return out
```

```python
import math
from contextlib import ExitStack

import numpy as np

import concourse.bass as bass
from concourse import mybir

F32 = mybir.dt.float32
BF16 = mybir.dt.bfloat16
I32 = mybir.dt.int32
ALU = mybir.AluOpType
ACT = mybir.ActivationFunctionType
AX = mybir.AxisListType

P = 128
D = 256
DC = 192
NB = 2
S = 256
T = NB * S
NT = T // P
S2 = 4096
H0, D0 = 16, 16
BLK = 512
NBB = S2 // BLK
NBLK = NB * NBB
NH = NB * H0
NCH = S2 // P
VW = D0 + 1
NSTK = 6
EPS = 1e-5


class Count:

    def __init__(self, nc, name, per, credit_steps=0):
        self.sem = nc.alloc_semaphore(name)
        self.per, self.credit = per, per * credit_steps + 1 if credit_steps else 0

    def give(self, eng):
        if self.credit:
            eng.sem_inc(self.sem, self.credit)

    def wait(self, eng, n, k=None):
        eng.wait_ge(self.sem, n * self.per + (self.per if k is None else k) + self.credit)

    def inc(self, ins):
        return ins.then_inc(self.sem, 1)


class Line:

    def __init__(self, nc, eng, name):
        self.eng, self.sem, self.n = eng, nc.alloc_semaphore(name), 0
        self.seen = {}

    def after(self, *tokens):
        for sem, value in tokens:
            if self.seen.get(sem.name, 0) < value:
                self.eng.wait_ge(sem, value)
                self.seen[sem.name] = value

    def done(self, ins):
        self.n += 1
        ins.then_inc(self.sem, 1)
        return (self.sem, self.n)

    def last(self):
        return (self.sem, self.n)


class Load:

    def __init__(self, nc, name):
        self.sem, self.n = nc.alloc_semaphore(name), 0

    def add(self, ins):
        self.n += 16
        ins.then_inc(self.sem, 16)

    def token(self):
        return (self.sem, self.n)


UNUSED = ()


def constants():
    w = 2 * np.pi * (np.arange(S)[None, :] + 0.5) * np.arange(S)[:, None] / (2 * S)
    dft = np.stack([np.cos(w), np.sin(w), np.cos(w).T / S, np.sin(w).T / S]).astype(np.float32)
    heads, width, base_len = 8, 32, 512.0
    pos = np.arange(S, dtype=np.float64)[None, :]
    base = ((np.arange(0, width, 2) + 0.4 * width) / (1.4 * width))[:, None]
    scale = base ** (pos / base_len)
    angle = pos / 10000.0 ** (np.arange(width // 2) / (width // 2))[:, None]
    gamma = 1 - np.exp(np.linspace(math.log(1 / 32), math.log(1 / 512), heads))[:, None]
    sign = np.tile([-1.0, 1.0], width // 2)[:, None]
    tabs = []
    for power in (1, -1):
        for f, s in ((np.cos, 1.0), (np.sin, sign)):
            t = np.repeat(f(angle) * scale ** power, 2, axis=0) * s
            tabs.append((t[None] * (gamma ** (power * pos))[:, None, :]).reshape(heads * width, S))
    return {"dft": dft, "rotary": np.stack(tabs).astype(np.float32)}


def build(nc, ins, out):
    pe, act, dve, pool, sp = nc.tensor, nc.scalar, nc.vector, nc.gpsimd, nc.sync
    PE, AC, DV, PO = Line(nc, pe, "pe_line"), Line(nc, act, "act_line"), Line(nc, dve, "dve_line"), Line(nc, pool, "pool_line")
    ENG = {id(x.sem.name): x for x in (PE, AC, DV, PO)}

    scopes = []

    def sb(name, shape, dt=F32):
        return scopes[-1].enter_context(nc.sbuf_tensor(name, shape, dt))

    def phase_begins():
        scopes.append(ExitStack())

    def phase_ends():
        nc.all_engine_barrier()
        scopes.pop().close()

    phase_begins()

    def load(name, pairs, eng=sp):
        ld = Load(nc, name)
        with nc.allow_non_contiguous_dma(reason="some are short vectors"):
            for dst, src in pairs:
                ld.add(eng.dma_start(dst, src))
        return ld.token()

    def row(name):
        return ins[name].rearrange("(a n) -> a n", a=1)

    bank = nc.alloc_psum_tensor("bank", [P, 8, 512], F32)

    ident = sb("ident", [P, P])
    identb = sb("identb", [P, P], BF16)
    ones = sb("ones", [P, 512])
    x = sb("x", [P, NT, D])
    xn = sb("xn", [P, NT, D])
    xT = sb("xT", [P, 2, T])
    stats = sb("stats", [P, NT, 6])
    mv = sb("mv", [P, NT, 2])
    rstd = sb("rstd", [P, NT])

    t_x = load("ld_x", [(x[:, :, :], ins["x"].rearrange("b (t p) d -> p (b t) d", p=P))])
    zeros = sb("zeros", [P, 512])
    t_zeros = DV.done(dve.memset(zeros[:, :], 0.0))
    t_ones = DV.done(dve.memset(ones[:, :], 1.0))
    t = PO.done(pool.memset(ident[:, :], 0.0))
    PO.after(t)
    t_ident = PO.done(pool.affine_select(out=ident[:, :], in_=ident[:, :], compare_op=ALU.not_equal, fill=1.0,
                                         base=0, pattern=[[-1, P]], channel_multiplier=1))
    DV.after(t_ident)
    t_identb = DV.done(dve.tensor_copy(identb[:, :], ident[:, :]))

    spare = nc.alloc_semaphore("spare")

    def hold(eng):
        eng.sem_inc(spare, 1)

    def layer_norm(dst, src, after, n_tiles=NT):
        DV.after(*after)
        for i in range(n_tiles):
            t = DV.done(dve.bn_stats(stats[:, i, :], src[:, i, :]))
        DV.after(t)
        for i in range(n_tiles):
            t = DV.done(dve.bn_aggr(mv[:, i, :], stats[:, i, :]))
        DV.after(t)
        t = DV.done(dve.tensor_scalar(rstd[:, 0:n_tiles], mv[:, 0:n_tiles, 1], EPS, None, ALU.add))
        AC.after(t)
        t = AC.done(act.sqrt(rstd[:, 0:n_tiles], rstd[:, 0:n_tiles]))
        DV.after(t)
        t = DV.done(dve.reciprocal(rstd[:, 0:n_tiles], rstd[:, 0:n_tiles]))
        DV.after(t)
        for i in range(n_tiles):
            t = DV.done(dve.tensor_scalar(dst[:, i, :], src[:, i, :], mv[:, i, 0:1], rstd[:, i:i + 1],
                                          ALU.subtract, ALU.mult))
        return t

    def features_on_partitions(dst, src, after, free, banks=(0, 1)):
        PE.after(*after, *free, t_ident)
        toks = []
        for kt in range(D // P):
            for i in range(NT):
                t = PE.done(pe.transpose(bank[:, banks[kt], i * P:(i + 1) * P], src(i, kt), ident[:, :]))
            AC.after(t, *free)
            toks.append(AC.done(act.copy(dst[:, kt, :], bank[:, banks[kt], :])))
        return toks[-1]

    NSTATE, LA, LB = 64, 32, 8
    Ap = [sb(f"Ap{c}", [P, 4, LA, 32]) for c in "ri"]
    Bp = [sb(f"Bp{c}", [P, 4, LB, 32]) for c in "ri"]
    phase_begins()
    W2 = 2 * NSTATE
    ldt = sb("ldt", [P, 2])
    dt_n = sb("dt_n", [P, 2])
    dt_r = sb("dt_r", [P, 2])
    dt_p = sb("dt_p", [P, 2])
    dt_i = sb("dt_i", [P, 2], I32)
    are, aim, cre, cim = (sb(n, [P, 2, NSTATE]) for n in ("are", "aim", "cre", "cim"))
    t_s4 = load("ld_s4", [(tile[:, :, :], ins["L1_xattn_" + n].rearrange("(t p) n -> p t n", p=P))
                          for tile, n in ((are, "A_re"), (aim, "A_im"), (cre, "C_re"), (cim, "C_im"))]
                + [(ldt[:, :], ins["L1_xattn_log_dt"].rearrange("(t p) -> p t", p=P))], eng=act)

    def ts(dst, src, a, b=None, op0=ALU.mult, op1=None, line=None, eng=None):
        line = line or DV
        line.after(line.last())
        return line.done(line.eng.tensor_scalar(dst, src, a, b, op0, op1) if op1 is not None
                         else line.eng.tensor_scalar(dst, src, a, b, op0))

    def tt(dst, a, b, op, line=None):
        line = line or DV
        line.after(line.last())
        return line.done(line.eng.tensor_tensor(dst, a, b, op))

    BIG = 1.5 * 2.0 ** 23
    LN2_HI = 0.693359375
    DV.after(t_s4)
    ts(dt_n[:, :], ldt[:, :], 1.0 / math.log(2.0), BIG, ALU.mult, ALU.add)
    ts(dt_n[:, :], dt_n[:, :], BIG, None, ALU.subtract)
    ts(dt_r[:, :], dt_n[:, :], -LN2_HI)
    tt(dt_r[:, :], ldt[:, :], dt_r[:, :], ALU.add)
    ts(dt_p[:, :], dt_n[:, :], -(math.log(2.0) - LN2_HI))
    tt(dt_r[:, :], dt_r[:, :], dt_p[:, :], ALU.add)
    ts(dt_p[:, :], dt_r[:, :], 1.0 / math.factorial(8), 1.0 / math.factorial(7), ALU.mult, ALU.add)
    for k in range(6, -1, -1):
        tt(dt_p[:, :], dt_p[:, :], dt_r[:, :], ALU.mult)
        ts(dt_p[:, :], dt_p[:, :], 1.0 / math.factorial(k), None, ALU.add)
    ts(dt_i[:, :], dt_n[:, :], 127.0, 2.0 ** 23, ALU.add, ALU.mult)
    t_dt = tt(dt_p[:, :], dt_p[:, :], dt_i[:, :].bitcast(F32), ALU.mult)

    HALVINGS = 10
    wr, wi, er, ei, fr, fi, g1, g2 = (sb(n, [P, W2]) for n in ("wr", "wi", "er", "ei", "fr", "fi", "g1", "g2"))
    PO.after(t_dt, t_s4)
    for t_ in range(2):
        sl = slice(t_ * NSTATE, (t_ + 1) * NSTATE)
        ts(wr[:, sl], are[:, t_, :], dt_p[:, t_:t_ + 1], 2.0 ** -HALVINGS, ALU.mult, ALU.mult, line=PO)
        ts(wi[:, sl], aim[:, t_, :], dt_p[:, t_:t_ + 1], 2.0 ** -HALVINGS, ALU.mult, ALU.mult, line=PO)

    def cmul(outr, outi, ar, ai, br, bi, s1, s2):
        tt(s1, ar, br, ALU.mult, PO)
        tt(s2, ai, bi, ALU.mult, PO)
        tt(outr, s1, s2, ALU.subtract, PO)
        tt(s1, ar, bi, ALU.mult, PO)
        tt(s2, ai, br, ALU.mult, PO)
        return tt(outi, s1, s2, ALU.add, PO)

    f, G1, G2 = slice(None), g1[:, :], g2[:, :]
    ts(er[:, :], wr[:, :], 1.0 / 5.0, 1.0, ALU.mult, ALU.add, line=PO)
    ts(ei[:, :], wi[:, :], 1.0 / 5.0, 0.0, ALU.mult, ALU.add, line=PO)
    for k in (4, 3, 2):
        cmul(fr[:, :], fi[:, :], er[:, :], ei[:, :], wr[:, :], wi[:, :], G1, G2)
        ts(er[:, :], fr[:, :], 1.0 / k, 1.0, ALU.mult, ALU.add, line=PO)
        ts(ei[:, :], fi[:, :], 1.0 / k, 0.0, ALU.mult, ALU.add, line=PO)
    cmul(fr[:, :], fi[:, :], er[:, :], ei[:, :], wr[:, :], wi[:, :], G1, G2)
    a, b = (fr, fi), (er, ei)
    for k in range(HALVINGS):
        ts(wr[:, :], a[0][:, :], 1.0, 2.0, ALU.mult, ALU.add, line=PO)
        cmul(b[0][:, :], b[1][:, :], a[0][:, :], a[1][:, :], wr[:, :], a[1][:, :], G1, G2)
        a, b = b, a
    AR, AI = (q[:, :, :].rearrange("p t n -> p (t n)") for q in (are, aim))
    CR, CI = (q[:, :, :].rearrange("p t n -> p (t n)") for q in (cre, cim))
    tt(G1, AR, AR, ALU.mult, PO)
    tt(G2, AI, AI, ALU.mult, PO)
    t = tt(G1, G1, G2, ALU.add, PO)
    DV.after(t)
    t = DV.done(dve.reciprocal(wi[:, :], g1[:, :]))
    PO.after(t)
    ts(wi[:, :], wi[:, :], 2.0, 0.0, ALU.mult, ALU.add, line=PO)
    tt(AR, AR, wi[:, :], ALU.mult, PO)
    tt(AI, AI, wi[:, :], ALU.mult, PO)
    ts(AI, AI, -1.0, 0.0, ALU.mult, ALU.add, line=PO)
    cmul(b[0][:, :], b[1][:, :], AR, AI, CR, CI, G1, G2)
    cmul(AR, AI, b[0][:, :], b[1][:, :], a[0][:, :], a[1][:, :], G1, G2)
    t_z = ts(a[0][:, :], a[0][:, :], 1.0, 1.0, ALU.mult, ALU.add, line=PO)

    phase_begins()
    t_xn = layer_norm(xn, x, [t_x])
    t_xT = features_on_partitions(xT, lambda i, kt: xn[:, i, kt * P:(kt + 1) * P], [t_xn], [])
    wq = sb("wq", [P, 2, D])
    bq = sb("bq", [1, D])
    t_wq = load("ld_wq", [(wq[:, :, :], ins["L0_xattn_Wq"].rearrange("(k p) n -> p k n", p=P)),
                          (bq[:, :], row("L0_xattn_bq"))])
    qf = sb("qf", [P, T])
    qr = sb("qr", [P, T])
    qparts = sb("qparts", [P, 2, 3, T], BF16)
    q_parts_d = nc.dram_tensor("q_parts_d", [NB * D, 3, S], BF16).ap()
    k_parts_d = nc.dram_tensor("k_parts_d", [NB * D, 3, S2], BF16).ap()
    k1_parts_d = nc.dram_tensor("k1_parts_d", [NB * P, 3, S2], BF16).ap()

    def three_parts(parts, full, rest, after):
        DV.after(*after)
        t = DV.done(dve.tensor_copy(parts(0), full))
        DV.after(t)
        t = DV.done(dve.tensor_tensor(rest, full, parts(0), ALU.subtract))
        DV.after(t)
        t = DV.done(dve.tensor_copy(parts(1), rest))
        DV.after(t)
        return DV.done(dve.tensor_tensor(parts(2), rest, parts(1), ALU.subtract))

    ld_q = Load(nc, "st_qparts")
    PE.after(t_wq, t_xT, t_ones)
    for mt in range(2):
        for kt in range(2):
            pe.matmul(bank[:, 2 + mt, :], wq[:, kt, mt * P:(mt + 1) * P], xT[:, kt, :], start=(kt == 0), stop=False)
        t_q = PE.done(pe.matmul(bank[:, 2 + mt, :], bq[0:1, mt * P:(mt + 1) * P], ones[0:1, :], start=False, stop=True))
        DV.after(t_q)
        t = DV.done(dve.tensor_scalar(qf[:, :], bank[:, 2 + mt, :], float(D0) ** -0.5, None, ALU.mult))
        t = three_parts(lambda k: qparts[:, mt, k, :], qf[:, :], qr[:, :], [t])
        sp.wait_ge(*t)
        for b in range(NB):
            ld_q.add(sp.dma_start(q_parts_d[b * D + mt * P:b * D + (mt + 1) * P, :, :], qparts[:, mt, :, b * S:(b + 1) * S]))
    t_qd = ld_q.token()
    sp.wait_ge(*t_qd)

    V = sb("V", [P, NB * NCH, H0, VW])
    phase_begins()
    wkv1 = sb("wkv1", [P, 2 * D + P])
    wkv2 = sb("wkv2", [DC - P + 1, 2 * D + P])
    wk_all = [("L0_xattn_Wk", 0, D), ("L0_xattn_Wv", D, D), ("L1_xattn_Wk", 2 * D, P)]
    pairs = []
    for name, at, n in wk_all:
        pairs += [(wkv1[:, at:at + n], ins[name][0:P, :]), (wkv2[0:DC - P, at:at + n], ins[name][P:DC, :])]
    pairs += [(wkv2[DC - P:DC - P + 1, 0:D], row("L0_xattn_bk")), (wkv2[DC - P:DC - P + 1, D:2 * D], row("L0_xattn_bv"))]
    t_m = DV.done(dve.memset(wkv2[DC - P:DC - P + 1, :], 0.0))
    sp.wait_ge(*t_m)
    t_wkv = load("ld_wkv", pairs)

    cx = [sb(f"cx{j}", [P, BLK // P, DC]) for j in range(2)]
    cT1 = [sb(f"cT1_{j}", [P, BLK]) for j in range(2)]
    cT2 = [sb(f"cT2_{j}", [DC - P + 1, BLK]) for j in range(2)]
    kf = sb("kf", [P, 3, BLK])
    kr = sb("kr", [P, 3, BLK])
    kparts = [sb(f"kparts{j}", [P, 3, 3, BLK], BF16) for j in range(2)]
    for j in range(2):
        t_c = DV.done(dve.memset(cT2[j][DC - P:DC - P + 1, :], 1.0))
    t_v1 = PO.done(pool.memset(V[:, :, :, D0:VW], 1.0))

    ctx_loaded = [Count(nc, f"ctx_loaded{j}", 16) for j in range(2)]
    ctx_turned = Count(nc, "ctx_turned", 1, 1)
    cT_copied = Count(nc, "cT_copied", 2, 1)
    k_made = Count(nc, "k_made", 3)
    v_made = Count(nc, "v_made", 2, 2)
    kf_copied = Count(nc, "kf_copied", 3, 1)
    v_copied = Count(nc, "v_copied", 2, 1)
    kh_done = Count(nc, "kh_done", 6, 1)
    kl_done = Count(nc, "kl_done", 6, 1)
    kparts_out = [Count(nc, f"kparts_out{j}", 48, 1) for j in range(2)]
    for c, e in ((ctx_turned, pe), (cT_copied, act), (v_made, pe), (kf_copied, act), (v_copied, act),
                 (kh_done, dve), (kl_done, pool), (kparts_out[0], sp), (kparts_out[1], sp)):
        c.give(e)

    ctx_d = ins["ctx_768"].rearrange("b (n c p) d -> (b n) p c d", p=P, c=BLK // P)
    PE.after(t_wkv, t_c, t_q, t_xT)
    AC.after(t_v1, t_xT)
    PO.after(t_ones)
    DV.after(t_q)

    def project(batch, bpair, j):
        blk = bpair * 2 + j
        pair, n = bpair + batch * (NBB // 2), blk + batch * NBB
        ctx_turned.wait(sp, n - 1)
        sp.dma_start(cx[j][:, :, :], ctx_d[bass.ds(n, 1), :, :, :].rearrange("a p c d -> (a p) c d"))\
            .then_inc(ctx_loaded[j].sem, 16)
        ctx_loaded[j].wait(pe, pair)
        cT_copied.wait(pe, n - 1)
        for c in range(BLK // P):
            pe.transpose(bank[:, 0, c * P:(c + 1) * P], cx[j][:, c, 0:P], ident[:, :])
            ins_ = pe.transpose(bank[0:DC - P, 1, c * P:(c + 1) * P], cx[j][:, c, P:DC], ident[:, :])
        ctx_turned.inc(ins_)
        ctx_turned.wait(act, n)
        v_made.wait(act, n - 2)
        cT_copied.inc(act.copy(cT1[j][:, :], bank[:, 0, :]))
        cT_copied.inc(act.copy(cT2[j][0:DC - P, :], bank[0:DC - P, 1, :]))
        cT_copied.wait(pe, n)
        for m, at in enumerate((0, P, 2 * D)):
            kf_copied.wait(pe, n - 1, m + 1)
            pe.matmul(bank[:, 2 + m, :], wkv1[:, at:at + P], cT1[j][:, :], start=True, stop=False)
            k_made.inc(pe.matmul(bank[:, 2 + m, :], wkv2[:, at:at + P], cT2[j][:, :], start=False, stop=True))
        for c in range(BLK // P):
            if c % 2 == 0:
                v_copied.wait(pe, n - 1, c // 2 + 1)
            o = bank[:, 5 + c // 2, (c % 2) * D:(c % 2 + 1) * D]
            pe.matmul(o, cT1[j][:, c * P:(c + 1) * P], wkv1[:, D:2 * D], start=True, stop=False)
            ins_ = pe.matmul(o, cT2[j][:, c * P:(c + 1) * P], wkv2[:, D:2 * D], start=False, stop=True)
            if c % 2 == 1:
                v_made.inc(ins_)
        for m in range(3):
            k_made.wait(act, n, m + 1)
            kl_done.wait(act, n - 1, 2 * m + 1)
            kh_done.wait(act, n - 1, 2 * m + 2)
            kf_copied.inc(act.copy(kf[:, m, :], bank[:, 2 + m, :]))
            kf_copied.wait(dve, n, m + 1)
            kparts_out[j].wait(dve, pair - 1)
            kh_done.inc(dve.tensor_scalar(kparts[j][:, m, 0, :], kf[:, m, :], 1.0, None, ALU.mult))
            kh_done.wait(dve, n, 2 * m + 1)
            kl_done.wait(dve, n - 1, 2 * m + 2)
            kh_done.inc(dve.tensor_tensor(kr[:, m, :], kf[:, m, :], kparts[j][:, m, 0, :], ALU.subtract))
            kh_done.wait(pool, n, 2 * m + 2)
            kparts_out[j].wait(pool, pair - 1)
            kl_done.inc(pool.tensor_tensor(kparts[j][:, m, 1, :], kr[:, m, :], zeros[:, :], ALU.add))
            kl_done.wait(pool, n, 2 * m + 1)
            kl_done.inc(pool.tensor_tensor(kparts[j][:, m, 2, :], kr[:, m, :], kparts[j][:, m, 1, :], ALU.subtract))
            kl_done.wait(sp, n, 2 * m + 2)
            dst, row0 = (k_parts_d, batch * D + m * P) if m < 2 else (k1_parts_d, batch * P)
            sp.dma_start(dst[row0:row0 + P, :, bass.ds(blk * BLK, BLK)],
                         kparts[j][:, m, :, :]).then_inc(kparts_out[j].sem, 16)
        for h in range(2):
            v_made.wait(act, n, h + 1)
            v_copied.inc(act.copy(V[:, bass.ds(n * 4 + 2 * h, 2), :, 0:D0],
                                  bank[:, 5 + h, :].rearrange("p (c h d) -> p c h d", c=2, h=H0)))

    for batch in range(NB):
        with nc.Fori(0, NBB // 2, 1) as bpair:
            for j in range(2):
                project(batch, bpair, j)
    for j in range(2):
        kparts_out[j].wait(sp, NBLK // 2 - 1)
    phase_ends()
    PE.after(t_z, t_ident)
    for k, src in enumerate((a[0][:, :], a[1][:, :], AR, AI)):
        t = PE.done(pe.transpose(bank[:, 7, k * P:(k + 1) * P], src, ident[:, :]))
    AC.after(t)
    zz = [[sb(f"zz{k}{c}", [P, P]) for c in "ri"] for k in range(2)]
    for dst, k in ((zz[0][0][:, :], 0), (zz[0][1][:, :], 1), (Bp[0][:, :, 1, :], 0), (Bp[1][:, :, 1, :], 1),
                   (Ap[0][:, :, 0, :], 2), (Ap[1][:, :, 0, :], 3)):
        q_ = bank[:, 7, k * P:(k + 1) * P]
        t = AC.done(act.copy(dst, q_ if dst.shape[1] == P else q_.rearrange("p (q g) -> p q g", q=4)))
    s1, s2 = sb("s1", [P, 4, LA // 2, 32]), sb("s2", [P, 4, LA // 2, 32])
    PO.after(t)
    PO.done(pool.memset(Bp[0][:, :, 0, :], 1.0))
    PO.done(pool.memset(Bp[1][:, :, 0, :], 0.0))
    cur = 0

    def square(cur):
        z, y = zz[cur], zz[1 - cur]
        cmul(y[0][:, :], y[1][:, :], z[0][:, :], z[1][:, :], z[0][:, :], z[1][:, :],
             *(q[:, 0, 0:4, :].rearrange("p a g -> p (a g)") for q in (s1, s2)))
        return 1 - cur

    def extend(pw, m, cur):
        zb = [q[:, :].rearrange("p (q a g) -> p q a g", q=4, a=1).to_broadcast([P, 4, m, 32]) for q in zz[cur]]
        return cmul(pw[0][:, :, m:2 * m, :], pw[1][:, :, m:2 * m, :], pw[0][:, :, 0:m, :], pw[1][:, :, 0:m, :],
                    zb[0], zb[1], s1[:, :, 0:m, :], s2[:, :, 0:m, :])

    for m in (2, 4):
        cur = square(cur)
        extend(Bp, m, cur)
    for m in (1, 2, 4, 8, 16):
        cur = square(cur)
        extend(Ap, m, cur)
    t_pow = ts(Bp[1][:, :, :, :], Bp[1][:, :, :, :], -1.0, 0.0, ALU.mult, ALU.add, line=PO)

    NS = NSTK * D0
    ks = [sb(f"ks{j}", [NS + 3, S2], BF16) for j in range(2)]
    qs = [sb(f"qs{j}", [NS + 3, S], BF16) for j in range(2)]
    vs = [sb(f"vs{j}", [P, NCH, VW]) for j in range(2)]
    pT = [sb(f"pT{j}", [P, 4 * S]) for j in range(2)]
    rmax = sb("rmax", [P, 2, 8])
    nmax = sb("nmax", [P, 2])
    nres = sb("nres", [P, 2])
    mparts = sb("mparts", [P, 2, 3], BF16)
    ao = sb("ao", [P, NH, 2, D0])
    rden = sb("rden", [P, 2, 2])
    for j in range(2):
        t = DV.done(dve.memset(ks[j][NS:NS + 3, :], 1.0))
    PE.after(t)

    stack_in = [Count(nc, f"stack_in{j}", 16 * 2 * NSTK) for j in range(2)]
    max_made = Count(nc, "max_made", 17)
    max_read = Count(nc, "max_read", 17, 1)
    max_step = Count(nc, "max_step", 6)
    st_made = Count(nc, "st_made", 8)
    p_made = Count(nc, "p_made", 8, 1)
    pv_made = Count(nc, "pv_made", 8, 2)
    vs_copied = Count(nc, "vs_copied", 1)
    o_done = Count(nc, "o_done", 2, 2)
    for c, e in ((max_read, dve), (p_made, act), (pv_made, pe), (o_done, dve)):
        c.give(e)

    def stack(pair, j):
        n = pair * 2 + j
        pv_made.wait(sp, n - 2)
        kd = k_parts_d[bass.ds(n * D0, D0), :, :]
        qd = q_parts_d[bass.ds(n * D0, D0), :, :]
        for s, (kp, qp) in enumerate(((0, 0), (0, 1), (0, 2), (1, 0), (1, 1), (2, 0))):
            sp.dma_start(ks[j][s * D0:(s + 1) * D0, :], kd[:, kp, :]).then_inc(stack_in[j].sem, 16)
            sp.dma_start(qs[j][s * D0:(s + 1) * D0, :], qd[:, qp, :]).then_inc(stack_in[j].sem, 16)

    def values(pair, j):
        n = pair * 2 + j
        pv_made.wait(dve, n - 2)
        vs_copied.inc(dve.tensor_scalar(vs[j][:, :, :], V[:, bass.ds((n // H0) * NCH, NCH), bass.ds(n % H0, 1), :]
                                        .rearrange("p c a d -> p c (a d)"), 1.0, None, ALU.mult))

    def max_chunk(pair, j, u):
        n, qt, c = pair * 2 + j, u // 8, u % 8
        max_read.wait(pe, n, u - 1 if u >= 2 else 0)
        max_made.inc(pe.matmul(bank[:, u % 2, :], qs[j][0:NS, qt * P:(qt + 1) * P], ks[j][0:NS, c * 512:(c + 1) * 512],
                               start=True, stop=True))
        max_made.wait(dve, n, u + 1)
        max_read.inc(dve.tensor_reduce(rmax[:, qt, c:c + 1], bank[:, u % 2, :], AX.X, ALU.max))

    def max_rows(pair, j):
        n = pair * 2 + j
        max_read.wait(dve, n, 16)
        max_step.inc(dve.tensor_reduce(nmax[:, :], rmax[:, :, :], AX.X, ALU.max, negate=True))
        for part in range(3):
            max_step.wait(dve, n, 2 * part + 1)
            max_step.inc(dve.tensor_copy(mparts[:, :, part], nmax[:, :] if part == 0 else nres[:, :]))
            if part < 2:
                max_step.wait(dve, n, 2 * part + 2)
                max_step.inc(dve.tensor_tensor(nres[:, :], nmax[:, :] if part == 0 else nres[:, :], mparts[:, :, part],
                                               ALU.subtract))
        max_step.wait(pe, n)
        max_read.wait(pe, n, 15)
        for qt in range(2):
            ins_ = pe.matmul(bank[NS:NS + 3, 0, qt * P:(qt + 1) * P], mparts[:, qt, :], identb[:, :], start=True, stop=True)
        max_made.inc(ins_)
        max_made.wait(dve, n)
        max_read.inc(dve.tensor_copy(qs[j][NS:NS + 3, :], bank[NS:NS + 3, 0, 0:S]))

    def scores(pair, j, g):
        n, b0 = pair * 2 + j, 2 + 2 * (g % 2)
        p_made.wait(pe, n if g >= 2 else n - 1, g - 1 if g >= 2 else 7 + g)
        if g == 0:
            max_read.wait(pe, n)
        for c in range(4):
            k0 = (4 * g + c) * P
            ins_ = pe.matmul(bank[:, b0 + c // 2, (c % 2) * S:(c % 2 + 1) * S], ks[j][:, k0:k0 + P], qs[j][:, :],
                             start=True, stop=True)
        st_made.inc(ins_)
        st_made.wait(act, n, g + 1)
        pv_made.wait(act, n if g >= 2 else n - 1, g - 1 if g >= 2 else 7 + g)
        p_made.inc(act.activation(pT[g % 2][:, :], bank[:, b0:b0 + 2, :].rearrange("p a k -> p (a k)"), ACT.Exp))

    def weigh(pair, j, g):
        n = pair * 2 + j
        p_made.wait(pe, n, g + 1)
        if g == 0:
            vs_copied.wait(pe, n)
            o_done.wait(pe, n - 1)
        for c in range(4):
            for qt in range(2):
                ins_ = pe.matmul(bank[:, 6 + qt, j * 32:j * 32 + VW], pT[g % 2][:, c * S + qt * P:c * S + (qt + 1) * P],
                                 vs[j][:, 4 * g + c, :], start=(g == 0 and c == 0), stop=(g == 7 and c == 3))
        pv_made.inc(ins_)

    def divide(pair, j):
        n = pair * 2 + j
        pv_made.wait(dve, n)
        o_done.inc(dve.reciprocal(rden[:, :, 0], bank[:, 6:8, j * 32 + D0]))
        o_done.wait(dve, n, 1)
        for qt in range(2):
            ins_ = dve.tensor_scalar(ao[:, bass.ds(n, 1), qt, :].rearrange("p a d -> p (a d)"),
                                     bank[:, 6 + qt, j * 32:j * 32 + D0], rden[:, qt, 0:1], None, ALU.mult)
        o_done.inc(ins_)

    def attend(pair, j, nxt):
        for g in range(8):
            scores(pair, j, g)
            if nxt:
                if g == 0:
                    stack_in[nxt[1]].wait(pe, nxt[0])
                max_chunk(*nxt, 2 * g)
                max_chunk(*nxt, 2 * g + 1)
            if g:
                weigh(pair, j, g - 1)
        weigh(pair, j, 7)
        if nxt:
            max_rows(*nxt)
        divide(pair, j)

    stack(0, 0)
    stack(0, 1)
    values(0, 0)
    values(0, 1)
    stack_in[0].wait(pe, 0)
    for u in range(16):
        max_chunk(0, 0, u)
    max_rows(0, 0)
    with nc.Fori(0, NH // 2 - 1, 1) as pair:
        attend(pair, 0, (pair, 1))
        stack(pair + 1, 0)
        values(pair + 1, 0)
        attend(pair, 1, (pair + 1, 0))
        stack(pair + 1, 1)
        values(pair + 1, 1)
    attend(NH // 2 - 1, 0, (NH // 2 - 1, 1))
    attend(NH // 2 - 1, 1, None)
    o_done.wait(pe, NH - 1)
    o_done.wait(dve, NH - 1)

    wo = sb("wo", [P, 2, D])
    bo = sb("bo", [1, D])
    t_wo = load("ld_wo", [(wo[:, :, :], ins["L0_xattn_Wo"].rearrange("(k p) n -> p k n", p=P)), (bo[:, :], row("L0_xattn_bo"))])
    aoc = sb("aoc", [P, NT, D])
    for i in range(NT):
        b, qt = i // 2, i % 2
        t = DV.done(dve.tensor_copy(aoc[:, i, :].rearrange("p (h d) -> p h d", h=H0), ao[:, b * H0:(b + 1) * H0, qt, :]))
    t_aoT = features_on_partitions(xT, lambda i, kt: aoc[:, i, kt * P:(kt + 1) * P], [t], [])

    def project_tokens(srcT, w, bias, after, first_bank=2, width=D):
        PE.after(*after)
        toks = []
        for i in range(NT):
            for kt in range(2):
                t = pe.matmul(bank[:, first_bank + i, 0:width], srcT[:, kt, i * P:(i + 1) * P], w[:, kt, :],
                              start=(kt == 0), stop=(kt == 1 and bias is None))
            if bias is not None:
                t = pe.matmul(bank[:, first_bank + i, 0:width], ones[0:1, 0:P], bias, start=False, stop=True)
            toks.append(PE.done(t))
        return toks

    def add_to_x(toks, first_bank=2):
        for i in range(NT):
            DV.after(toks[i])
            t = DV.done(dve.tensor_tensor(x[:, i, :], bank[:, first_bank + i, 0:D], x[:, i, :], ALU.add))
        return t

    t_x1 = add_to_x(project_tokens(xT, wo, bo[0:1, :], [t_wo, t_aoT]))
    phase_ends()
    phase_ends()

    HA, DA = 8, 32
    phase_begins()
    t_xn = layer_norm(xn, x, [t_x1])
    t_xT = features_on_partitions(xT, lambda i, kt: xn[:, i, kt * P:(kt + 1) * P], [t_xn], [])
    lowV = {c: sb(f"lowV{c}", [P, 2, P]) for c in "qkv"}
    lowU = {c: sb(f"lowU{c}", [P, 2, P]) for c in "qkv"}
    lowb = sb("lowb", [P, 3, 2])
    lowbv = sb("lowbv", [1, D])
    raw = sb("raw", [P, 2, 2, P])
    pairs = [(lowbv[:, :], ins["L0_attn_bv"].rearrange("h d -> (h d)").rearrange("(a n) -> a n", a=1))]
    for k, c in enumerate("qkv"):
        t = PO.done(pool.memset(lowV[c][:, :, :], 0.0))
        t = PO.done(pool.memset(lowU[c][:, :, :], 0.0))
    sp.wait_ge(*t)
    ld = Load(nc, "ld_lowrank")
    with nc.allow_non_contiguous_dma(reason="small transposed weights"):
        for dst, src in pairs:
            ld.add(sp.dma_start(dst, src))
        for k, c in enumerate("qkv"):
            for h in range(HA):
                r = slice((h % 4) * DA, (h % 4 + 1) * DA)
                ld.add(sp.dma_start(lowV[c][r, h // 4, r], ins["L0_attn_V" + c][h, :, :].rearrange("r d -> d r")))
                ld.add(sp.dma_start(lowU[c][r, h // 4, r], ins["L0_attn_U" + c][h, :, :].rearrange("d r -> r d")))
            for m in range(2):
                ld.add(sp.dma_start(lowb[:, k, m:m + 1], ins["L0_attn_b" + c][4 * m:4 * m + 4, :].rearrange("h (d a) -> (h d) a", a=1)))
    t_low = ld.token()
    lowT = sb("lowT", [P, 2, T])
    qk = {c: sb(f"low_{c}", [P, 2, T]) for c in "qk"}
    vA = sb("vA", [P, NT, HA, DA + 1])
    t_vo = PO.done(pool.memset(vA[:, :, :, DA:DA + 1], 1.0))
    free = [t_xT, t_x1]
    for k, c in enumerate("qkv"):
        for m in range(2):
            PE.after(t_low, t_xT, *free)
            t = PE.done(pe.matmul(bank[:, 2 + m, :], lowV[c][:, m, :], xT[:, m, :], start=True, stop=True))
            AC.after(t, *free)
            t_l = AC.done(act.copy(lowT[:, m, :], bank[:, 2 + m, :]))
            PE.after(t_l)
            if c != "v":
                t = PE.done(pe.matmul(bank[:, 4 + m, :], lowU[c][:, m, :], lowT[:, m, :], start=True, stop=True))
                DV.after(t)
                t = DV.done(dve.tensor_scalar(qk[c][:, m, :], bank[:, 4 + m, :], lowb[:, k, m:m + 1],
                                              float(DA) ** -0.5 if c == "q" else 1.0, ALU.add, ALU.mult))
                free = [t]
        if c == "v":
            for i in range(NT):
                b, h = 6 + i // 2, (i % 2) * D
                for m in range(2):
                    o = bank[:, b, h + m * P:h + (m + 1) * P]
                    pe.matmul(o, lowT[:, m, i * P:(i + 1) * P], lowU[c][:, m, :], start=True, stop=False)
                    t = PE.done(pe.matmul(o, ones[0:1, 0:P], lowbv[:, m * P:(m + 1) * P], start=False, stop=True))
            AC.after(t, t_vo)
            for i in range(NT):
                b, h = 6 + i // 2, (i % 2) * D
                t_v = AC.done(act.copy(vA[:, i, :, 0:DA], bank[:, b, h:h + D].rearrange("p (h d) -> p h d", h=HA)))
    sA = sb("sA", [P, HA, S])
    sAT = sb("sAT", [P, HA, 2, P])
    mA = sb("mA", [P, HA])
    oA = sb("oA", [P, NT, HA, DA])
    rA = sb("rA", [P, HA])
    t_done = t_v
    for i in range(NT):
        b = i // 2
        PE.after(t_done, free[0], t_v)
        for h in range(HA):
            r = slice((h % 4) * DA, (h % 4 + 1) * DA)
            t = pe.matmul(bank[:, h % 4, (h // 4) * S:(h // 4 + 1) * S], qk["q"][r, h // 4, i * P:(i + 1) * P],
                          qk["k"][r, h // 4, b * S:(b + 1) * S], start=True, stop=True)
        t = PE.done(t)
        DV.after(t)
        t = DV.done(dve.tensor_reduce(mA[:, :], bank[:, 0:4, :].rearrange("p c (a k) -> p a c k", a=2), AX.X, ALU.max, negate=True))
        AC.after(t)
        for h in range(HA):
            t = AC.done(act.activation(sA[:, h, :], bank[:, h % 4, (h // 4) * S:(h // 4 + 1) * S], ACT.Exp, bias=mA[:, h:h + 1]))
        PE.after(t)
        for h in range(HA):
            for k in range(2):
                t = pe.transpose(bank[:, h // 2, (h % 2) * S + k * P:(h % 2) * S + (k + 1) * P], sA[:, h, k * P:(k + 1) * P], ident[:, :])
        t = PE.done(t)
        DV.after(t)
        t = DV.done(dve.tensor_copy(sAT[:, :, :, :].rearrange("p h k q -> p (h k q)"), bank[:, 0:4, :].rearrange("p a n -> p (a n)")))
        PE.after(t)
        for h in range(HA):
            for k in range(2):
                t = pe.matmul(bank[:, 4, h * 64:h * 64 + DA + 1], sAT[:, h, k, :], vA[:, b * 2 + k, h, :], start=(k == 0), stop=(k == 1))
        t = PE.done(t)
        o = bank[:, 4, :].rearrange("p (h d) -> p h d", h=HA)
        DV.after(t)
        t = DV.done(dve.reciprocal(rA[:, :], o[:, :, DA]))
        DV.after(t)
        for h in range(HA):
            t_done = DV.done(dve.tensor_scalar(oA[:, i, h, :], o[:, h, 0:DA], rA[:, h:h + 1], None, ALU.mult))
        DV.after(t_done)
        t_x2 = DV.done(dve.tensor_tensor(x[:, i, :], x[:, i, :], oA[:, i, :, :].rearrange("p h d -> p (h d)"), ALU.add))
    phase_ends()

    NE, FI, TOP = 16, 128, 4
    phase_begins()
    t_xn = layer_norm(xn, x, [t_x2])
    t_xT = features_on_partitions(xT, lambda i, kt: xn[:, i, kt * P:(kt + 1) * P], [t_xn], [])
    gwr = sb("gwr", [NE, D])
    gwT = sb("gwT", [P, 2, NE])
    t_g = load("ld_gate", [(gwr[:, :], ins["L0_ffn_gate_w"])])
    PE.after(t_g, t_xT)
    for kt in range(2):
        t = PE.done(pe.transpose(bank[:, 2, kt * NE:(kt + 1) * NE], gwr[:, kt * P:(kt + 1) * P], ident[0:NE, 0:NE]))
    DV.after(t)
    t = DV.done(dve.tensor_copy(gwT[:, :, :].rearrange("p a b -> p (a b)"), bank[:, 2, 0:2 * NE]))
    PE.after(t)
    for i in range(NT):
        for kt in range(2):
            t = pe.matmul(bank[:, 3, i * NE:(i + 1) * NE], xT[:, kt, i * P:(i + 1) * P], gwT[:, kt, :], start=(kt == 0), stop=(kt == 1))
    t = PE.done(t)
    PAD = 4
    lg = sb("lg", [P, NT, NE])
    best = sb("best", [P, NT, 8])
    prob = sb("prob", [P, NT, NE + PAD])
    rest = sb("rest", [P, NT, NE + PAD])
    score = sb("score", [P, NT, NE])
    nm = sb("nm", [P, NT])
    den = sb("den", [P, NT])
    DV.after(t)
    t = DV.done(dve.tensor_copy(lg[:, :, :].rearrange("p a b -> p (a b)"), bank[:, 3, 0:NT * NE]))
    DV.after(t)
    t = DV.done(dve.tensor_reduce(nm[:, :], lg[:, :, :], AX.X, ALU.max, negate=True))
    AC.after(t)
    for i in range(NT):
        t = AC.done(act.activation(prob[:, i, 0:NE], lg[:, i, :], ACT.Exp, bias=nm[:, i:i + 1], accum_out=den[:, i:i + 1]))
    DV.after(t)
    for k in range(PAD):
        t = DV.done(dve.memset(prob[:, :, NE + k:NE + k + 1], -1.0 - k))
    t = DV.done(dve.reciprocal(den[:, :], den[:, :]))
    DV.after(t)
    for i in range(NT):
        t = DV.done(dve.tensor_scalar(prob[:, i, 0:NE], prob[:, i, 0:NE], den[:, i:i + 1], None, ALU.mult))
    DV.after(t)
    for i in range(NT):
        t = DV.done(dve.max(best[:, i, :], prob[:, i, :]))
    DV.after(t)
    for k in range(PAD):
        t = DV.done(dve.memset(best[:, :, TOP + k:TOP + k + 1], -1.0 - k))
    DV.after(t)
    for i in range(NT):
        t = DV.done(dve.match_replace(rest[:, i, :], best[:, i, :], prob[:, i, :], 0.0))
    t = DV.done(dve.tensor_reduce(den[:, :], best[:, :, 0:TOP], AX.X, ALU.add))
    DV.after(t)
    t = DV.done(dve.reciprocal(den[:, :], den[:, :]))
    t = DV.done(dve.tensor_tensor(score[:, :, :], prob[:, :, 0:NE], rest[:, :, 0:NE], ALU.subtract))
    DV.after(t)
    for i in range(NT):
        t_score = DV.done(dve.tensor_scalar(score[:, i, :], score[:, i, :], den[:, i:i + 1], None, ALU.mult))

    w13 = [sb(f"w13_{j}", [P, 2, 2, FI]) for j in range(2)]
    w2e = [sb(f"w2e_{j}", [P, D]) for j in range(2)]
    gate = [sb(f"gate{j}", [P, T]) for j in range(2)]
    hid = [sb(f"hid{j}", [P, T]) for j in range(2)]
    sce = [sb(f"sce{j}", [P, NT]) for j in range(2)]
    w_in = [Count(nc, f"w_in{j}", 48) for j in range(2)]
    gu_made = Count(nc, "gu_made", 1)
    gate_done = Count(nc, "gate_done", 1)
    hid_done = Count(nc, "hid_done", 2, 2)
    y_made = Count(nc, "y_made", 1, 2)
    y_added = Count(nc, "y_added", NT, 2)
    for c, e in ((hid_done, dve), (y_made, pe), (y_added, dve)):
        c.give(e)
    PE.after(t_xT, t_score)
    DV.after(t_score)
    w1_d, w3_d, w2_d = ins["L0_ffn_w1"], ins["L0_ffn_w3"], ins["L0_ffn_w2"]

    def load_expert(pair, j):
        e = pair * 2 + j
        y_made.wait(sp, e - 2)
        for k, w in enumerate((w1_d, w3_d)):
            sp.dma_start(w13[j][:, k, :, :], w[bass.ds(e, 1), :, :].rearrange("a (k p) i -> p (a k) i", p=P)).then_inc(w_in[j].sem, 16)
        sp.dma_start(w2e[j][:, :], w2_d[bass.ds(e, 1), :, :].rearrange("a i h -> (a i) h")).then_inc(w_in[j].sem, 16)

    def expert_up(pair, j):
        e = pair * 2 + j
        w_in[j].wait(pe, pair)
        hid_done.wait(pe, e - 2, 1)
        for k in range(2):
            for kt in range(2):
                ins_ = pe.matmul(bank[:, 2 * j + k, :], w13[j][:, k, kt, :], xT[:, kt, :], start=(kt == 0), stop=(kt == 1))
        gu_made.inc(ins_)
        gu_made.wait(act, e)
        gate_done.inc(act.activation(gate[j][:, :], bank[:, 2 * j, :], ACT.Silu))
        gate_done.wait(dve, e)
        y_made.wait(dve, e - 2)
        hid_done.inc(dve.tensor_tensor(hid[j][:, :], bank[:, 2 * j + 1, :], gate[j][:, :], ALU.mult))
        y_added.wait(dve, e - 2)
        hid_done.inc(dve.tensor_scalar(sce[j][:, :], score[:, :, bass.ds(e, 1)].rearrange("p t a -> p (t a)"), 1.0, None, ALU.mult))

    def expert_down(pair, j):
        e = pair * 2 + j
        hid_done.wait(pe, e)
        y_added.wait(pe, e - 2)
        for i in range(NT):
            ins_ = pe.matmul(bank[:, 4 + 2 * j + i // 2, (i % 2) * D:(i % 2 + 1) * D], hid[j][:, i * P:(i + 1) * P], w2e[j][:, :],
                             start=True, stop=True)
        y_made.inc(ins_)
        y_made.wait(dve, e)
        y_added.wait(dve, e - 1)
        for i in range(NT):
            y_added.inc(dve.scalar_tensor_tensor(x[:, i, :], bank[:, 4 + 2 * j + i // 2, (i % 2) * D:(i % 2 + 1) * D],
                                                 sce[j][:, i:i + 1], x[:, i, :], ALU.mult, ALU.add))

    load_expert(0, 0)
    load_expert(0, 1)
    expert_up(0, 0)
    with nc.Fori(0, NE // 2 - 1, 1) as pair:
        expert_up(pair, 1)
        expert_down(pair, 0)
        load_expert(pair + 1, 0)
        expert_up(pair + 1, 0)
        expert_down(pair, 1)
        load_expert(pair + 1, 1)
    expert_up(NE // 2 - 1, 1)
    expert_down(NE // 2 - 1, 0)
    expert_down(NE // 2 - 1, 1)
    y_added.wait(dve, NE - 1)
    y_added.wait(act, NE - 1)
    y_added.wait(pe, NE - 1)
    t_x3 = DV.done(dve.tensor_copy(nm[:, 0:1], nm[:, 0:1]))
    phase_ends()

    H1, D1, KTOP = 4, 32, 32
    DCM = DC - P
    phase_begins()
    xt = sb("xt", [P, NT, D])
    xh = sb("xh", [P, NT, D])
    c0T = [sb("c0T1", [P, T]), sb("c0T2", [DCM, T])]
    t_xt = layer_norm(xt, x, [t_x3])
    t_xT = features_on_partitions(xT, lambda i, kt: xt[:, i, kt * P:(kt + 1) * P], [t_xt], [])

    tabs = sb("tabs", [P, 4, 2, S])
    KT = sb("KT", [P, 2, D])
    Kf = sb("Kf", [P, 2, 2, D])
    phase_begins()
    t_tab = load("ld_tab", [(tabs[:, k, :, :], ins["dft"][k].rearrange("(t p) n -> p t n", p=P)) for k in range(4)])
    kst = sb("kst", [P, LB, 2, LA])
    PE.after(t_pow, t_xT)
    for t_ in range(2):
        for g in range(LA):
            hs = slice(t_ * NSTATE, (t_ + 1) * NSTATE)
            c0 = (t_ * LA + g) * 32
            for c in range(2):
                t = pe.matmul(bank[:, 4 + c0 // 512, c0 % 512:c0 % 512 + 32],
                              Ap[c][hs, :, :, g].rearrange("p q a -> p (q a)"), Bp[c][hs, :, :, g], start=(c == 0), stop=(c == 1))
    t = PE.done(t)
    AC.after(t)
    blk = bank[:, 4:8, :].rearrange("p c n -> p (c n)").rearrange("p (g q b) -> p q b g", q=4, b=LB)
    for q in range(4):
        t = AC.done(act.copy(kst[32 * q:32 * q + 32, :, :, :].rearrange("p b t g -> p b (t g)"), blk[32 * q:32 * q + 32, q, :, :]))
    K_d = nc.dram_tensor("K_d", [S, D], F32).ap()
    sp.wait_ge(*t)
    ld = Load(nc, "st_K")
    for q in range(4):
        for t_ in range(2):
            at = t_ * P + q * 32
            ld.add(sp.dma_start(K_d.rearrange("(a b) d -> a b d", b=LB)[:, :, at:at + 32], kst[32 * q:32 * q + 32, :, t_, :]))
    sp.wait_ge(*ld.token())
    t_KT = load("ld_KT", [(KT[:, :, :], K_d.rearrange("(t p) d -> p t d", p=P))])

    wq1 = sb("wq1", [P, 2, P])
    t_w = load("ld_wq1", [(wq1[:, :, :], ins["L1_xattn_Wq"].rearrange("(k p) n -> p k n", p=P))])
    q1f, q1r, q1p = sb("q1f", [P, T]), sb("q1r", [P, T]), sb("q1p", [P, 3, T], BF16)
    q1_parts_d = nc.dram_tensor("q1_parts_d", [NB * P, 3, S], BF16).ap()
    PE.after(t_w, t_xT)
    for kt in range(2):
        t = pe.matmul(bank[:, 2, :], wq1[:, kt, :], xT[:, kt, :], start=(kt == 0), stop=(kt == 1))
    t = PE.done(t)
    DV.after(t)
    t = DV.done(dve.tensor_scalar(q1f[:, :], bank[:, 2, :], 1.0 / math.sqrt(D1), None, ALU.mult))
    t = three_parts(lambda k: q1p[:, k, :], q1f[:, :], q1r[:, :], [t])
    sp.wait_ge(*t)
    ld = Load(nc, "st_q1")
    for b in range(NB):
        ld.add(sp.dma_start(q1_parts_d[b * P:(b + 1) * P, :, :], q1p[:, :, b * S:(b + 1) * S]))
    m8 = sb("m8", [NB, S2], mybir.dt.uint8)
    mrow = sb("mrow", [NB, S2], BF16)
    mask_d = nc.dram_tensor("mask_d", [NB, S2], BF16).ap()
    t_m = load("ld_mask", [(m8[:, :], ins["mask_BxS2_bf1"])])
    DV.after(t_m)
    t = DV.done(dve.tensor_scalar(mrow[:, :], m8[:, :], 1e30, -1e30, ALU.mult, ALU.add))
    sp.wait_ge(*t)
    ld.add(sp.dma_start(mask_d, mrow[:, :]))
    sp.wait_ge(*ld.token())
    PE.after(t_KT, t_tab)
    for c in range(2):
        for ft in range(2):
            for lt in range(2):
                t = pe.matmul(bank[:, 4 + c, ft * D:(ft + 1) * D], tabs[:, c, lt, ft * P:(ft + 1) * P], KT[:, lt, :],
                              start=(lt == 0), stop=(lt == 1))
        t = PE.done(t)
        AC.after(t)
        t_Kf = AC.done(act.copy(Kf[:, c, :, :].rearrange("p f d -> p (f d)"), bank[:, 4 + c, :]))
    phase_ends()

    phase_begins()
    NS1 = 3 * D1
    NM = NB * H1
    k1s = [[sb(f"k1s{j}{g}", [NS1 + 1, S2], BF16) for g in range(2)] for j in range(1)] * 2
    q1s = [[sb(f"q1s{j}{g}", [NS1 + 1, S], BF16) for g in range(2)] for j in range(1)] * 2
    Sc = sb("Sc", [P, S2])
    Wk = sb("Wk", [P, S2])
    amean = sb("amean", [P, 2, S2])
    top = sb("top", [P, KTOP])
    etop = sb("etop", [P, KTOP])
    ntop = sb("ntop", [P, 1])
    ssum = sb("ssum", [P, 1])
    cn = sb("cn", [P, NCH, DC])
    aT = [sb(f"aT{j}", [P, 4, P]) for j in range(2)]
    c0 = sb("c0", [P, NT, DC])
    for g in range(2):
        t_o = DV.done(dve.memset(q1s[0][g][NS1:NS1 + 1, :], 1.0 if g == 0 else 0.0))
        t_o = DV.done(dve.memset(k1s[0][g][NS1:NS1 + 1, :], 0.0))
    t_cov = DV.done(dve.memset(amean[:, :, :], 0.0))
    stack1_in = Count(nc, "stack1_in", 16 * 13)
    s_made = Count(nc, "s_made", 2, 1)
    s_copied = Count(nc, "s_copied", 2, 1)
    t_step = Count(nc, "t_step", 13, 1)
    a_step = Count(nc, "a_step", 3, 1)
    for c, e in ((s_made, pe), (s_copied, act), (t_step, dve), (a_step, act)):
        c.give(e)
    PE.after(t_Kf, t_o)
    sp.wait_ge(*t_o)
    GROUPS = (((0, 0), (0, 1), (1, 0)), ((0, 2), (2, 0), (1, 1)))

    def stack1(b, h):
        r = b * H1 * 2 + h * 2
        s_made.wait(sp, r - 1)
        kd = k1_parts_d[bass.ds(h * D1 + b * P, D1), :, :]
        qd = q1_parts_d[bass.ds(h * D1 + b * P, D1), :, :]
        for g in range(2):
            for s, (kp, qp) in enumerate(GROUPS[g]):
                sp.dma_start(k1s[0][g][s * D1:(s + 1) * D1, :], kd[:, kp, :]).then_inc(stack1_in.sem, 16)
                sp.dma_start(q1s[0][g][s * D1:(s + 1) * D1, :], qd[:, qp, :]).then_inc(stack1_in.sem, 16)
        sp.dma_start(k1s[0][0][NS1:NS1 + 1, :], mask_d[b:b + 1, :]).then_inc(stack1_in.sem, 16)

    def row_tile(b, h, qt):
        m = b * H1 + h
        r = m * 2 + qt
        if qt == 0:
            stack1_in.wait(pe, m)
        for half in range(2):
            s_copied.wait(pe, r - 1, half + 1)
            for c in range(4):
                k0 = half * 2048 + c * 512
                for g in range(2):
                    ins_ = pe.matmul(bank[:, half * 4 + c, :], q1s[0][g][:, qt * P:(qt + 1) * P], k1s[0][g][:, k0:k0 + 512],
                                     start=(g == 0), stop=(g == 1))
            s_made.inc(ins_)
            s_made.wait(act, r, half + 1)
            t_step.wait(act, r - 1)
            s_copied.inc(act.copy(Sc[:, half * 2048:(half + 1) * 2048], bank[:, half * 4:half * 4 + 4, :].rearrange("p c n -> p (c n)")))
        s_copied.wait(dve, r)
        a_step.wait(dve, r - 1)
        hold(dve)
        src = Sc
        for k in range(KTOP // 8):
            t_step.inc(dve.max(top[:, 8 * k:8 * k + 8], src[:, :]))
            t_step.wait(dve, r, 2 * k + 1)
            hold(dve)
            t_step.inc(dve.match_replace(Wk[:, :], top[:, 8 * k:8 * k + 8], src[:, :], -3e38))
            t_step.wait(dve, r, 2 * k + 2)
            hold(dve)
            src = Wk
        t_step.inc(dve.tensor_scalar(ntop[:, :], top[:, 0:1], -1.0, None, ALU.mult))
        t_step.wait(act, r, 9)
        a_step.inc(act.activation(etop[:, :], top[:, :], ACT.Exp, bias=ntop[:, :], accum_out=ssum[:, :]))
        a_step.inc(act.activation(Sc[:, :], Sc[:, :], ACT.Exp, bias=ntop[:, :]))
        a_step.inc(act.activation(Wk[:, :], Wk[:, :], ACT.Exp, bias=ntop[:, :]))
        a_step.wait(dve, r)
        t_step.inc(dve.tensor_scalar(ssum[:, :], ssum[:, :], float(H1), None, ALU.mult))
        t_step.wait(dve, r, 10)
        t_step.inc(dve.reciprocal(ssum[:, :], ssum[:, :]))
        t_step.inc(dve.tensor_tensor(Sc[:, :], Sc[:, :], Wk[:, :], ALU.subtract))
        t_step.wait(dve, r, 12)
        t_step.inc(dve.scalar_tensor_tensor(amean[:, qt, :], Sc[:, :], ssum[:, :], amean[:, qt, :], ALU.mult, ALU.add))

    ctxn_d = ins["ctx_768"].rearrange("b (c p) d -> b p c d", p=P)
    for b in range(NB):
        ldc = Load(nc, f"ld_cn{b}")
        ldc.add(act.dma_start(cn[:, :, :], ctxn_d[b]))
        with nc.Fori(0, H1, 1) as h:
            stack1(b, h)
            row_tile(b, h, 0)
            row_tile(b, h, 1)
        t_step.wait(pe, NM * (b + 1) - 1 if b else 2 * H1 - 1)
        t_step.wait(dve, NM * (b + 1) - 1 if b else 2 * H1 - 1)
        PE.after(ldc.token())
        prev = [None, None]
        for qt in range(2):
            for g in range(NCH // 4):
                j = g % 2
                if prev[j]:
                    PE.after(prev[j])
                for c in range(4):
                    k0 = (4 * g + c) * P
                    t = pe.transpose(bank[:, j, c * P:(c + 1) * P], amean[:, qt, k0:k0 + P], ident[:, :])
                t = PE.done(t)
                AC.after(t)
                if g >= 2:
                    AC.after(used[j])
                elif qt or b:
                    AC.after(used[j])
                t_c = AC.done(act.copy(aT[j][:, :, :].rearrange("p c q -> p (c q)"), bank[:, j, :]))
                prev[j] = t_c
                PE.after(t_c)
                for c in range(4):
                    t = pe.matmul(bank[:, 2 + qt, 0:DC], aT[j][:, c, :], cn[:, 4 * g + c, :], start=(g == 0 and c == 0),
                                  stop=(g == NCH // 4 - 1 and c == 3))
                t = PE.done(t)
                used = {**(used if (g or qt or b) else {}), j: t}
            DV.after(t)
            t_c0 = DV.done(dve.tensor_copy(c0[:, b * 2 + qt, :], bank[:, 2 + qt, 0:DC]))
        DV.after(used[0], used[1])
        if b == 0:
            t_z = DV.done(dve.memset(amean[:, :, :], 0.0))
        PE.after(DV.last())
        act.wait_ge(*DV.last())
        act.wait_ge(*PE.last())
    tm8 = sb("tm8", [P, NT], mybir.dt.uint8)
    tmask = sb("tmask", [P, NT])
    with nc.allow_non_contiguous_dma(reason="512 mask bytes"):
        t_tm = load("ld_tm", [(tm8[:, :], ins["mask_BxS_bf1"].rearrange("b (t p) -> p (b t)", p=P))])
    DV.after(t_tm, t_c0)
    t = DV.done(dve.tensor_copy(tmask[:, :], tm8[:, :]))
    DV.after(t)
    for i in range(NT):
        t = DV.done(dve.tensor_scalar(c0[:, i, :], c0[:, i, :], tmask[:, i:i + 1], None, ALU.mult))
    PE.after(t)
    for k, (lo, n) in enumerate(((0, P), (P, DCM))):
        for i in range(NT):
            t = PE.done(pe.transpose(bank[0:n, 4 + k, i * P:(i + 1) * P], c0[:, i, lo:lo + n], ident[:, :]))
        AC.after(t)
        t_c0T = AC.done(act.copy(c0T[k][:, :], bank[0:n, 4 + k, :]))
    phase_ends()

    phase_begins()
    wv1, wv2 = sb("wv1", [P, D]), sb("wv2", [DCM, D])
    film = sb("film", [P, 2, 2, 2 * D])
    bfilm = sb("bfilm", [1, 2, 2 * D])
    vecs = sb("vecs", [P, 7, D])
    mgate = sb("mgate", [P, 1])
    NAMES = ("g_norm_in", "b_norm_in", "g_norm_out", "b_norm_out", "g_ffn", "b_ffn", "D_skip")
    pairs = [(wv1[:, :], ins["L1_xattn_Wv"][0:P, :]), (wv2[:, :], ins["L1_xattn_Wv"][P:DC, :]),
             (mgate[:, :], ins["L1_xattn_mod_gate"].rearrange("(a n) -> a n", a=1).to_broadcast([P, 1]))]
    pairs += [(vecs[:, k, :], row("L1_xattn_" + n).to_broadcast([P, D])) for k, n in enumerate(NAMES)]
    for k, n in enumerate(("in", "out")):
        pairs += [(film[:, k, :, :], ins["L1_xattn_W_film_" + n].rearrange("(k p) n -> p k n", p=P)),
                  (bfilm[:, k, :], row("L1_xattn_b_film_" + n))]
    HID = 4 * D
    MT = HID // P
    W1 = sb("W1", [P, 2, HID])
    W2 = sb("W2", [P, MT, D])
    b1 = sb("b1", [P, MT])
    b2 = sb("b2", [1, D])
    pairs += [(W1[:, :, :], ins["L1_xattn_W1"].rearrange("(k p) n -> p k n", p=P)),
              (W2[:, :, :], ins["L1_xattn_W2"].rearrange("(k p) n -> p k n", p=P)), (b2[:, :], row("L1_xattn_b2"))]
    with nc.allow_non_contiguous_dma(reason="1024 bias values"):
        t_w = load("ld_film", pairs + [(b1[:, :], ins["L1_xattn_b1"].rearrange("(k p) -> p k", p=P))])
    VEC = {n: vecs[:, k, :] for k, n in enumerate(NAMES)}

    def seq(*fns):
        for fn in fns:
            DV.after(DV.last())
            t = DV.done(fn())
        return t

    ctT = sb("ctT", [P, 2, T])
    mod = sb("mod", [P, 2, NT, 2 * D])
    PE.after(t_w, t_c0T)
    for m in range(2):
        pe.matmul(bank[:, m, :], wv1[:, m * P:(m + 1) * P], c0T[0][:, :], start=True, stop=False)
        t = PE.done(pe.matmul(bank[:, m, :], wv2[:, m * P:(m + 1) * P], c0T[1][:, :], start=False, stop=True))
        AC.after(t)
        t_ct = AC.done(act.copy(ctT[:, m, :], bank[:, m, :]))
    AC.after(t_w)
    for k in range(2):
        toks = []
        PE.after(t_ct)
        for i in range(NT):
            if k and i == 0:
                PE.after(t_mod)
            for kt in range(2):
                pe.matmul(bank[:, 4 + i, :], ctT[:, kt, i * P:(i + 1) * P], film[:, k, kt, :], start=(kt == 0), stop=False)
            t = PE.done(pe.matmul(bank[:, 4 + i, :], ones[0:1, 0:P], bfilm[0:1, k, :], start=False, stop=True))
            AC.after(t)
            t_mod = AC.done(act.activation(mod[:, k, i, :], bank[:, 4 + i, :], ACT.Copy, scale=mgate[:, 0:1]))

    def affine(dst, src, g, b, i):
        seq(lambda: dve.tensor_tensor(dst[:, i, :], src[:, i, :], VEC[g], ALU.mult),
            lambda: dve.tensor_tensor(dst[:, i, :], dst[:, i, :], VEC[b], ALU.add))

    def modulate(dst, k, i):
        seq(lambda: dve.scalar_tensor_tensor(dst[:, i, :], mod[:, k, i, 0:D], 1.0, dst[:, i, :], ALU.add, ALU.mult),
            lambda: dve.tensor_tensor(dst[:, i, :], dst[:, i, :], mod[:, k, i, D:2 * D], ALU.add))

    layer_norm(xh, xt, [t_xt])
    DV.after(t_mod, t_w)
    for i in range(NT):
        affine(xh, xh, "g_norm_in", "b_norm_in", i)
        modulate(xh, 0, i)
    t_xh = DV.last()
    Xf = sb("Xf", [P, 2, 2, NB, D])
    Yf = sb("Yf", [P, 2, 2, NB, D])
    tmpf = sb("tmpf", [P, NB, D])
    xhv = xh[:, :, :].rearrange("p (b t) d -> p t b d", b=NB)
    PE.after(t_xh, t_tab, t_ct)
    for c in range(2):
        for ft in range(2):
            o = bank[:, c * 2 + ft, :]
            for lt in range(2):
                t = pe.matmul(o, tabs[:, c, lt, ft * P:(ft + 1) * P], xhv[:, lt, :, :], start=(lt == 0), stop=(lt == 1))
            t = PE.done(t)
            AC.after(t)
            t_Xf = AC.done(act.copy(Xf[:, c, ft, :, :].rearrange("p b d -> p (b d)"), o))
    DV.after(t_Xf, t_Kf)
    for ft in range(2):
        kb = [Kf[:, c, ft:ft + 1, :].to_broadcast([P, NB, D]) for c in range(2)]
        Xc, Xs = (Xf[:, c, ft, :, :] for c in range(2))
        for c, (a0, a1, op) in enumerate(((kb[0], kb[1], ALU.subtract), (kb[1], kb[0], ALU.add))):
            seq(lambda: dve.tensor_tensor(Yf[:, c, ft, :, :], Xc, a0, ALU.mult),
                lambda: dve.tensor_tensor(tmpf[:, :, :], Xs, a1, ALU.mult),
                lambda: dve.tensor_tensor(Yf[:, c, ft, :, :], Yf[:, c, ft, :, :], tmpf[:, :, :], op))
    PE.after(DV.last())
    for nt in range(2):
        for n_, (c, ft) in enumerate(((0, 0), (0, 1), (1, 0), (1, 1))):
            t = pe.matmul(bank[:, nt, :], tabs[:, 2 + c, ft, nt * P:(nt + 1) * P], Yf[:, c, ft, :, :].rearrange("p b d -> p (b d)"),
                          start=(n_ == 0), stop=(n_ == 3))
        t = PE.done(t)
    DV.after(t)
    xt2 = sb("xt2", [P, NT, D])
    for i in range(NT):
        b, nt = i // 2, i % 2
        seq(lambda: dve.tensor_tensor(xh[:, i, :], xh[:, i, :], VEC["D_skip"], ALU.mult),
            lambda: dve.tensor_tensor(xh[:, i, :], bank[:, nt, b * D:(b + 1) * D], xh[:, i, :], ALU.add))
        modulate(xh, 1, i)
        seq(lambda: dve.tensor_tensor(xt2[:, i, :], xh[:, i, :], xt[:, i, :], ALU.add))
    layer_norm(xh, xt2, [DV.last()])
    for i in range(NT):
        affine(xh, xh, "g_ffn", "b_ffn", i)
    t_hT = features_on_partitions(xT, lambda i, kt: xh[:, i, kt * P:(kt + 1) * P], [DV.last()], [], banks=(2, 3))
    ffh = sb("ffh", [P, MT, T])
    PE.after(t_hT)
    AC.after(t_w)
    used = [None] * 2
    for m in range(MT):
        j = m % 2
        if used[j]:
            PE.after(used[j])
        for kt in range(2):
            t = pe.matmul(bank[:, 2 + j, :], W1[:, kt, m * P:(m + 1) * P], xT[:, kt, :], start=(kt == 0), stop=(kt == 1))
        t = PE.done(t)
        AC.after(t)
        used[j] = t_h = AC.done(act.activation(ffh[:, m, :], bank[:, 2 + j, :], ACT.Gelu, bias=b1[:, m:m + 1]))
    PE.after(t_h)
    for i in range(NT):
        for m in range(MT):
            pe.matmul(bank[:, 4 + i, 0:D], ffh[:, m, i * P:(i + 1) * P], W2[:, m, :], start=(m == 0), stop=False)
        t = PE.done(pe.matmul(bank[:, 4 + i, 0:D], ones[0:1, 0:P], b2[0:1, :], start=False, stop=True))
        DV.after(t)
        t = DV.done(dve.tensor_tensor(xt2[:, i, :], bank[:, 4 + i, 0:D], xt2[:, i, :], ALU.add))
    layer_norm(xh, xt2, [t])
    for i in range(NT):
        affine(xh, xh, "g_norm_out", "b_norm_out", i)
        seq(lambda: dve.tensor_tensor(x[:, i, :], x[:, i, :], xh[:, i, :], ALU.add))
    t_x4 = DV.last()
    phase_ends()
    phase_ends()

    HR, DR = 8, 32
    phase_begins()
    xr = xn
    t_xn = layer_norm(xr, x, [t_x4])
    t_xT = features_on_partitions(xT, lambda i, kt: xr[:, i, kt * P:(kt + 1) * P], [t_xn], [])
    wr_ = {c: sb(f"wr_{c}", [P, 2, D]) for c in "QKVGO"}
    wsw = {c: sb(f"wsw_{c}", [P, 2, D]) for c in "QK"}
    rtab = sb("rtab", [P, 4, 2, S])
    rmask = sb("rmask", [P, 3, P])
    gnv = sb("gnv", [P, 2, D])
    pairs = [(wr_[c][:, k, :].rearrange("p (h e) -> p h e", h=HR), ins["L1_attn_W_" + c][:, k * P:(k + 1) * P, :].rearrange("h p e -> p h e"))
             for c in "QKV" for k in range(2)]
    pairs += [(wr_[c][:, :, :], ins["L1_attn_W_" + c].rearrange("(k p) n -> p k n", p=P)) for c in "GO"]
    pairs += [(rtab[:, k, :, :], ins["rotary"][k].rearrange("(t p) n -> p t n", p=P)) for k in range(4)]
    pairs += [(gnv[:, k, :], row("L1_attn_gn_" + n).to_broadcast([P, D])) for k, n in enumerate(("weight", "bias"))]
    t_w = load("ld_ret", pairs)
    t = PO.done(pool.memset(rmask[:, :, :], 1.0))
    PO.after(t)
    for k in (0, 2):
        t_rm = PO.done(pool.affine_select(out=rmask[:, k, :], in_=rmask[:, k, :], compare_op=ALU.is_ge, fill=0.0, base=0,
                                          pattern=[[1, P]], channel_multiplier=-1))
    DV.after(t_w)
    for c in "QK":
        for par in range(2):
            t_sw = DV.done(dve.tensor_copy(wsw[c][:, :, :].rearrange("p k (e two) -> p (k e) two", two=2)[:, :, par],
                                           wr_[c][:, :, :].rearrange("p k (e two) -> p (k e) two", two=2)[:, :, 1 - par]))
    qkr = {c: sb(f"qkr_{c}", [P, 2, T]) for c in "QK"}
    rtmp = sb("rtmp", [P, T])
    PE.after(t_w, t_sw, t_xT)
    last_rot = {}
    for n_, c in enumerate("QK"):
        for m in range(2):
            b0 = 2 * m
            if n_:
                PE.after(last_rot[m])
            for k, w in enumerate((wr_[c], wsw[c])):
                for kt in range(2):
                    t = pe.matmul(bank[:, b0 + k, :], w[:, kt, m * P:(m + 1) * P], xT[:, kt, :], start=(kt == 0), stop=(kt == 1))
            t = PE.done(t)
            DV.after(t)
            ctab, stab = (rtab[:, 2 * n_ + k, m:m + 1, :].to_broadcast([P, NB, S]) for k in range(2))
            v3 = lambda a: a.rearrange("p (b s) -> p b s", b=NB)
            last_rot[m] = seq(lambda: dve.tensor_tensor(v3(qkr[c][:, m, :]), v3(bank[:, b0, :]), ctab, ALU.mult),
                              lambda: dve.tensor_tensor(v3(rtmp[:, :]), v3(bank[:, b0 + 1, :]), stab, ALU.mult),
                              lambda: dve.tensor_tensor(qkr[c][:, m, :], qkr[c][:, m, :], rtmp[:, :], ALU.add))
    t_rot = DV.last()
    vr = sb("vr", [P, NT, D])
    gr = sb("gr", [P, NT, D])
    for i in range(NT):
        for k, w in enumerate((wr_["V"], wr_["G"])):
            for kt in range(2):
                t = pe.matmul(bank[:, 4 + i, k * D:(k + 1) * D], xT[:, kt, i * P:(i + 1) * P], w[:, kt, :], start=(kt == 0), stop=(kt == 1))
        t = PE.done(t)
        AC.after(t)
        AC.done(act.copy(vr[:, i, :], bank[:, 4 + i, 0:D]))
        t_v = AC.done(act.activation(gr[:, i, :], bank[:, 4 + i, D:2 * D], ACT.Silu))
    sR = [sb(f"sR{j}", [P, 3, P]) for j in range(2)]
    yr = sb("yr", [P, NT, HR, DR])
    PE.after(t_rot, t_v)
    DV.after(t_rm)
    masked, used, y_read = {}, {}, {}
    for b in range(NB):
        for h in range(HR):
            j = h % 2
            if j in masked:
                PE.after(masked[j])
            rs = slice((h % 4) * DR, (h % 4 + 1) * DR)
            kq = lambda c, lo, n: qkr[c][rs, h // 4, b * S + lo:b * S + lo + n]
            pe.matmul(bank[:, j, 0:2 * P], kq("K", 0, P), kq("Q", 0, 2 * P), start=True, stop=True)
            t = PE.done(pe.matmul(bank[:, j, 2 * P:3 * P], kq("K", P, P), kq("Q", P, P), start=True, stop=True))
            DV.after(t)
            if j in used:
                DV.after(used[j])
            masked[j] = DV.done(dve.tensor_tensor(sR[j][:, :, :].rearrange("p c q -> p (c q)"), bank[:, j, 0:3 * P],
                                                  rmask[:, :, :].rearrange("p c q -> p (c q)"), ALU.mult))
            PE.after(masked[j])
            if b and h == 0:
                PE.after(y_read[0], y_read[1])
            vv = lambda kt: vr[:, b * 2 + kt, h * DR:(h + 1) * DR]
            o = [bank[:, 2 + qt, h * DR:(h + 1) * DR] for qt in range(2)]
            pe.matmul(o[0], sR[j][:, 0, :], vv(0), start=True, stop=True)
            pe.matmul(o[1], sR[j][:, 1, :], vv(0), start=True, stop=False)
            used[j] = PE.done(pe.matmul(o[1], sR[j][:, 2, :], vv(1), start=False, stop=True))
        for qt in range(2):
            AC.after(used[1])
            y_read[qt] = AC.done(act.copy(yr[:, b * 2 + qt, :, :].rearrange("p h d -> p (h d)"), bank[:, 2 + qt, 0:D]))
    gm, gv = sb("gm", [P, NT * HR]), sb("gv", [P, NT * HR])
    ysq = sb("ysq", [P, NT * HR, DR])
    y3 = yr[:, :, :, :].rearrange("p t h d -> p (t h) d")
    gb = lambda a: a[:, :].rearrange("p (n a) -> p n a", a=1).to_broadcast([P, NT * HR, DR])
    DV.after(y_read[0], y_read[1])
    t = seq(lambda: dve.tensor_reduce(gm[:, :], y3, AX.X, ALU.add),
            lambda: dve.tensor_scalar(gm[:, :], gm[:, :], 1.0 / DR, None, ALU.mult),
            lambda: dve.tensor_tensor(y3, y3, gb(gm), ALU.subtract),
            lambda: dve.tensor_tensor(ysq[:, :, :], y3, y3, ALU.mult),
            lambda: dve.tensor_reduce(gv[:, :], ysq[:, :, :], AX.X, ALU.add),
            lambda: dve.tensor_scalar(gv[:, :], gv[:, :], 1.0 / DR, EPS, ALU.mult, ALU.add))
    AC.after(t)
    t = AC.done(act.sqrt(gv[:, :], gv[:, :]))
    DV.after(t)
    seq(lambda: dve.reciprocal(gv[:, :], gv[:, :]),
        lambda: dve.tensor_tensor(y3, y3, gb(gv), ALU.mult))
    for i in range(NT):
        yi = yr[:, i, :, :].rearrange("p h d -> p (h d)")
        seq(lambda: dve.tensor_tensor(yi, yi, gnv[:, 0, :], ALU.mult),
            lambda: dve.tensor_tensor(yi, yi, gnv[:, 1, :], ALU.add),
            lambda: dve.tensor_tensor(yi, yi, gr[:, i, :], ALU.mult))
    t_yT = features_on_partitions(xT, lambda i, kt: yr[:, i, :, :].rearrange("p h d -> p (h d)")[:, kt * P:(kt + 1) * P],
                                  [DV.last()], [t_rot])
    t_x5 = add_to_x(project_tokens(xT, wr_["O"], None, [t_yT, t_v], first_bank=4), first_bank=4)
    phase_ends()

    KA = 8
    phase_begins()
    ids = sb("ids", [1, KA], I32)
    wts = sb("wts", [P, KA])
    wsel = sb("wsel", [P, KA, 2, D])
    bsel = sb("bsel", [1, KA, D])
    wmix = sb("wmix", [P, 2, D])
    wmT = sb("wmT", [P, 2, D])
    bmix = sb("bmix", [1, D])
    t_ids = load("ld_ids", [(ids[:, :], row("L1_ffn_ids")), (wts[:, :], row("L1_ffn_weights").to_broadcast([P, KA]))])
    sp.wait_ge(*t_ids)
    ld = Load(nc, "ld_sel")
    for k in range(KA):
        a = sp.value_load(ids[0:1, k:k + 1], min_val=0, max_val=31)
        ld.add(sp.dma_start(wsel[:, k, :, :], ins["L1_ffn_W"][bass.ds(a, 1), :, :].rearrange("a (t p) d -> p (a t) d", p=P)))
        ld.add(sp.dma_start(bsel[:, k, :], ins["L1_ffn_b"][bass.ds(a, 1), :]))
    t_xn = layer_norm(xn, x, [t_x5])
    t_xT = features_on_partitions(xT, lambda i, kt: xn[:, i, kt * P:(kt + 1) * P], [t_xn], [])
    DV.after(ld.token(), t_ids)
    flat = lambda t: t.rearrange("p t d -> p (t d)")
    seq(lambda: dve.tensor_scalar(flat(wmix[:, :, :]), flat(wsel[:, 0, :, :]), wts[:, 0:1], None, ALU.mult))
    seq(lambda: dve.tensor_scalar(bmix[:, :], bsel[:, 0, :], wts[0:1, 0:1], None, ALU.mult))
    for k in range(1, KA):
        seq(lambda: dve.scalar_tensor_tensor(flat(wmix[:, :, :]), flat(wsel[:, k, :, :]), wts[:, k:k + 1], flat(wmix[:, :, :]), ALU.mult, ALU.add))
        seq(lambda: dve.scalar_tensor_tensor(bmix[:, :], bsel[:, k, :], wts[0:1, k:k + 1], bmix[:, :], ALU.mult, ALU.add))
    PE.after(DV.last())
    for kt in range(2):
        for ot in range(2):
            t = PE.done(pe.transpose(bank[:, 2 + kt, ot * P:(ot + 1) * P], wmix[:, ot, kt * P:(kt + 1) * P], ident[:, :]))
        AC.after(t)
        t_wm = AC.done(act.copy(wmT[:, kt, :], bank[:, 2 + kt, 0:D]))
    t_x6 = add_to_x(project_tokens(xT, wmT, bmix[0:1, :], [t_wm, t_xT], first_bank=4), first_bank=4)

    sp.wait_ge(*t_x6)
    done = Load(nc, "stored")
    done.add(sp.dma_start(out.rearrange("b (t p) d -> p (b t) d", p=P), x[:, :, :]))
    sp.wait_ge(*done.token())


def kernel(**inputs):
    import numpy as _np
    import concourse.bacc as _bacc
    from concourse.bass_utils import run_bass_kernel_spmd as _run

    nc = _bacc.Bacc("TRN2", target_bir_lowering=False, num_devices=1)
    arrays, aps = {}, {}
    for name in inputs:
        a = _np.ascontiguousarray(inputs[name])
        if a.shape == ():
            a = a.reshape(1)
        if a.dtype == _np.bool_:
            a = a.view(_np.uint8)
        if name in UNUSED:
            continue
        arrays["in_" + name] = a
        aps[name] = nc.dram_tensor("in_" + name, a.shape, mybir.dt.from_np(a.dtype), kind="ExternalInput").ap()
    for name, a in constants().items():
        arrays["in_" + name] = a
        aps[name] = nc.dram_tensor("in_" + name, a.shape, mybir.dt.from_np(a.dtype), kind="ExternalInput").ap()
    out = nc.dram_tensor("out_x", (NB, S, D), F32, kind="ExternalOutput").ap()
    build(nc, aps, out)
    r = _run(nc, [arrays], core_ids=[0])
    return r.results[0]["out_x"]
```

```python
import math
from contextlib import ExitStack

import numpy as np

import concourse.bass as bass
from concourse import mybir

F32 = mybir.dt.float32
BF16 = mybir.dt.bfloat16
I32 = mybir.dt.int32
ALU = mybir.AluOpType
ACT = mybir.ActivationFunctionType
AX = mybir.AxisListType

P = 128
D = 256
DC = 192
NB = 2
S = 256
T = NB * S
NT = T // P
S2 = 4096
H0, D0 = 16, 16
BLK = 512
NBB = S2 // BLK
NBLK = NB * NBB
NH = NB * H0
NCH = S2 // P
VW = D0 + 1
NSTK = 6
STACK = ((0, 0), (0, 1), (0, 2), (1, 0), (1, 1), (2, 0))
EPS = 1e-5


class Count:

    def __init__(self, nc, name, per, credit_steps=0):
        self.sem = nc.alloc_semaphore(name)
        self.per, self.credit = per, per * credit_steps + 1 if credit_steps else 0

    def give(self, eng):
        if self.credit:
            eng.sem_inc(self.sem, self.credit)

    def wait(self, eng, n, k=None):
        eng.wait_ge(self.sem, n * self.per + (self.per if k is None else k) + self.credit)

    def inc(self, ins):
        return ins.then_inc(self.sem, 1)


class Line:

    def __init__(self, nc, eng, name):
        self.eng, self.sem, self.n = eng, nc.alloc_semaphore(name), 0
        self.seen = {}

    def after(self, *tokens):
        for sem, value in tokens:
            if self.seen.get(sem.name, 0) < value:
                self.eng.wait_ge(sem, value)
                self.seen[sem.name] = value

    def done(self, ins):
        self.n += 1
        ins.then_inc(self.sem, 1)
        return (self.sem, self.n)

    def last(self):
        return (self.sem, self.n)


class Load:

    def __init__(self, nc, name):
        self.sem, self.n = nc.alloc_semaphore(name), 0

    def add(self, ins):
        self.n += 16
        ins.then_inc(self.sem, 16)

    def token(self):
        return (self.sem, self.n)


UNUSED = ()


def constants():
    w = 2 * np.pi * (np.arange(S)[None, :] + 0.5) * np.arange(S)[:, None] / (2 * S)
    dft = np.stack([np.cos(w), np.sin(w), np.cos(w).T / S, np.sin(w).T / S]).astype(np.float32)
    heads, width, base_len = 8, 32, 512.0
    pos = np.arange(S, dtype=np.float64)[None, :]
    base = ((np.arange(0, width, 2) + 0.4 * width) / (1.4 * width))[:, None]
    scale = base ** (pos / base_len)
    angle = pos / 10000.0 ** (np.arange(width // 2) / (width // 2))[:, None]
    gamma = 1 - np.exp(np.linspace(math.log(1 / 32), math.log(1 / 512), heads))[:, None]
    sign = np.tile([-1.0, 1.0], width // 2)[:, None]
    tabs = []
    for power in (1, -1):
        for f, s in ((np.cos, 1.0), (np.sin, sign)):
            t = np.repeat(f(angle) * scale ** power, 2, axis=0) * s
            tabs.append((t[None] * (gamma ** (power * pos))[:, None, :]).reshape(heads * width, S))
    return {"dft": dft, "rotary": np.stack(tabs).astype(np.float32)}


def build(nc, ins, out):
    pe, act, dve, pool, sp = nc.tensor, nc.scalar, nc.vector, nc.gpsimd, nc.sync
    PE, AC, DV, PO = Line(nc, pe, "pe_line"), Line(nc, act, "act_line"), Line(nc, dve, "dve_line"), Line(nc, pool, "pool_line")
    ENG = {id(x.sem.name): x for x in (PE, AC, DV, PO)}

    scopes = []

    def sb(name, shape, dt=F32):
        return scopes[-1].enter_context(nc.sbuf_tensor(name, shape, dt))

    def phase_begins():
        scopes.append(ExitStack())

    def phase_ends():
        nc.all_engine_barrier()
        scopes.pop().close()

    phase_begins()

    def load(name, pairs, eng=sp):
        ld = Load(nc, name)
        with nc.allow_non_contiguous_dma(reason="some are short vectors"):
            for dst, src in pairs:
                ld.add(eng.dma_start(dst, src))
        return ld.token()

    def row(name):
        return ins[name].rearrange("(a n) -> a n", a=1)

    bank = nc.alloc_psum_tensor("bank", [P, 8, 512], F32)

    ident = sb("ident", [P, P])
    identb = sb("identb", [P, P], BF16)
    ones = sb("ones", [P, 512])
    x = sb("x", [P, NT, D])
    xn = sb("xn", [P, NT, D])
    xT = sb("xT", [P, 2, T])
    stats = sb("stats", [P, NT, 6])
    mv = sb("mv", [P, NT, 2])
    rstd = sb("rstd", [P, NT])

    t_x = load("ld_x", [(x[:, :, :], ins["x"].rearrange("b (t p) d -> p (b t) d", p=P))])
    zeros = sb("zeros", [P, 512])
    t_zeros = DV.done(dve.memset(zeros[:, :], 0.0))
    t_ones = DV.done(dve.memset(ones[:, :], 1.0))
    t = PO.done(pool.memset(ident[:, :], 0.0))
    PO.after(t)
    t_ident = PO.done(pool.affine_select(out=ident[:, :], in_=ident[:, :], compare_op=ALU.not_equal, fill=1.0,
                                         base=0, pattern=[[-1, P]], channel_multiplier=1))
    DV.after(t_ident)
    t_identb = DV.done(dve.tensor_copy(identb[:, :], ident[:, :]))

    spare = nc.alloc_semaphore("spare")

    def hold(eng):
        eng.sem_inc(spare, 1)

    def layer_norm(dst, src, after, n_tiles=NT):
        DV.after(*after)
        for i in range(n_tiles):
            t = DV.done(dve.bn_stats(stats[:, i, :], src[:, i, :]))
        DV.after(t)
        for i in range(n_tiles):
            t = DV.done(dve.bn_aggr(mv[:, i, :], stats[:, i, :]))
        DV.after(t)
        t = DV.done(dve.tensor_scalar(rstd[:, 0:n_tiles], mv[:, 0:n_tiles, 1], EPS, None, ALU.add))
        AC.after(t)
        t = AC.done(act.sqrt(rstd[:, 0:n_tiles], rstd[:, 0:n_tiles]))
        DV.after(t)
        t = DV.done(dve.reciprocal(rstd[:, 0:n_tiles], rstd[:, 0:n_tiles]))
        DV.after(t)
        for i in range(n_tiles):
            t = DV.done(dve.tensor_scalar(dst[:, i, :], src[:, i, :], mv[:, i, 0:1], rstd[:, i:i + 1],
                                          ALU.subtract, ALU.mult))
        return t

    def features_on_partitions(dst, src, after, free, banks=(0, 1)):
        PE.after(*after, *free, t_ident)
        toks = []
        for kt in range(D // P):
            for i in range(NT):
                t = PE.done(pe.transpose(bank[:, banks[kt], i * P:(i + 1) * P], src(i, kt), ident[:, :]))
            AC.after(t, *free)
            toks.append(AC.done(act.copy(dst[:, kt, :], bank[:, banks[kt], :])))
        return toks[-1]

    NSTATE, LA, LB = 64, 32, 8
    Ap = [sb(f"Ap{c}", [P, 4, LA, 32]) for c in "ri"]
    Bp = [sb(f"Bp{c}", [P, 4, LB, 32]) for c in "ri"]
    phase_begins()
    W2 = 2 * NSTATE
    ldt = sb("ldt", [P, 2])
    dt_n = sb("dt_n", [P, 2])
    dt_r = sb("dt_r", [P, 2])
    dt_p = sb("dt_p", [P, 2])
    dt_i = sb("dt_i", [P, 2], I32)
    are, aim, cre, cim = (sb(n, [P, 2, NSTATE]) for n in ("are", "aim", "cre", "cim"))
    t_s4 = load("ld_s4", [(tile[:, :, :], ins["L1_xattn_" + n].rearrange("(t p) n -> p t n", p=P))
                          for tile, n in ((are, "A_re"), (aim, "A_im"), (cre, "C_re"), (cim, "C_im"))]
                + [(ldt[:, :], ins["L1_xattn_log_dt"].rearrange("(t p) -> p t", p=P))], eng=act)

    def ts(dst, src, a, b=None, op0=ALU.mult, op1=None, line=None, eng=None):
        line = line or DV
        line.after(line.last())
        return line.done(line.eng.tensor_scalar(dst, src, a, b, op0, op1) if op1 is not None
                         else line.eng.tensor_scalar(dst, src, a, b, op0))

    def tt(dst, a, b, op, line=None):
        line = line or DV
        line.after(line.last())
        return line.done(line.eng.tensor_tensor(dst, a, b, op))

    BIG = 1.5 * 2.0 ** 23
    LN2_HI = 0.693359375
    DV.after(t_s4)
    ts(dt_n[:, :], ldt[:, :], 1.0 / math.log(2.0), BIG, ALU.mult, ALU.add)
    ts(dt_n[:, :], dt_n[:, :], BIG, None, ALU.subtract)
    ts(dt_r[:, :], dt_n[:, :], -LN2_HI)
    tt(dt_r[:, :], ldt[:, :], dt_r[:, :], ALU.add)
    ts(dt_p[:, :], dt_n[:, :], -(math.log(2.0) - LN2_HI))
    tt(dt_r[:, :], dt_r[:, :], dt_p[:, :], ALU.add)
    ts(dt_p[:, :], dt_r[:, :], 1.0 / math.factorial(8), 1.0 / math.factorial(7), ALU.mult, ALU.add)
    for k in range(6, -1, -1):
        tt(dt_p[:, :], dt_p[:, :], dt_r[:, :], ALU.mult)
        ts(dt_p[:, :], dt_p[:, :], 1.0 / math.factorial(k), None, ALU.add)
    ts(dt_i[:, :], dt_n[:, :], 127.0, 2.0 ** 23, ALU.add, ALU.mult)
    t_dt = tt(dt_p[:, :], dt_p[:, :], dt_i[:, :].bitcast(F32), ALU.mult)

    HALVINGS = 10
    wr, wi, er, ei, fr, fi, g1, g2 = (sb(n, [P, W2]) for n in ("wr", "wi", "er", "ei", "fr", "fi", "g1", "g2"))
    PO.after(t_dt, t_s4)
    for t_ in range(2):
        sl = slice(t_ * NSTATE, (t_ + 1) * NSTATE)
        ts(wr[:, sl], are[:, t_, :], dt_p[:, t_:t_ + 1], 2.0 ** -HALVINGS, ALU.mult, ALU.mult, line=PO)
        ts(wi[:, sl], aim[:, t_, :], dt_p[:, t_:t_ + 1], 2.0 ** -HALVINGS, ALU.mult, ALU.mult, line=PO)

    def cmul(outr, outi, ar, ai, br, bi, s1, s2):
        tt(s1, ar, br, ALU.mult, PO)
        tt(s2, ai, bi, ALU.mult, PO)
        tt(outr, s1, s2, ALU.subtract, PO)
        tt(s1, ar, bi, ALU.mult, PO)
        tt(s2, ai, br, ALU.mult, PO)
        return tt(outi, s1, s2, ALU.add, PO)

    f, G1, G2 = slice(None), g1[:, :], g2[:, :]
    ts(er[:, :], wr[:, :], 1.0 / 5.0, 1.0, ALU.mult, ALU.add, line=PO)
    ts(ei[:, :], wi[:, :], 1.0 / 5.0, 0.0, ALU.mult, ALU.add, line=PO)
    for k in (4, 3, 2):
        cmul(fr[:, :], fi[:, :], er[:, :], ei[:, :], wr[:, :], wi[:, :], G1, G2)
        ts(er[:, :], fr[:, :], 1.0 / k, 1.0, ALU.mult, ALU.add, line=PO)
        ts(ei[:, :], fi[:, :], 1.0 / k, 0.0, ALU.mult, ALU.add, line=PO)
    cmul(fr[:, :], fi[:, :], er[:, :], ei[:, :], wr[:, :], wi[:, :], G1, G2)
    a, b = (fr, fi), (er, ei)
    for k in range(HALVINGS):
        ts(wr[:, :], a[0][:, :], 1.0, 2.0, ALU.mult, ALU.add, line=PO)
        cmul(b[0][:, :], b[1][:, :], a[0][:, :], a[1][:, :], wr[:, :], a[1][:, :], G1, G2)
        a, b = b, a
    AR, AI = (q[:, :, :].rearrange("p t n -> p (t n)") for q in (are, aim))
    CR, CI = (q[:, :, :].rearrange("p t n -> p (t n)") for q in (cre, cim))
    tt(G1, AR, AR, ALU.mult, PO)
    tt(G2, AI, AI, ALU.mult, PO)
    t = tt(G1, G1, G2, ALU.add, PO)
    DV.after(t)
    t = DV.done(dve.reciprocal(wi[:, :], g1[:, :]))
    PO.after(t)
    ts(wi[:, :], wi[:, :], 2.0, 0.0, ALU.mult, ALU.add, line=PO)
    tt(AR, AR, wi[:, :], ALU.mult, PO)
    tt(AI, AI, wi[:, :], ALU.mult, PO)
    ts(AI, AI, -1.0, 0.0, ALU.mult, ALU.add, line=PO)
    cmul(b[0][:, :], b[1][:, :], AR, AI, CR, CI, G1, G2)
    cmul(AR, AI, b[0][:, :], b[1][:, :], a[0][:, :], a[1][:, :], G1, G2)
    t_z = ts(a[0][:, :], a[0][:, :], 1.0, 1.0, ALU.mult, ALU.add, line=PO)

    phase_begins()
    V = sb("V", [P, NB * NCH, H0, VW])
    phase_begins()
    wkv1 = sb("wkv1", [P, 2 * D + P])
    wkv2 = sb("wkv2", [DC - P + 1, 2 * D + P])
    wk_all = [("L0_xattn_Wk", 0, D), ("L0_xattn_Wv", D, D), ("L1_xattn_Wk", 2 * D, P)]
    pairs = []
    for name, at, n in wk_all:
        pairs += [(wkv1[:, at:at + n], ins[name][0:P, :]), (wkv2[0:DC - P, at:at + n], ins[name][P:DC, :])]
    pairs += [(wkv2[DC - P:DC - P + 1, 0:D], row("L0_xattn_bk")), (wkv2[DC - P:DC - P + 1, D:2 * D], row("L0_xattn_bv"))]
    t_m = DV.done(dve.memset(wkv2[DC - P:DC - P + 1, :], 0.0))
    act.wait_ge(*t_m)
    t_wkv = load("ld_wkv", pairs, eng=act)

    cx = [sb(f"cx{j}", [P, BLK // P, DC]) for j in range(2)]
    ctx_d = ins["ctx_768"].rearrange("b (n c p) d -> (b n) p c d", p=P, c=BLK // P)
    ctx_loaded = [Count(nc, f"ctx_loaded{j}", 16) for j in range(2)]
    ctx_turned = Count(nc, "ctx_turned", 1, 2)
    ctx_turned.give(pe)

    def load_ctx(n, j):
        ctx_turned.wait(sp, n - 2)
        sp.dma_start(cx[j][:, :, :], ctx_d[bass.ds(n, 1), :, :, :].rearrange("a p c d -> (a p) c d"))\
            .then_inc(ctx_loaded[j].sem, 16)

    for j in range(2):
        load_ctx(j, j)
    t_xn = layer_norm(xn, x, [t_x])
    t_xT = features_on_partitions(xT, lambda i, kt: xn[:, i, kt * P:(kt + 1) * P], [t_xn], [])
    wq = sb("wq", [P, 2, D])
    bq = sb("bq", [1, D])
    t_wq = load("ld_wq", [(wq[:, :, :], ins["L0_xattn_Wq"].rearrange("(k p) n -> p k n", p=P)),
                          (bq[:, :], row("L0_xattn_bq"))])
    qf = sb("qf", [P, T])
    qr = sb("qr", [P, T])
    qparts = sb("qparts", [P, 2, 3, T], BF16)
    q_stack_d = nc.dram_tensor("q_stack_d", [NH, NSTK, D0, S], BF16).ap()
    k_parts_d = nc.dram_tensor("k_parts_d", [NB * D, 3, S2], BF16).ap()
    k1_parts_d = nc.dram_tensor("k1_parts_d", [NB * P, 3, S2], BF16).ap()

    def three_parts(parts, full, rest, after):
        DV.after(*after)
        t = DV.done(dve.tensor_copy(parts(0), full))
        DV.after(t)
        t = DV.done(dve.tensor_tensor(rest, full, parts(0), ALU.subtract))
        DV.after(t)
        t = DV.done(dve.tensor_copy(parts(1), rest))
        DV.after(t)
        return DV.done(dve.tensor_tensor(parts(2), rest, parts(1), ALU.subtract))

    ld_q = Load(nc, "st_qparts")
    PE.after(t_wq, t_xT, t_ones)
    for mt in range(2):
        for kt in range(2):
            pe.matmul(bank[:, 2 + mt, :], wq[:, kt, mt * P:(mt + 1) * P], xT[:, kt, :], start=(kt == 0), stop=False)
        t_q = PE.done(pe.matmul(bank[:, 2 + mt, :], bq[0:1, mt * P:(mt + 1) * P], ones[0:1, :], start=False, stop=True))
        DV.after(t_q)
        t = DV.done(dve.tensor_scalar(qf[:, :], bank[:, 2 + mt, :], float(D0) ** -0.5, None, ALU.mult))
        t = three_parts(lambda k: qparts[:, mt, k, :], qf[:, :], qr[:, :], [t])
        act.wait_ge(*t)
        for b in range(NB):
            h0 = b * H0 + mt * (P // D0)
            for s, (kp, qp) in enumerate(STACK):
                ld_q.add(act.dma_start(q_stack_d[h0:h0 + P // D0, s, :, :], qparts[:, mt, qp, b * S:(b + 1) * S]))

    cT1 = [sb(f"cT1_{j}", [P, BLK]) for j in range(2)]
    cT2 = [sb(f"cT2_{j}", [DC - P + 1, BLK]) for j in range(2)]
    kf = sb("kf", [P, 3, BLK])
    kr = sb("kr", [P, 3, BLK])
    kparts = [sb(f"kparts{j}", [P, 3, 3, BLK], BF16) for j in range(2)]
    for j in range(2):
        t_c = DV.done(dve.memset(cT2[j][DC - P:DC - P + 1, :], 1.0))
    t_v1 = PO.done(pool.memset(V[:, :, :, D0:VW], 1.0))

    cT_copied = Count(nc, "cT_copied", 2, 1)
    k_made = Count(nc, "k_made", 3)
    v_made = Count(nc, "v_made", 2, 2)
    kf_copied = Count(nc, "kf_copied", 3, 1)
    v_copied = Count(nc, "v_copied", 2, 1)
    kh_done = Count(nc, "kh_done", 6, 1)
    kl_done = Count(nc, "kl_done", 6, 1)
    kparts_out = [Count(nc, f"kparts_out{j}", 48, 1) for j in range(2)]
    for c, e in ((cT_copied, act), (v_made, pe), (kf_copied, act), (v_copied, act),
                 (kh_done, dve), (kl_done, pool), (kparts_out[0], sp), (kparts_out[1], sp)):
        c.give(e)

    PE.after(t_wkv, t_c, t_q, t_xT)
    AC.after(t_v1, t_xT)
    PO.after(t_ones)
    DV.after(t_q)

    def turn(batch, bpair, j):
        pair, n = bpair + batch * (NBB // 2), bpair * 2 + j + batch * NBB
        ctx_loaded[j].wait(pe, pair)
        cT_copied.wait(pe, n - 1)
        for c in range(BLK // P):
            pe.transpose(bank[:, 0, c * P:(c + 1) * P], cx[j][:, c, 0:P], ident[:, :])
            ins_ = pe.transpose(bank[0:DC - P, 1, c * P:(c + 1) * P], cx[j][:, c, P:DC], ident[:, :])
        ctx_turned.inc(ins_)
        ctx_turned.wait(act, n)
        v_made.wait(act, n - 2)
        cT_copied.inc(act.copy(cT1[j][:, :], bank[:, 0, :]))
        cT_copied.inc(act.copy(cT2[j][0:DC - P, :], bank[0:DC - P, 1, :]))

    def project(batch, bpair, j):
        blk = bpair * 2 + j
        pair, n = bpair + batch * (NBB // 2), blk + batch * NBB
        cT_copied.wait(pe, n)
        for m, at in enumerate((0, P, 2 * D)):
            kf_copied.wait(pe, n - 1, m + 1)
            pe.matmul(bank[:, 2 + m, :], wkv1[:, at:at + P], cT1[j][:, :], start=True, stop=False)
            k_made.inc(pe.matmul(bank[:, 2 + m, :], wkv2[:, at:at + P], cT2[j][:, :], start=False, stop=True))
        for c in range(BLK // P):
            if c % 2 == 0:
                v_copied.wait(pe, n - 1, c // 2 + 1)
            o = bank[:, 5 + c // 2, (c % 2) * D:(c % 2 + 1) * D]
            pe.matmul(o, cT1[j][:, c * P:(c + 1) * P], wkv1[:, D:2 * D], start=True, stop=False)
            ins_ = pe.matmul(o, cT2[j][:, c * P:(c + 1) * P], wkv2[:, D:2 * D], start=False, stop=True)
            if c % 2 == 1:
                v_made.inc(ins_)
        for m in range(3):
            k_made.wait(act, n, m + 1)
            kl_done.wait(act, n - 1, 2 * m + 1)
            kh_done.wait(act, n - 1, 2 * m + 2)
            kf_copied.inc(act.copy(kf[:, m, :], bank[:, 2 + m, :]))
            kf_copied.wait(dve, n, m + 1)
            kparts_out[j].wait(dve, pair - 1)
            kh_done.inc(dve.tensor_scalar(kparts[j][:, m, 0, :], kf[:, m, :], 1.0, None, ALU.mult))
            kh_done.wait(dve, n, 2 * m + 1)
            kl_done.wait(dve, n - 1, 2 * m + 2)
            kh_done.inc(dve.tensor_tensor(kr[:, m, :], kf[:, m, :], kparts[j][:, m, 0, :], ALU.subtract))
            kh_done.wait(pool, n, 2 * m + 2)
            kparts_out[j].wait(pool, pair - 1)
            kl_done.inc(pool.tensor_tensor(kparts[j][:, m, 1, :], kr[:, m, :], zeros[:, :], ALU.add))
            kl_done.wait(pool, n, 2 * m + 1)
            kl_done.inc(pool.tensor_tensor(kparts[j][:, m, 2, :], kr[:, m, :], kparts[j][:, m, 1, :], ALU.subtract))
            kl_done.wait(sp, n, 2 * m + 2)
            dst, row0 = (k_parts_d, batch * D + m * P) if m < 2 else (k1_parts_d, batch * P)
            sp.dma_start(dst[row0:row0 + P, :, bass.ds(blk * BLK, BLK)],
                         kparts[j][:, m, :, :]).then_inc(kparts_out[j].sem, 16)
        for h in range(2):
            v_made.wait(act, n, h + 1)
            v_copied.inc(act.copy(V[:, bass.ds(n * 4 + 2 * h, 2), :, 0:D0],
                                  bank[:, 5 + h, :].rearrange("p (c h d) -> p c h d", c=2, h=H0)))

    for batch in range(NB):
        n0 = batch * NBB
        turn(batch, 0, 0)
        with nc.Fori(0, NBB // 2 - 1, 1) as bpair:
            load_ctx(bpair * 2 + 2 + n0, 0)
            turn(batch, bpair, 1)
            project(batch, bpair, 0)
            load_ctx(bpair * 2 + 3 + n0, 1)
            turn(batch, bpair + 1, 0)
            project(batch, bpair, 1)
        if batch < NB - 1:
            load_ctx(n0 + NBB, 0)
        turn(batch, NBB // 2 - 1, 1)
        project(batch, NBB // 2 - 1, 0)
        if batch < NB - 1:
            load_ctx(n0 + NBB + 1, 1)
        project(batch, NBB // 2 - 1, 1)
    for j in range(2):
        kparts_out[j].wait(sp, NBLK // 2 - 1)
    sp.wait_ge(*ld_q.token())
    phase_ends()
    PE.after(t_z, t_ident)
    for k, src in enumerate((a[0][:, :], a[1][:, :], AR, AI)):
        t = PE.done(pe.transpose(bank[:, 7, k * P:(k + 1) * P], src, ident[:, :]))
    AC.after(t)
    zz = [[sb(f"zz{k}{c}", [P, P]) for c in "ri"] for k in range(2)]
    for dst, k in ((zz[0][0][:, :], 0), (zz[0][1][:, :], 1), (Bp[0][:, :, 1, :], 0), (Bp[1][:, :, 1, :], 1),
                   (Ap[0][:, :, 0, :], 2), (Ap[1][:, :, 0, :], 3)):
        q_ = bank[:, 7, k * P:(k + 1) * P]
        t = AC.done(act.copy(dst, q_ if dst.shape[1] == P else q_.rearrange("p (q g) -> p q g", q=4)))
    PE.after(t)
    s1, s2 = sb("s1", [P, 4, LA // 2, 32]), sb("s2", [P, 4, LA // 2, 32])
    PO.after(t)
    PO.done(pool.memset(Bp[0][:, :, 0, :], 1.0))
    PO.done(pool.memset(Bp[1][:, :, 0, :], 0.0))
    cur = 0

    def square(cur):
        z, y = zz[cur], zz[1 - cur]
        cmul(y[0][:, :], y[1][:, :], z[0][:, :], z[1][:, :], z[0][:, :], z[1][:, :],
             *(q[:, 0, 0:4, :].rearrange("p a g -> p (a g)") for q in (s1, s2)))
        return 1 - cur

    def extend(pw, m, cur):
        zb = [q[:, :].rearrange("p (q a g) -> p q a g", q=4, a=1).to_broadcast([P, 4, m, 32]) for q in zz[cur]]
        return cmul(pw[0][:, :, m:2 * m, :], pw[1][:, :, m:2 * m, :], pw[0][:, :, 0:m, :], pw[1][:, :, 0:m, :],
                    zb[0], zb[1], s1[:, :, 0:m, :], s2[:, :, 0:m, :])

    for m in (2, 4):
        cur = square(cur)
        extend(Bp, m, cur)
    for m in (1, 2, 4, 8, 16):
        cur = square(cur)
        extend(Ap, m, cur)
    t_pow = ts(Bp[1][:, :, :, :], Bp[1][:, :, :, :], -1.0, 0.0, ALU.mult, ALU.add, line=PO)

    NS = NSTK * D0
    HK = S2 // 2
    ks = [sb(f"ks{i}", [NS + 3, S2], BF16) for i in range(4)]
    qs = [sb(f"qs{j}", [NS + 3, S], BF16) for j in range(4)]
    vs = [sb(f"vs{j}", [P, NCH, 32]) for j in range(2)]
    pT = [sb(f"pT{j}", [P, 4 * S]) for j in range(2)]
    rmax = [sb(f"rmax{j}", [P, 2, 8]) for j in range(2)]
    nmax = sb("nmax", [P, 2])
    nres = sb("nres", [P, 2])
    mparts = sb("mparts", [P, 2, 3], BF16)
    ao = sb("ao", [P, NH, 2, D0])
    oT = sb("oT", [P, S])
    fold = sb("fold", [P, VW])
    rden = sb("rden", [P, 2])
    for i in range(4):
        t = DV.done(dve.memset(ks[i][NS:NS + 3, :], 1.0))
    for j in range(2):
        t_vz = DV.done(dve.memset(vs[j][:, :, :], 0.0))
    PO.after(t_vz)
    t_f = DV.done(dve.tensor_copy(fold[0:32, :], ident[0:32, 0:VW]))
    for q in range(1, 4):
        t_f = DV.done(dve.tensor_copy(fold[32 * q:32 * q + 32, :], ident[0:32, 0:VW]))
    PE.after(t_f)

    key_in = [Count(nc, f"key_in{i}", 16 * NSTK) for i in range(4)]
    query_in = [Count(nc, f"query_in{j}", 16) for j in range(4)]
    max_made = Count(nc, "max_made", 16)
    max_read = Count(nc, "max_read", 16, 1)
    rows_made = Count(nc, "rows_made", 1)
    rows_read = Count(nc, "rows_read", 1, 1)
    max_step = Count(nc, "max_step", 6)
    st_made = Count(nc, "st_made", 8, 4)
    p_made = Count(nc, "p_made", 8, 1)
    pv_made = Count(nc, "pv_made", 8, 4)
    vs_copied = Count(nc, "vs_copied", 1)
    oT_copied = Count(nc, "oT_copied", 1, 1)
    o_made = Count(nc, "o_made", 1, 1)
    o_done = Count(nc, "o_done", 2, 2)
    for c, e in ((max_read, dve), (rows_read, act), (st_made, pe), (p_made, act), (pv_made, pe), (oT_copied, act), (o_made, pe), (o_done, dve)):
        c.give(e)

    def load_queries(four, i):
        n = four * 4 + i
        st_made.wait(sp, n - 4)
        sp.dma_start(qs[i][0:NS, :], q_stack_d[bass.ds(n, 1), :, :, :].rearrange("a s d q -> (a s d) q"))\
            .then_inc(query_in[i].sem, 16)

    def load_keys(four, i):
        n = four * 4 + i
        st_made.wait(sp, n - 4)
        kd = k_parts_d[bass.ds(n * D0, D0), :, :]
        for s, (kp, qp) in enumerate(STACK):
            sp.dma_start(ks[i][s * D0:(s + 1) * D0, :], kd[:, kp, :]).then_inc(key_in[i].sem, 16)

    def values(four, i):
        n, j = four * 4 + i, i % 2
        pv_made.wait(pool, n - 2)
        hold(pool)
        vs_copied.inc(pool.tensor_tensor(vs[j][:, :, 0:VW], V[:, bass.ds((n // H0) * NCH, NCH), bass.ds(n % H0, 1), :]
                                         .rearrange("p c a d -> p c (a d)"),
                                         zeros[:, 0:VW].rearrange("p (a d) -> p a d", a=1).to_broadcast([P, NCH, VW]), ALU.add))

    def max_chunk(four, i, u):
        n, qt, c, b = four * 4 + i, u // 8, u % 8, u % 2
        if u == 0:
            query_in[i].wait(pe, four)
            key_in[i].wait(pe, four)
        if u < 2:
            max_read.wait(pe, n - 1, u + 15)
        else:
            max_read.wait(pe, n, u - 1)
        max_made.inc(pe.matmul(bank[:, b, :], qs[i][0:NS, qt * P:(qt + 1) * P], ks[i][0:NS, c * 512:(c + 1) * 512],
                               start=True, stop=True))
        max_made.wait(dve, n, u + 1)
        max_read.inc(dve.tensor_reduce(rmax[i % 2][:, qt, c:c + 1], bank[:, b, :], AX.X, ALU.max))

    def max_rows_step(four, i, k):
        n, part = four * 4 + i, (k - 1) // 2
        if k == 0:
            max_read.wait(dve, n, 16)
            max_step.inc(dve.tensor_reduce(nmax[:, :], rmax[i % 2][:, :, :], AX.X, ALU.max, negate=True))
            return
        max_step.wait(dve, n, k)
        src = nmax if part == 0 else nres
        if k % 2:
            max_step.inc(dve.tensor_copy(mparts[:, :, part], src[:, :]))
        else:
            max_step.inc(dve.tensor_tensor(nres[:, :], src[:, :], mparts[:, :, part], ALU.subtract))

    def max_rows(four, i):
        n = four * 4 + i
        max_step.wait(pe, n)
        o_done.wait(pe, n - 2)
        for qt in range(2):
            ins_ = pe.matmul(bank[NS:NS + 3, 7, qt * P:(qt + 1) * P], mparts[:, qt, :], identb[:, :],
                             start=True, stop=True)
        rows_made.inc(ins_)
        rows_made.wait(act, n)
        rows_read.inc(act.copy(qs[i][NS:NS + 3, :], bank[NS:NS + 3, 7, 0:S]))

    def scores(four, i, g):
        n, j, b0 = four * 4 + i, i % 2, 2 + 2 * (g % 2)
        p_made.wait(pe, n if g >= 2 else n - 1, g - 1 if g >= 2 else 7 + g)
        if g == 0:
            rows_read.wait(pe, n)
        for c in range(4):
            k0 = (4 * g + c) * P
            ins_ = pe.matmul(bank[:, b0 + c // 2, (c % 2) * S:(c % 2 + 1) * S], ks[i][:, k0:k0 + P], qs[i][:, :],
                             start=True, stop=True)
        st_made.inc(ins_)
        st_made.wait(act, n, g + 1)
        pv_made.wait(act, n if g >= 2 else n - 1, g - 1 if g >= 2 else 7 + g)
        p_made.inc(act.activation(pT[g % 2][:, :], bank[:, b0:b0 + 2, :].rearrange("p a k -> p (a k)"), ACT.Exp))

    def weigh(four, i, g):
        n, j = four * 4 + i, i % 2
        p_made.wait(pe, n, g + 1)
        if g == 0:
            vs_copied.wait(pe, n)
            oT_copied.wait(pe, n - 1)
        for c in range(4):
            ins_ = pe.matmul(bank[32 * c:32 * c + 32, 6, 0:S], vs[j][:, 4 * g + c, :], pT[g % 2][:, c * S:(c + 1) * S],
                             start=(g == 0), stop=(g == 7))
        pv_made.inc(ins_)

    def sum_out(four, i):
        n = four * 4 + i
        pv_made.wait(act, n)
        o_made.wait(act, n - 1)
        oT_copied.inc(act.copy(oT[:, :], bank[:, 6, 0:S]))

    def add_quarters(four, i):
        n = four * 4 + i
        oT_copied.wait(pe, n)
        o_done.wait(pe, n - 1)
        for qt in range(2):
            ins_ = pe.matmul(bank[:, 7, qt * 32:qt * 32 + VW], oT[:, qt * P:(qt + 1) * P], fold[:, :], start=True, stop=True)
        o_made.inc(ins_)

    def divide(four, i):
        n = four * 4 + i
        o_made.wait(dve, n)
        o_done.inc(dve.reciprocal(rden[:, :], bank[:, 7, 0:64].rearrange("p (a k) -> p a k", a=2)[:, :, D0]))
        o_done.wait(dve, n, 1)
        for qt in range(2):
            ins_ = dve.tensor_scalar(ao[:, bass.ds(n, 1), qt, :].rearrange("p a d -> p (a d)"),
                                     bank[:, 7, qt * 32:qt * 32 + D0], rden[:, qt:qt + 1], None, ALU.mult)
        o_done.inc(ins_)

    LEAD = 2

    def attend(four, i, before, nxt, after_nxt):
        for g in range(8):
            slots = []
            for u in (2 * g, 2 * g + 1):
                m = nxt if u + 2 * LEAD < 16 else after_nxt
                slots.append((*m, (u + 2 * LEAD) % 16) if m else None)
            if g == 8 - LEAD and nxt:
                max_rows_step(*nxt, 0)
            if slots[0]:
                max_chunk(*slots[0])
            if g == 7 and nxt:
                max_rows(*nxt)
            if g == 8 - LEAD and nxt:
                max_rows_step(*nxt, 1)
                max_rows_step(*nxt, 2)
            scores(four, i, g)
            if g == 1 and before:
                add_quarters(*before)
            if slots[1]:
                max_chunk(*slots[1])
            if g == 8 - LEAD and nxt:
                max_rows_step(*nxt, 3)
                max_rows_step(*nxt, 4)
                max_rows_step(*nxt, 5)
            if g == 0 and before:
                weigh(*before, 7)
                sum_out(*before)
            if g == 1 and before:
                divide(*before)
            if g == 1 and nxt:
                values(*nxt)
            if g:
                weigh(four, i, g - 1)

    for i in range(4):
        load_queries(0, i)
        load_keys(0, i)
        if i < 1:
            values(0, i)
    for u in range(16):
        max_chunk(0, 0, u)
    for k in range(6):
        max_rows_step(0, 0, k)
    max_rows(0, 0)
    for u in range(2 * LEAD):
        max_chunk(0, 1, u)

    def place(four, i):
        return (four + i // 4, i % 4)

    def steps_of(four, first=False):
        for i in range(4):
            last = four == NH // 4 - 1 if isinstance(four, int) else False
            attend(four, i, place(four, i - 1) if not (first and i == 0) else None,
                   place(four, i + 1) if not (last and i > 2) else None,
                   place(four, i + 2) if not (last and i > 1) else None)
            if not last and i:
                load_queries(four + 1, i - 1)
                load_keys(four + 1, i - 1)

    steps_of(0, first=True)
    with nc.Fori(1, NH // 4 - 1, 1) as four:
        load_queries(four, 3)
        load_keys(four, 3)
        steps_of(four)
    four = NH // 4 - 1
    load_queries(four, 3)
    load_keys(four, 3)
    steps_of(four)
    weigh(four, 3, 7)
    sum_out(four, 3)
    add_quarters(four, 3)
    divide(four, 3)
    o_done.wait(pe, NH - 1)
    o_done.wait(dve, NH - 1)

    wo = sb("wo", [P, 2, D])
    bo = sb("bo", [1, D])
    t_wo = load("ld_wo", [(wo[:, :, :], ins["L0_xattn_Wo"].rearrange("(k p) n -> p k n", p=P)), (bo[:, :], row("L0_xattn_bo"))])
    aoc = pT[0][:, :].rearrange("p (t d) -> p t d", t=NT)
    for i in range(NT):
        b, qt = i // 2, i % 2
        t = DV.done(dve.tensor_copy(aoc[:, i, :].rearrange("p (h d) -> p h d", h=H0), ao[:, b * H0:(b + 1) * H0, qt, :]))
    t_aoT = features_on_partitions(xT, lambda i, kt: aoc[:, i, kt * P:(kt + 1) * P], [t], [])

    def project_tokens(srcT, w, bias, after, first_bank=2, width=D):
        PE.after(*after)
        toks = []
        for i in range(NT):
            for kt in range(2):
                t = pe.matmul(bank[:, first_bank + i, 0:width], srcT[:, kt, i * P:(i + 1) * P], w[:, kt, :],
                              start=(kt == 0), stop=(kt == 1 and bias is None))
            if bias is not None:
                t = pe.matmul(bank[:, first_bank + i, 0:width], ones[0:1, 0:P], bias, start=False, stop=True)
            toks.append(PE.done(t))
        return toks

    def add_to_x(toks, first_bank=2):
        for i in range(NT):
            DV.after(toks[i])
            t = DV.done(dve.tensor_tensor(x[:, i, :], bank[:, first_bank + i, 0:D], x[:, i, :], ALU.add))
        return t

    t_x1 = add_to_x(project_tokens(xT, wo, bo[0:1, :], [t_wo, t_aoT]))
    phase_ends()
    phase_ends()

    HA, DA = 8, 32
    phase_begins()
    t_xn = layer_norm(xn, x, [t_x1])
    t_xT = features_on_partitions(xT, lambda i, kt: xn[:, i, kt * P:(kt + 1) * P], [t_xn], [])
    lowV = {c: sb(f"lowV{c}", [P, 2, P]) for c in "qkv"}
    lowU = {c: sb(f"lowU{c}", [P, 2, P]) for c in "qkv"}
    lowb = sb("lowb", [P, 3, 2])
    lowbv = sb("lowbv", [1, D])
    raw = sb("raw", [P, 2, 2, P])
    pairs = [(lowbv[:, :], ins["L0_attn_bv"].rearrange("h d -> (h d)").rearrange("(a n) -> a n", a=1))]
    for k, c in enumerate("qkv"):
        t = PO.done(pool.memset(lowV[c][:, :, :], 0.0))
        t = PO.done(pool.memset(lowU[c][:, :, :], 0.0))
    sp.wait_ge(*t)
    ld = Load(nc, "ld_lowrank")
    with nc.allow_non_contiguous_dma(reason="small transposed weights"):
        for dst, src in pairs:
            ld.add(sp.dma_start(dst, src))
        for k, c in enumerate("qkv"):
            for h in range(HA):
                r = slice((h % 4) * DA, (h % 4 + 1) * DA)
                ld.add(sp.dma_start(lowV[c][r, h // 4, r], ins["L0_attn_V" + c][h, :, :].rearrange("r d -> d r")))
                ld.add(sp.dma_start(lowU[c][r, h // 4, r], ins["L0_attn_U" + c][h, :, :].rearrange("d r -> r d")))
            for m in range(2):
                ld.add(sp.dma_start(lowb[:, k, m:m + 1], ins["L0_attn_b" + c][4 * m:4 * m + 4, :].rearrange("h (d a) -> (h d) a", a=1)))
    t_low = ld.token()
    lowT = sb("lowT", [P, 2, T])
    qk = {c: sb(f"low_{c}", [P, 2, T]) for c in "qk"}
    vA = sb("vA", [P, NT, HA, DA + 1])
    t_vo = PO.done(pool.memset(vA[:, :, :, DA:DA + 1], 1.0))
    free = [t_xT, t_x1]
    for k, c in enumerate("qkv"):
        for m in range(2):
            PE.after(t_low, t_xT, *free)
            t = PE.done(pe.matmul(bank[:, 2 + m, :], lowV[c][:, m, :], xT[:, m, :], start=True, stop=True))
            AC.after(t, *free)
            t_l = AC.done(act.copy(lowT[:, m, :], bank[:, 2 + m, :]))
            PE.after(t_l)
            if c != "v":
                t = PE.done(pe.matmul(bank[:, 4 + m, :], lowU[c][:, m, :], lowT[:, m, :], start=True, stop=True))
                DV.after(t)
                t = DV.done(dve.tensor_scalar(qk[c][:, m, :], bank[:, 4 + m, :], lowb[:, k, m:m + 1],
                                              float(DA) ** -0.5 if c == "q" else 1.0, ALU.add, ALU.mult))
                free = [t]
        if c == "v":
            for i in range(NT):
                b, h = 6 + i // 2, (i % 2) * D
                for m in range(2):
                    o = bank[:, b, h + m * P:h + (m + 1) * P]
                    pe.matmul(o, lowT[:, m, i * P:(i + 1) * P], lowU[c][:, m, :], start=True, stop=False)
                    t = PE.done(pe.matmul(o, ones[0:1, 0:P], lowbv[:, m * P:(m + 1) * P], start=False, stop=True))
            AC.after(t, t_vo)
            for i in range(NT):
                b, h = 6 + i // 2, (i % 2) * D
                t_v = AC.done(act.copy(vA[:, i, :, 0:DA], bank[:, b, h:h + D].rearrange("p (h d) -> p h d", h=HA)))
    sA = sb("sA", [P, HA, S])
    sAT = sb("sAT", [P, HA, 2, P])
    mA = sb("mA", [P, HA])
    oA = sb("oA", [P, NT, HA, DA])
    rA = sb("rA", [P, HA])
    t_done = t_v
    for i in range(NT):
        b = i // 2
        PE.after(t_done, free[0], t_v)
        for h in range(HA):
            r = slice((h % 4) * DA, (h % 4 + 1) * DA)
            t = pe.matmul(bank[:, h % 4, (h // 4) * S:(h // 4 + 1) * S], qk["q"][r, h // 4, i * P:(i + 1) * P],
                          qk["k"][r, h // 4, b * S:(b + 1) * S], start=True, stop=True)
        t = PE.done(t)
        DV.after(t)
        t = DV.done(dve.tensor_reduce(mA[:, :], bank[:, 0:4, :].rearrange("p c (a k) -> p a c k", a=2), AX.X, ALU.max, negate=True))
        AC.after(t)
        for h in range(HA):
            t = AC.done(act.activation(sA[:, h, :], bank[:, h % 4, (h // 4) * S:(h // 4 + 1) * S], ACT.Exp, bias=mA[:, h:h + 1]))
        PE.after(t)
        for h in range(HA):
            for k in range(2):
                t = pe.transpose(bank[:, h // 2, (h % 2) * S + k * P:(h % 2) * S + (k + 1) * P], sA[:, h, k * P:(k + 1) * P], ident[:, :])
        t = PE.done(t)
        DV.after(t)
        t = DV.done(dve.tensor_copy(sAT[:, :, :, :].rearrange("p h k q -> p (h k q)"), bank[:, 0:4, :].rearrange("p a n -> p (a n)")))
        PE.after(t)
        for h in range(HA):
            for k in range(2):
                t = pe.matmul(bank[:, 4, h * 64:h * 64 + DA + 1], sAT[:, h, k, :], vA[:, b * 2 + k, h, :], start=(k == 0), stop=(k == 1))
        t = PE.done(t)
        o = bank[:, 4, :].rearrange("p (h d) -> p h d", h=HA)
        DV.after(t)
        t = DV.done(dve.reciprocal(rA[:, :], o[:, :, DA]))
        DV.after(t)
        for h in range(HA):
            t_done = DV.done(dve.tensor_scalar(oA[:, i, h, :], o[:, h, 0:DA], rA[:, h:h + 1], None, ALU.mult))
        DV.after(t_done)
        t_x2 = DV.done(dve.tensor_tensor(x[:, i, :], x[:, i, :], oA[:, i, :, :].rearrange("p h d -> p (h d)"), ALU.add))
    phase_ends()

    NE, FI, TOP = 16, 128, 4
    phase_begins()
    t_xn = layer_norm(xn, x, [t_x2])
    t_xT = features_on_partitions(xT, lambda i, kt: xn[:, i, kt * P:(kt + 1) * P], [t_xn], [])
    gwr = sb("gwr", [NE, D])
    gwT = sb("gwT", [P, 2, NE])
    t_g = load("ld_gate", [(gwr[:, :], ins["L0_ffn_gate_w"])])
    PE.after(t_g, t_xT)
    for kt in range(2):
        t = PE.done(pe.transpose(bank[:, 2, kt * NE:(kt + 1) * NE], gwr[:, kt * P:(kt + 1) * P], ident[0:NE, 0:NE]))
    DV.after(t)
    t = DV.done(dve.tensor_copy(gwT[:, :, :].rearrange("p a b -> p (a b)"), bank[:, 2, 0:2 * NE]))
    PE.after(t)
    for i in range(NT):
        for kt in range(2):
            t = pe.matmul(bank[:, 3, i * NE:(i + 1) * NE], xT[:, kt, i * P:(i + 1) * P], gwT[:, kt, :], start=(kt == 0), stop=(kt == 1))
    t = PE.done(t)
    PAD = 4
    lg = sb("lg", [P, NT, NE])
    best = sb("best", [P, NT, 8])
    prob = sb("prob", [P, NT, NE + PAD])
    rest = sb("rest", [P, NT, NE + PAD])
    score = sb("score", [P, NT, NE])
    nm = sb("nm", [P, NT])
    den = sb("den", [P, NT])
    DV.after(t)
    t = DV.done(dve.tensor_copy(lg[:, :, :].rearrange("p a b -> p (a b)"), bank[:, 3, 0:NT * NE]))
    DV.after(t)
    t = DV.done(dve.tensor_reduce(nm[:, :], lg[:, :, :], AX.X, ALU.max, negate=True))
    AC.after(t)
    for i in range(NT):
        t = AC.done(act.activation(prob[:, i, 0:NE], lg[:, i, :], ACT.Exp, bias=nm[:, i:i + 1], accum_out=den[:, i:i + 1]))
    DV.after(t)
    for k in range(PAD):
        t = DV.done(dve.memset(prob[:, :, NE + k:NE + k + 1], -1.0 - k))
    t = DV.done(dve.reciprocal(den[:, :], den[:, :]))
    DV.after(t)
    for i in range(NT):
        t = DV.done(dve.tensor_scalar(prob[:, i, 0:NE], prob[:, i, 0:NE], den[:, i:i + 1], None, ALU.mult))
    DV.after(t)
    for i in range(NT):
        t = DV.done(dve.max(best[:, i, :], prob[:, i, :]))
    DV.after(t)
    for k in range(PAD):
        t = DV.done(dve.memset(best[:, :, TOP + k:TOP + k + 1], -1.0 - k))
    DV.after(t)
    for i in range(NT):
        t = DV.done(dve.match_replace(rest[:, i, :], best[:, i, :], prob[:, i, :], 0.0))
    t = DV.done(dve.tensor_reduce(den[:, :], best[:, :, 0:TOP], AX.X, ALU.add))
    DV.after(t)
    t = DV.done(dve.reciprocal(den[:, :], den[:, :]))
    t = DV.done(dve.tensor_tensor(score[:, :, :], prob[:, :, 0:NE], rest[:, :, 0:NE], ALU.subtract))
    DV.after(t)
    for i in range(NT):
        t_score = DV.done(dve.tensor_scalar(score[:, i, :], score[:, i, :], den[:, i:i + 1], None, ALU.mult))

    w13 = [sb(f"w13_{j}", [P, 2, 2, FI]) for j in range(2)]
    w2e = [sb(f"w2e_{j}", [P, D]) for j in range(2)]
    gate = [sb(f"gate{j}", [P, T]) for j in range(2)]
    hid = [sb(f"hid{j}", [P, T]) for j in range(2)]
    sce = [sb(f"sce{j}", [P, NT]) for j in range(2)]
    w_in = [Count(nc, f"w_in{j}", 48) for j in range(2)]
    gu_made = Count(nc, "gu_made", 1)
    gate_done = Count(nc, "gate_done", 1)
    hid_done = Count(nc, "hid_done", 2, 2)
    y_made = Count(nc, "y_made", 1, 2)
    y_added = Count(nc, "y_added", NT, 2)
    for c, e in ((hid_done, dve), (y_made, pe), (y_added, dve)):
        c.give(e)
    PE.after(t_xT, t_score)
    DV.after(t_score)
    w1_d, w3_d, w2_d = ins["L0_ffn_w1"], ins["L0_ffn_w3"], ins["L0_ffn_w2"]

    def load_expert(pair, j):
        e = pair * 2 + j
        y_made.wait(sp, e - 2)
        for k, w in enumerate((w1_d, w3_d)):
            sp.dma_start(w13[j][:, k, :, :], w[bass.ds(e, 1), :, :].rearrange("a (k p) i -> p (a k) i", p=P)).then_inc(w_in[j].sem, 16)
        sp.dma_start(w2e[j][:, :], w2_d[bass.ds(e, 1), :, :].rearrange("a i h -> (a i) h")).then_inc(w_in[j].sem, 16)

    def expert_up(pair, j):
        e = pair * 2 + j
        w_in[j].wait(pe, pair)
        hid_done.wait(pe, e - 2, 1)
        for k in range(2):
            for kt in range(2):
                ins_ = pe.matmul(bank[:, 2 * j + k, :], w13[j][:, k, kt, :], xT[:, kt, :], start=(kt == 0), stop=(kt == 1))
        gu_made.inc(ins_)
        gu_made.wait(act, e)
        gate_done.inc(act.activation(gate[j][:, :], bank[:, 2 * j, :], ACT.Silu))
        gate_done.wait(dve, e)
        y_made.wait(dve, e - 2)
        hid_done.inc(dve.tensor_tensor(hid[j][:, :], bank[:, 2 * j + 1, :], gate[j][:, :], ALU.mult))
        y_added.wait(dve, e - 2)
        hid_done.inc(dve.tensor_scalar(sce[j][:, :], score[:, :, bass.ds(e, 1)].rearrange("p t a -> p (t a)"), 1.0, None, ALU.mult))

    def expert_down(pair, j):
        e = pair * 2 + j
        hid_done.wait(pe, e)
        y_added.wait(pe, e - 2)
        for i in range(NT):
            ins_ = pe.matmul(bank[:, 4 + 2 * j + i // 2, (i % 2) * D:(i % 2 + 1) * D], hid[j][:, i * P:(i + 1) * P], w2e[j][:, :],
                             start=True, stop=True)
        y_made.inc(ins_)
        y_made.wait(dve, e)
        y_added.wait(dve, e - 1)
        for i in range(NT):
            y_added.inc(dve.scalar_tensor_tensor(x[:, i, :], bank[:, 4 + 2 * j + i // 2, (i % 2) * D:(i % 2 + 1) * D],
                                                 sce[j][:, i:i + 1], x[:, i, :], ALU.mult, ALU.add))

    load_expert(0, 0)
    load_expert(0, 1)
    expert_up(0, 0)
    with nc.Fori(0, NE // 2 - 1, 1) as pair:
        expert_up(pair, 1)
        expert_down(pair, 0)
        load_expert(pair + 1, 0)
        expert_up(pair + 1, 0)
        expert_down(pair, 1)
        load_expert(pair + 1, 1)
    expert_up(NE // 2 - 1, 1)
    expert_down(NE // 2 - 1, 0)
    expert_down(NE // 2 - 1, 1)
    y_added.wait(dve, NE - 1)
    y_added.wait(act, NE - 1)
    y_added.wait(pe, NE - 1)
    t_x3 = DV.done(dve.tensor_copy(nm[:, 0:1], nm[:, 0:1]))
    phase_ends()

    H1, D1, KTOP = 4, 32, 32
    DCM = DC - P
    phase_begins()
    xt = sb("xt", [P, NT, D])
    xh = sb("xh", [P, NT, D])
    c0T = [sb("c0T1", [P, T]), sb("c0T2", [DCM, T])]
    t_xt = layer_norm(xt, x, [t_x3])
    t_xT = features_on_partitions(xT, lambda i, kt: xt[:, i, kt * P:(kt + 1) * P], [t_xt], [])

    tabs = sb("tabs", [P, 4, 2, S])
    KT = sb("KT", [P, 2, D])
    Kf = sb("Kf", [P, 2, 2, D])
    phase_begins()
    t_tab = load("ld_tab", [(tabs[:, k, :, :], ins["dft"][k].rearrange("(t p) n -> p t n", p=P)) for k in range(4)])
    kst = sb("kst", [P, LB, 2, LA])
    PE.after(t_pow, t_xT)
    for t_ in range(2):
        for g in range(LA):
            hs = slice(t_ * NSTATE, (t_ + 1) * NSTATE)
            c0 = (t_ * LA + g) * 32
            for c in range(2):
                t = pe.matmul(bank[:, 4 + c0 // 512, c0 % 512:c0 % 512 + 32],
                              Ap[c][hs, :, :, g].rearrange("p q a -> p (q a)"), Bp[c][hs, :, :, g], start=(c == 0), stop=(c == 1))
    t = PE.done(t)
    AC.after(t)
    blk = bank[:, 4:8, :].rearrange("p c n -> p (c n)").rearrange("p (g q b) -> p q b g", q=4, b=LB)
    for q in range(4):
        t = AC.done(act.copy(kst[32 * q:32 * q + 32, :, :, :].rearrange("p b t g -> p b (t g)"), blk[32 * q:32 * q + 32, q, :, :]))
    K_d = nc.dram_tensor("K_d", [S, D], F32).ap()
    sp.wait_ge(*t)
    ld = Load(nc, "st_K")
    for q in range(4):
        for t_ in range(2):
            at = t_ * P + q * 32
            ld.add(sp.dma_start(K_d.rearrange("(a b) d -> a b d", b=LB)[:, :, at:at + 32], kst[32 * q:32 * q + 32, :, t_, :]))
    sp.wait_ge(*ld.token())
    t_KT = load("ld_KT", [(KT[:, :, :], K_d.rearrange("(t p) d -> p t d", p=P))])

    wq1 = sb("wq1", [P, 2, P])
    t_w = load("ld_wq1", [(wq1[:, :, :], ins["L1_xattn_Wq"].rearrange("(k p) n -> p k n", p=P))])
    q1f, q1r, q1p = sb("q1f", [P, T]), sb("q1r", [P, T]), sb("q1p", [P, 3, T], BF16)
    q1_parts_d = nc.dram_tensor("q1_parts_d", [NB * P, 3, S], BF16).ap()
    PE.after(t_w, t_xT)
    for kt in range(2):
        t = pe.matmul(bank[:, 2, :], wq1[:, kt, :], xT[:, kt, :], start=(kt == 0), stop=(kt == 1))
    t = PE.done(t)
    DV.after(t)
    t = DV.done(dve.tensor_scalar(q1f[:, :], bank[:, 2, :], 1.0 / math.sqrt(D1), None, ALU.mult))
    t = three_parts(lambda k: q1p[:, k, :], q1f[:, :], q1r[:, :], [t])
    sp.wait_ge(*t)
    ld = Load(nc, "st_q1")
    for b in range(NB):
        ld.add(sp.dma_start(q1_parts_d[b * P:(b + 1) * P, :, :], q1p[:, :, b * S:(b + 1) * S]))
    m8 = sb("m8", [NB, S2], mybir.dt.uint8)
    mrow = sb("mrow", [NB, S2], BF16)
    mask_d = nc.dram_tensor("mask_d", [NB, S2], BF16).ap()
    t_m = load("ld_mask", [(m8[:, :], ins["mask_BxS2_bf1"])])
    DV.after(t_m)
    t = DV.done(dve.tensor_scalar(mrow[:, :], m8[:, :], 1e30, -1e30, ALU.mult, ALU.add))
    sp.wait_ge(*t)
    ld.add(sp.dma_start(mask_d, mrow[:, :]))
    sp.wait_ge(*ld.token())
    PE.after(t_KT, t_tab)
    for c in range(2):
        for ft in range(2):
            for lt in range(2):
                t = pe.matmul(bank[:, 4 + c, ft * D:(ft + 1) * D], tabs[:, c, lt, ft * P:(ft + 1) * P], KT[:, lt, :],
                              start=(lt == 0), stop=(lt == 1))
        t = PE.done(t)
        AC.after(t)
        t_Kf = AC.done(act.copy(Kf[:, c, :, :].rearrange("p f d -> p (f d)"), bank[:, 4 + c, :]))
    phase_ends()

    phase_begins()
    NS1 = 3 * D1
    NM = NB * H1
    k1s = [sb(f"k1s{g}", [NS1 + 1, S2], BF16) for g in range(2)]
    q1s = [sb(f"q1s{g}", [NS1 + 1, S], BF16) for g in range(2)]
    GC = 128
    NG = S2 // GC
    Sc = [sb(f"Sc{j}", [P, S2]) for j in range(2)]
    Ex = [sb(f"Ex{j}", [P, S2]) for j in range(2)]
    amean = sb("amean", [P, 2, S2])
    cand = sb("cand", [P, NG, 8])
    cleft = sb("cleft", [P, NG * 8])
    top = [sb(f"top{j}", [P, KTOP]) for j in range(2)]
    rest8 = sb("rest8", [P, 8])
    worst = sb("worst", [P, 1])
    flag = sb("flag", [P, 1])
    flags = [sb(f"flags{j}", [1, 1], I32) for j in range(2)]
    thr = [sb(f"thr{j}", [P, 1]) for j in range(2)]
    ntop = [sb(f"ntop{j}", [P, 1]) for j in range(2)]
    etop = sb("etop", [P, KTOP])
    ssum = [sb(f"ssum{j}", [P, 1]) for j in range(2)]
    aT = [sb(f"aT{j}", [P, 4, P]) for j in range(2)]
    c0 = sb("c0", [P, NT, DC])
    for g in range(2):
        t_o = DV.done(dve.memset(q1s[g][NS1:NS1 + 1, :], 1.0 if g == 0 else 0.0))
        t_o = DV.done(dve.memset(k1s[g][NS1:NS1 + 1, :], 0.0))
    t_cov = DV.done(dve.memset(amean[:, :, :], 0.0))
    NSEL, NEX = 15, 10
    stack1_in = Count(nc, "stack1_in", 16 * 13)
    s_made = Count(nc, "s_made", 4)
    s_copied = Count(nc, "s_copied", 4, 1)
    ex_made = Count(nc, "ex_made", 1)
    sel = Count(nc, "sel", NSEL, 1)
    flag_summed = Count(nc, "flag_summed", 1)
    flag_in = Count(nc, "flag_in", 1, 1)
    exact = Count(nc, "exact", NEX)
    sum_made = Count(nc, "sum_made", 1)
    fin = Count(nc, "fin", 4, 2)
    for c, e in ((s_copied, act), (sel, dve), (flag_in, dve), (fin, dve)):
        c.give(e)
    PE.after(t_Kf, t_o)
    sp.wait_ge(*t_o)
    GROUPS = (((0, 0), (0, 1), (1, 0)), ((0, 2), (2, 0), (1, 1)))

    def stack1(b, h):
        r = b * H1 * 2 + h * 2
        if not (b == 0 and isinstance(h, int) and h == 0):
            s_made.wait(sp, r - 1)
        kd = k1_parts_d[bass.ds(h * D1 + b * P, D1), :, :]
        qd = q1_parts_d[bass.ds(h * D1 + b * P, D1), :, :]
        for g in range(2):
            for s, (kp, qp) in enumerate(GROUPS[g]):
                sp.dma_start(k1s[g][s * D1:(s + 1) * D1, :], kd[:, kp, :]).then_inc(stack1_in.sem, 16)
                sp.dma_start(q1s[g][s * D1:(s + 1) * D1, :], qd[:, qp, :]).then_inc(stack1_in.sem, 16)
        sp.dma_start(k1s[0][NS1:NS1 + 1, :], mask_d[b:b + 1, :]).then_inc(stack1_in.sem, 16)

    def tile_no(b, h, qt):
        return (h + b * H1) * 2 + qt

    def score(b, h, qt):
        r, j = tile_no(b, h, qt), qt
        if qt == 0:
            stack1_in.wait(pe, h + b * H1)
        for k in range(4):
            s_copied.wait(pe, r if k >= 2 else r - 1, k - 1 if k >= 2 else k + 3)
            b0 = 2 * (k % 2)
            for c in range(2):
                k0 = (2 * k + c) * 512
                for g in range(2):
                    ins_ = pe.matmul(bank[:, b0 + c, :], q1s[g][:, qt * P:(qt + 1) * P], k1s[g][:, k0:k0 + 512],
                                     start=(g == 0), stop=(g == 1))
            s_made.inc(ins_)
            s_made.wait(act, r, k + 1)
            fin.wait(act, r - 2, 1)
            s_copied.inc(act.copy(Sc[j][:, k * 1024:(k + 1) * 1024], bank[:, b0:b0 + 2, :].rearrange("p c n -> p (c n)")))

    def take8(n, k, dst, src, left, count, wait0):
        count.wait(dve, n, wait0)
        hold(dve)
        count.inc(dve.max(dst, src))
        count.wait(dve, n, wait0 + 1)
        hold(dve)
        count.inc(dve.match_replace(left, dst, src, -3e38))

    def select(b, h, qt):
        r, j = tile_no(b, h, qt), qt
        flat = cand[:, :, :].rearrange("p g k -> p (g k)")
        sel.wait(dve, r - 1)
        fin.wait(dve, r - 2, 3)
        for k in range(4):
            s_copied.wait(dve, r, k + 1)
            hold(dve)
            for g in range(NG // 4 * k, NG // 4 * (k + 1)):
                ins_ = dve.max(cand[:, g, :], Sc[j][:, g * GC:(g + 1) * GC])
        sel.inc(ins_)
        take8(r, 0, top[j][:, 0:8], flat, cleft[:, :], sel, 1)
        sel.inc(dve.tensor_scalar(ntop[j][:, :], top[j][:, 0:1], -1.0, None, ALU.mult))
        for k in range(1, KTOP // 8):
            take8(r, k, top[j][:, 8 * k:8 * k + 8], cleft[:, :], cleft[:, :], sel, 2 * k + 2)
        sel.inc(dve.tensor_reduce(worst[:, :], cand[:, :, 7], AX.X, ALU.max))
        sel.wait(dve, r, 11)
        hold(dve)
        sel.inc(dve.max(rest8[:, :], cleft[:, :]))
        sel.inc(dve.tensor_copy(thr[j][:, :], top[j][:, KTOP - 1:KTOP]))
        sel.wait(dve, r, 13)
        sel.inc(dve.tensor_tensor(worst[:, :], worst[:, :], rest8[:, 0:1], ALU.max))
        sel.wait(dve, r, 14)
        flag_in.wait(dve, r - 1)
        sel.inc(dve.tensor_scalar(flag[:, :], worst[:, :], thr[j][:, 0:1], None, ALU.is_ge))
        sel.wait(act, r, 4)
        fin.wait(act, r - 2)
        ex_made.inc(act.activation(Ex[j][:, :], Sc[j][:, :], ACT.Exp, bias=ntop[j][:, :]))
        sel.wait(pe, r)
        flag_in.wait(pe, r - 1)
        flag_summed.inc(pe.matmul(bank[0:1, 6, 0:1], flag[:, :], ones[:, 0:1], start=True, stop=True))

    def flag_to_sbuf(b, h, qt):
        r = tile_no(b, h, qt)
        flag_summed.wait(dve, r)
        flag_in.inc(dve.tensor_copy(flags[qt][:, :], bank[0:1, 6, 0:1]))

    flagged = dve.alloc_register("flagged")

    def finish(b, h, qt):
        r, j = tile_no(b, h, qt), qt
        flag_in.wait(dve, r)
        ex_made.wait(dve, r)
        hold(dve)
        dve.reg_load(flagged, flags[j][0:1, 0:1])
        with dve.If_ne(flagged, 0):
            for k in range(KTOP // 8):
                take8(r, k, top[j][:, 8 * k:8 * k + 8], Sc[j][:, :], Sc[j][:, :], exact, 2 * k)
            exact.wait(dve, r, 8)
            exact.inc(dve.tensor_scalar(Sc[j][:, :], Sc[j][:, :], -3e38, 2.0, ALU.is_equal, ALU.mult))
            exact.inc(dve.memset(thr[j][:, :], 1.0))
        with dve.If_eq(flagged, 0):
            dve.sem_inc(exact.sem, NEX)
        exact.wait(dve, r)
        fin.inc(dve.scalar_tensor_tensor(Ex[j][:, :], Sc[j][:, :], thr[j][:, 0:1], Ex[j][:, :], ALU.is_ge, ALU.mult))
        exact.wait(act, r)
        fin.wait(act, r - 1, 3)
        sum_made.inc(act.activation(etop[:, :], top[j][:, :], ACT.Exp, bias=ntop[j][:, :], accum_out=ssum[j][:, :]))
        sum_made.wait(dve, r)
        fin.inc(dve.tensor_scalar(ssum[j][:, :], ssum[j][:, :], float(H1), None, ALU.mult))
        fin.wait(dve, r, 2)
        fin.inc(dve.reciprocal(ssum[j][:, :], ssum[j][:, :]))
        fin.wait(dve, r, 3)
        fin.inc(dve.scalar_tensor_tensor(amean[:, qt, :], Ex[j][:, :], ssum[j][:, :], amean[:, qt, :], ALU.mult, ALU.add))

    def tile_step(b, h, qt, first=False, last=False):
        select(b, h, qt)
        if not first:
            finish(b, *((h, 0) if qt else (h - 1, 1)))
        flag_to_sbuf(b, h, qt)
        if not last:
            score(b, *((h + 1, 0) if qt else (h, 1)))

    ctxn_d = ins["ctx_768"].rearrange("b (c p) d -> b p c d", p=P)
    for b in range(NB):
        ldc = [Load(nc, f"ld_cn{b}{j}") for j in range(2)]
        HC = NCH // 2
        cn = [Sc[j][:, 0:HC * DC].rearrange("p (c d) -> p c d", c=HC) for j in range(2)]

        def load_context(j):
            fin.wait(sp, 2 * H1 * b + 2 * H1 - 2 + j, 1)
            ldc[j].add(sp.dma_start(cn[j], ctxn_d[b][:, j * HC:(j + 1) * HC, :]))

        stack1(b, 0)
        score(b, 0, 0)
        tile_step(b, 0, 0, first=True)
        stack1(b, 1)
        tile_step(b, 0, 1)
        with nc.Fori(1, H1 - 1, 1) as h:
            tile_step(b, h, 0)
            stack1(b, h + 1)
            tile_step(b, h, 1)
        tile_step(b, H1 - 1, 0)
        tile_step(b, H1 - 1, 1, last=True)
        load_context(0)
        finish(b, H1 - 1, 1)
        load_context(1)
        fin.wait(pe, 2 * H1 * (b + 1) - 1)
        fin.wait(dve, 2 * H1 * (b + 1) - 1)
        prev = [None, None]
        for qt in range(2):
            for g in range(NCH // 4):
                j = g % 2
                if prev[j]:
                    PE.after(prev[j])
                for c in range(4):
                    k0 = (4 * g + c) * P
                    t = pe.transpose(bank[:, j, c * P:(c + 1) * P], amean[:, qt, k0:k0 + P], ident[:, :])
                t = PE.done(t)
                AC.after(t)
                if g >= 2:
                    AC.after(used[j])
                elif qt or b:
                    AC.after(used[j])
                t_c = AC.done(act.copy(aT[j][:, :, :].rearrange("p c q -> p (c q)"), bank[:, j, :]))
                prev[j] = t_c
                PE.after(t_c, ldc[4 * g // HC].token())
                for c in range(4):
                    t = pe.matmul(bank[:, 2 + qt, 0:DC], aT[j][:, c, :], cn[4 * g // HC][:, (4 * g + c) % HC, :], start=(g == 0 and c == 0),
                                  stop=(g == NCH // 4 - 1 and c == 3))
                t = PE.done(t)
                used = {**(used if (g or qt or b) else {}), j: t}
            DV.after(t)
            t_c0 = DV.done(dve.tensor_copy(c0[:, b * 2 + qt, :], bank[:, 2 + qt, 0:DC]))
        DV.after(used[0], used[1])
        if b == 0:
            t_z = DV.done(dve.memset(amean[:, :, :], 0.0))
        PE.after(DV.last())
        act.wait_ge(*DV.last())
        act.wait_ge(*PE.last())
    tm8 = sb("tm8", [P, NT], mybir.dt.uint8)
    tmask = sb("tmask", [P, NT])
    with nc.allow_non_contiguous_dma(reason="512 mask bytes"):
        t_tm = load("ld_tm", [(tm8[:, :], ins["mask_BxS_bf1"].rearrange("b (t p) -> p (b t)", p=P))])
    DV.after(t_tm, t_c0)
    t = DV.done(dve.tensor_copy(tmask[:, :], tm8[:, :]))
    DV.after(t)
    for i in range(NT):
        t = DV.done(dve.tensor_scalar(c0[:, i, :], c0[:, i, :], tmask[:, i:i + 1], None, ALU.mult))
    PE.after(t)
    for k, (lo, n) in enumerate(((0, P), (P, DCM))):
        for i in range(NT):
            t = PE.done(pe.transpose(bank[0:n, 4 + k, i * P:(i + 1) * P], c0[:, i, lo:lo + n], ident[:, :]))
        AC.after(t)
        t_c0T = AC.done(act.copy(c0T[k][:, :], bank[0:n, 4 + k, :]))
    phase_ends()

    phase_begins()
    wv1, wv2 = sb("wv1", [P, D]), sb("wv2", [DCM, D])
    film = sb("film", [P, 2, 2, 2 * D])
    bfilm = sb("bfilm", [1, 2, 2 * D])
    vecs = sb("vecs", [P, 7, D])
    mgate = sb("mgate", [P, 1])
    NAMES = ("g_norm_in", "b_norm_in", "g_norm_out", "b_norm_out", "g_ffn", "b_ffn", "D_skip")
    pairs = [(wv1[:, :], ins["L1_xattn_Wv"][0:P, :]), (wv2[:, :], ins["L1_xattn_Wv"][P:DC, :]),
             (mgate[:, :], ins["L1_xattn_mod_gate"].rearrange("(a n) -> a n", a=1).to_broadcast([P, 1]))]
    pairs += [(vecs[:, k, :], row("L1_xattn_" + n).to_broadcast([P, D])) for k, n in enumerate(NAMES)]
    for k, n in enumerate(("in", "out")):
        pairs += [(film[:, k, :, :], ins["L1_xattn_W_film_" + n].rearrange("(k p) n -> p k n", p=P)),
                  (bfilm[:, k, :], row("L1_xattn_b_film_" + n))]
    HID = 4 * D
    MT = HID // P
    W1 = sb("W1", [P, 2, HID])
    W2 = sb("W2", [P, MT, D])
    b1 = sb("b1", [P, MT])
    b2 = sb("b2", [1, D])
    pairs += [(W1[:, :, :], ins["L1_xattn_W1"].rearrange("(k p) n -> p k n", p=P)),
              (W2[:, :, :], ins["L1_xattn_W2"].rearrange("(k p) n -> p k n", p=P)), (b2[:, :], row("L1_xattn_b2"))]
    with nc.allow_non_contiguous_dma(reason="1024 bias values"):
        t_w = load("ld_film", pairs + [(b1[:, :], ins["L1_xattn_b1"].rearrange("(k p) -> p k", p=P))])
    VEC = {n: vecs[:, k, :] for k, n in enumerate(NAMES)}

    def seq(*fns):
        for fn in fns:
            DV.after(DV.last())
            t = DV.done(fn())
        return t

    ctT = sb("ctT", [P, 2, T])
    mod = sb("mod", [P, 2, NT, 2 * D])
    PE.after(t_w, t_c0T)
    for m in range(2):
        pe.matmul(bank[:, m, :], wv1[:, m * P:(m + 1) * P], c0T[0][:, :], start=True, stop=False)
        t = PE.done(pe.matmul(bank[:, m, :], wv2[:, m * P:(m + 1) * P], c0T[1][:, :], start=False, stop=True))
        AC.after(t)
        t_ct = AC.done(act.copy(ctT[:, m, :], bank[:, m, :]))
    AC.after(t_w)
    for k in range(2):
        toks = []
        PE.after(t_ct)
        for i in range(NT):
            if k and i == 0:
                PE.after(t_mod)
            for kt in range(2):
                pe.matmul(bank[:, 4 + i, :], ctT[:, kt, i * P:(i + 1) * P], film[:, k, kt, :], start=(kt == 0), stop=False)
            t = PE.done(pe.matmul(bank[:, 4 + i, :], ones[0:1, 0:P], bfilm[0:1, k, :], start=False, stop=True))
            AC.after(t)
            t_mod = AC.done(act.activation(mod[:, k, i, :], bank[:, 4 + i, :], ACT.Copy, scale=mgate[:, 0:1]))

    def affine(dst, src, g, b, i):
        seq(lambda: dve.tensor_tensor(dst[:, i, :], src[:, i, :], VEC[g], ALU.mult),
            lambda: dve.tensor_tensor(dst[:, i, :], dst[:, i, :], VEC[b], ALU.add))

    def modulate(dst, k, i):
        seq(lambda: dve.scalar_tensor_tensor(dst[:, i, :], mod[:, k, i, 0:D], 1.0, dst[:, i, :], ALU.add, ALU.mult),
            lambda: dve.tensor_tensor(dst[:, i, :], dst[:, i, :], mod[:, k, i, D:2 * D], ALU.add))

    layer_norm(xh, xt, [t_xt])
    DV.after(t_mod, t_w)
    for i in range(NT):
        affine(xh, xh, "g_norm_in", "b_norm_in", i)
        modulate(xh, 0, i)
    t_xh = DV.last()
    Xf = sb("Xf", [P, 2, 2, NB, D])
    Yf = sb("Yf", [P, 2, 2, NB, D])
    tmpf = sb("tmpf", [P, NB, D])
    xhv = xh[:, :, :].rearrange("p (b t) d -> p t b d", b=NB)
    PE.after(t_xh, t_tab, t_ct)
    for c in range(2):
        for ft in range(2):
            o = bank[:, c * 2 + ft, :]
            for lt in range(2):
                t = pe.matmul(o, tabs[:, c, lt, ft * P:(ft + 1) * P], xhv[:, lt, :, :], start=(lt == 0), stop=(lt == 1))
            t = PE.done(t)
            AC.after(t)
            t_Xf = AC.done(act.copy(Xf[:, c, ft, :, :].rearrange("p b d -> p (b d)"), o))
    DV.after(t_Xf, t_Kf)
    for ft in range(2):
        kb = [Kf[:, c, ft:ft + 1, :].to_broadcast([P, NB, D]) for c in range(2)]
        Xc, Xs = (Xf[:, c, ft, :, :] for c in range(2))
        for c, (a0, a1, op) in enumerate(((kb[0], kb[1], ALU.subtract), (kb[1], kb[0], ALU.add))):
            seq(lambda: dve.tensor_tensor(Yf[:, c, ft, :, :], Xc, a0, ALU.mult),
                lambda: dve.tensor_tensor(tmpf[:, :, :], Xs, a1, ALU.mult),
                lambda: dve.tensor_tensor(Yf[:, c, ft, :, :], Yf[:, c, ft, :, :], tmpf[:, :, :], op))
    PE.after(DV.last())
    for nt in range(2):
        for n_, (c, ft) in enumerate(((0, 0), (0, 1), (1, 0), (1, 1))):
            t = pe.matmul(bank[:, nt, :], tabs[:, 2 + c, ft, nt * P:(nt + 1) * P], Yf[:, c, ft, :, :].rearrange("p b d -> p (b d)"),
                          start=(n_ == 0), stop=(n_ == 3))
        t = PE.done(t)
    DV.after(t)
    xt2 = sb("xt2", [P, NT, D])
    for i in range(NT):
        b, nt = i // 2, i % 2
        seq(lambda: dve.tensor_tensor(xh[:, i, :], xh[:, i, :], VEC["D_skip"], ALU.mult),
            lambda: dve.tensor_tensor(xh[:, i, :], bank[:, nt, b * D:(b + 1) * D], xh[:, i, :], ALU.add))
        modulate(xh, 1, i)
        seq(lambda: dve.tensor_tensor(xt2[:, i, :], xh[:, i, :], xt[:, i, :], ALU.add))
    layer_norm(xh, xt2, [DV.last()])
    for i in range(NT):
        affine(xh, xh, "g_ffn", "b_ffn", i)
    t_hT = features_on_partitions(xT, lambda i, kt: xh[:, i, kt * P:(kt + 1) * P], [DV.last()], [], banks=(2, 3))
    ffh = sb("ffh", [P, MT, T])
    PE.after(t_hT)
    AC.after(t_w)
    used = [None] * 2
    for m in range(MT):
        j = m % 2
        if used[j]:
            PE.after(used[j])
        for kt in range(2):
            t = pe.matmul(bank[:, 2 + j, :], W1[:, kt, m * P:(m + 1) * P], xT[:, kt, :], start=(kt == 0), stop=(kt == 1))
        t = PE.done(t)
        AC.after(t)
        used[j] = t_h = AC.done(act.activation(ffh[:, m, :], bank[:, 2 + j, :], ACT.Gelu, bias=b1[:, m:m + 1]))
    PE.after(t_h)
    for i in range(NT):
        for m in range(MT):
            pe.matmul(bank[:, 4 + i, 0:D], ffh[:, m, i * P:(i + 1) * P], W2[:, m, :], start=(m == 0), stop=False)
        t = PE.done(pe.matmul(bank[:, 4 + i, 0:D], ones[0:1, 0:P], b2[0:1, :], start=False, stop=True))
        DV.after(t)
        t = DV.done(dve.tensor_tensor(xt2[:, i, :], bank[:, 4 + i, 0:D], xt2[:, i, :], ALU.add))
    layer_norm(xh, xt2, [t])
    for i in range(NT):
        affine(xh, xh, "g_norm_out", "b_norm_out", i)
        seq(lambda: dve.tensor_tensor(x[:, i, :], x[:, i, :], xh[:, i, :], ALU.add))
    t_x4 = DV.last()
    phase_ends()
    phase_ends()

    HR, DR = 8, 32
    phase_begins()
    xr = xn
    t_xn = layer_norm(xr, x, [t_x4])
    t_xT = features_on_partitions(xT, lambda i, kt: xr[:, i, kt * P:(kt + 1) * P], [t_xn], [])
    wr_ = {c: sb(f"wr_{c}", [P, 2, D]) for c in "QKVGO"}
    wsw = {c: sb(f"wsw_{c}", [P, 2, D]) for c in "QK"}
    rtab = sb("rtab", [P, 4, 2, S])
    rmask = sb("rmask", [P, 3, P])
    gnv = sb("gnv", [P, 2, D])
    pairs = [(wr_[c][:, k, :].rearrange("p (h e) -> p h e", h=HR), ins["L1_attn_W_" + c][:, k * P:(k + 1) * P, :].rearrange("h p e -> p h e"))
             for c in "QKV" for k in range(2)]
    pairs += [(wr_[c][:, :, :], ins["L1_attn_W_" + c].rearrange("(k p) n -> p k n", p=P)) for c in "GO"]
    pairs += [(rtab[:, k, :, :], ins["rotary"][k].rearrange("(t p) n -> p t n", p=P)) for k in range(4)]
    pairs += [(gnv[:, k, :], row("L1_attn_gn_" + n).to_broadcast([P, D])) for k, n in enumerate(("weight", "bias"))]
    t_w = load("ld_ret", pairs)
    t = PO.done(pool.memset(rmask[:, :, :], 1.0))
    PO.after(t)
    for k in (0, 2):
        t_rm = PO.done(pool.affine_select(out=rmask[:, k, :], in_=rmask[:, k, :], compare_op=ALU.is_ge, fill=0.0, base=0,
                                          pattern=[[1, P]], channel_multiplier=-1))
    DV.after(t_w)
    for c in "QK":
        for par in range(2):
            t_sw = DV.done(dve.tensor_copy(wsw[c][:, :, :].rearrange("p k (e two) -> p (k e) two", two=2)[:, :, par],
                                           wr_[c][:, :, :].rearrange("p k (e two) -> p (k e) two", two=2)[:, :, 1 - par]))
    qkr = {c: sb(f"qkr_{c}", [P, 2, T]) for c in "QK"}
    rtmp = sb("rtmp", [P, T])
    PE.after(t_w, t_sw, t_xT)
    last_rot = {}
    for n_, c in enumerate("QK"):
        for m in range(2):
            b0 = 2 * m
            if n_:
                PE.after(last_rot[m])
            for k, w in enumerate((wr_[c], wsw[c])):
                for kt in range(2):
                    t = pe.matmul(bank[:, b0 + k, :], w[:, kt, m * P:(m + 1) * P], xT[:, kt, :], start=(kt == 0), stop=(kt == 1))
            t = PE.done(t)
            DV.after(t)
            ctab, stab = (rtab[:, 2 * n_ + k, m:m + 1, :].to_broadcast([P, NB, S]) for k in range(2))
            v3 = lambda a: a.rearrange("p (b s) -> p b s", b=NB)
            last_rot[m] = seq(lambda: dve.tensor_tensor(v3(qkr[c][:, m, :]), v3(bank[:, b0, :]), ctab, ALU.mult),
                              lambda: dve.tensor_tensor(v3(rtmp[:, :]), v3(bank[:, b0 + 1, :]), stab, ALU.mult),
                              lambda: dve.tensor_tensor(qkr[c][:, m, :], qkr[c][:, m, :], rtmp[:, :], ALU.add))
    t_rot = DV.last()
    vr = sb("vr", [P, NT, D])
    gr = sb("gr", [P, NT, D])
    for i in range(NT):
        for k, w in enumerate((wr_["V"], wr_["G"])):
            for kt in range(2):
                t = pe.matmul(bank[:, 4 + i, k * D:(k + 1) * D], xT[:, kt, i * P:(i + 1) * P], w[:, kt, :], start=(kt == 0), stop=(kt == 1))
        t = PE.done(t)
        AC.after(t)
        AC.done(act.copy(vr[:, i, :], bank[:, 4 + i, 0:D]))
        t_v = AC.done(act.activation(gr[:, i, :], bank[:, 4 + i, D:2 * D], ACT.Silu))
    sR = [sb(f"sR{j}", [P, 3, P]) for j in range(2)]
    yr = sb("yr", [P, NT, HR, DR])
    PE.after(t_rot, t_v)
    DV.after(t_rm)
    masked, used, y_read = {}, {}, {}
    for b in range(NB):
        for h in range(HR):
            j = h % 2
            if j in masked:
                PE.after(masked[j])
            rs = slice((h % 4) * DR, (h % 4 + 1) * DR)
            kq = lambda c, lo, n: qkr[c][rs, h // 4, b * S + lo:b * S + lo + n]
            pe.matmul(bank[:, j, 0:2 * P], kq("K", 0, P), kq("Q", 0, 2 * P), start=True, stop=True)
            t = PE.done(pe.matmul(bank[:, j, 2 * P:3 * P], kq("K", P, P), kq("Q", P, P), start=True, stop=True))
            DV.after(t)
            if j in used:
                DV.after(used[j])
            masked[j] = DV.done(dve.tensor_tensor(sR[j][:, :, :].rearrange("p c q -> p (c q)"), bank[:, j, 0:3 * P],
                                                  rmask[:, :, :].rearrange("p c q -> p (c q)"), ALU.mult))
            PE.after(masked[j])
            if b and h == 0:
                PE.after(y_read[0], y_read[1])
            vv = lambda kt: vr[:, b * 2 + kt, h * DR:(h + 1) * DR]
            o = [bank[:, 2 + qt, h * DR:(h + 1) * DR] for qt in range(2)]
            pe.matmul(o[0], sR[j][:, 0, :], vv(0), start=True, stop=True)
            pe.matmul(o[1], sR[j][:, 1, :], vv(0), start=True, stop=False)
            used[j] = PE.done(pe.matmul(o[1], sR[j][:, 2, :], vv(1), start=False, stop=True))
        for qt in range(2):
            AC.after(used[1])
            y_read[qt] = AC.done(act.copy(yr[:, b * 2 + qt, :, :].rearrange("p h d -> p (h d)"), bank[:, 2 + qt, 0:D]))
    gm, gv = sb("gm", [P, NT * HR]), sb("gv", [P, NT * HR])
    ysq = sb("ysq", [P, NT * HR, DR])
    y3 = yr[:, :, :, :].rearrange("p t h d -> p (t h) d")
    gb = lambda a: a[:, :].rearrange("p (n a) -> p n a", a=1).to_broadcast([P, NT * HR, DR])
    DV.after(y_read[0], y_read[1])
    t = seq(lambda: dve.tensor_reduce(gm[:, :], y3, AX.X, ALU.add),
            lambda: dve.tensor_scalar(gm[:, :], gm[:, :], 1.0 / DR, None, ALU.mult),
            lambda: dve.tensor_tensor(y3, y3, gb(gm), ALU.subtract),
            lambda: dve.tensor_tensor(ysq[:, :, :], y3, y3, ALU.mult),
            lambda: dve.tensor_reduce(gv[:, :], ysq[:, :, :], AX.X, ALU.add),
            lambda: dve.tensor_scalar(gv[:, :], gv[:, :], 1.0 / DR, EPS, ALU.mult, ALU.add))
    AC.after(t)
    t = AC.done(act.sqrt(gv[:, :], gv[:, :]))
    DV.after(t)
    seq(lambda: dve.reciprocal(gv[:, :], gv[:, :]),
        lambda: dve.tensor_tensor(y3, y3, gb(gv), ALU.mult))
    for i in range(NT):
        yi = yr[:, i, :, :].rearrange("p h d -> p (h d)")
        seq(lambda: dve.tensor_tensor(yi, yi, gnv[:, 0, :], ALU.mult),
            lambda: dve.tensor_tensor(yi, yi, gnv[:, 1, :], ALU.add),
            lambda: dve.tensor_tensor(yi, yi, gr[:, i, :], ALU.mult))
    t_yT = features_on_partitions(xT, lambda i, kt: yr[:, i, :, :].rearrange("p h d -> p (h d)")[:, kt * P:(kt + 1) * P],
                                  [DV.last()], [t_rot])
    t_x5 = add_to_x(project_tokens(xT, wr_["O"], None, [t_yT, t_v], first_bank=4), first_bank=4)
    phase_ends()

    KA = 8
    phase_begins()
    ids = sb("ids", [1, KA], I32)
    wts = sb("wts", [P, KA])
    wsel = sb("wsel", [P, KA, 2, D])
    bsel = sb("bsel", [1, KA, D])
    wmix = sb("wmix", [P, 2, D])
    wmT = sb("wmT", [P, 2, D])
    bmix = sb("bmix", [1, D])
    t_ids = load("ld_ids", [(ids[:, :], row("L1_ffn_ids")), (wts[:, :], row("L1_ffn_weights").to_broadcast([P, KA]))])
    sp.wait_ge(*t_ids)
    ld = Load(nc, "ld_sel")
    for k in range(KA):
        a = sp.value_load(ids[0:1, k:k + 1], min_val=0, max_val=31)
        ld.add(sp.dma_start(wsel[:, k, :, :], ins["L1_ffn_W"][bass.ds(a, 1), :, :].rearrange("a (t p) d -> p (a t) d", p=P)))
        ld.add(sp.dma_start(bsel[:, k, :], ins["L1_ffn_b"][bass.ds(a, 1), :]))
    t_xn = layer_norm(xn, x, [t_x5])
    t_xT = features_on_partitions(xT, lambda i, kt: xn[:, i, kt * P:(kt + 1) * P], [t_xn], [])
    DV.after(ld.token(), t_ids)
    flat = lambda t: t.rearrange("p t d -> p (t d)")
    seq(lambda: dve.tensor_scalar(flat(wmix[:, :, :]), flat(wsel[:, 0, :, :]), wts[:, 0:1], None, ALU.mult))
    seq(lambda: dve.tensor_scalar(bmix[:, :], bsel[:, 0, :], wts[0:1, 0:1], None, ALU.mult))
    for k in range(1, KA):
        seq(lambda: dve.scalar_tensor_tensor(flat(wmix[:, :, :]), flat(wsel[:, k, :, :]), wts[:, k:k + 1], flat(wmix[:, :, :]), ALU.mult, ALU.add))
        seq(lambda: dve.scalar_tensor_tensor(bmix[:, :], bsel[:, k, :], wts[0:1, k:k + 1], bmix[:, :], ALU.mult, ALU.add))
    PE.after(DV.last())
    for kt in range(2):
        for ot in range(2):
            t = PE.done(pe.transpose(bank[:, 2 + kt, ot * P:(ot + 1) * P], wmix[:, ot, kt * P:(kt + 1) * P], ident[:, :]))
        AC.after(t)
        t_wm = AC.done(act.copy(wmT[:, kt, :], bank[:, 2 + kt, 0:D]))
    t_x6 = add_to_x(project_tokens(xT, wmT, bmix[0:1, :], [t_wm, t_xT], first_bank=4), first_bank=4)

    sp.wait_ge(*t_x6)
    done = Load(nc, "stored")
    done.add(sp.dma_start(out.rearrange("b (t p) d -> p (b t) d", p=P), x[:, :, :]))
    sp.wait_ge(*done.token())


def kernel(**inputs):
    import numpy as _np
    import concourse.bacc as _bacc
    from concourse.bass_utils import run_bass_kernel_spmd as _run

    nc = _bacc.Bacc("TRN2", target_bir_lowering=False, num_devices=1)
    arrays, aps = {}, {}
    for name in inputs:
        a = _np.ascontiguousarray(inputs[name])
        if a.shape == ():
            a = a.reshape(1)
        if a.dtype == _np.bool_:
            a = a.view(_np.uint8)
        if name in UNUSED:
            continue
        arrays["in_" + name] = a
        aps[name] = nc.dram_tensor("in_" + name, a.shape, mybir.dt.from_np(a.dtype), kind="ExternalInput").ap()
    for name, a in constants().items():
        arrays["in_" + name] = a
        aps[name] = nc.dram_tensor("in_" + name, a.shape, mybir.dt.from_np(a.dtype), kind="ExternalInput").ap()
    out = nc.dram_tensor("out_x", (NB, S, D), F32, kind="ExternalOutput").ap()
    build(nc, aps, out)
    r = _run(nc, [arrays], core_ids=[0])
    return r.results[0]["out_x"]
```

```python
import math
from contextlib import ExitStack

import numpy as np

import concourse.bass as bass
from concourse import mybir

F32 = mybir.dt.float32
BF16 = mybir.dt.bfloat16
I32 = mybir.dt.int32
ALU = mybir.AluOpType
ACT = mybir.ActivationFunctionType
AX = mybir.AxisListType

P = 128
D = 256
DC = 192
NB = 2
S = 256
T = NB * S
NT = T // P
S2 = 4096
H0, D0 = 16, 16
BLK = 512
NBB = S2 // BLK
NBLK = NB * NBB
NH = NB * H0
NCH = S2 // P
VW = D0 + 1
NSTK = 6
STACK = ((0, 0), (0, 1), (0, 2), (1, 0), (1, 1), (2, 0))
EPS = 1e-5


class Count:

    def __init__(self, nc, name, per, credit_steps=0):
        self.sem = nc.alloc_semaphore(name)
        self.per, self.credit = per, per * credit_steps + 1 if credit_steps else 0

    def give(self, eng):
        if self.credit:
            eng.sem_inc(self.sem, self.credit)

    def wait(self, eng, n, k=None):
        eng.wait_ge(self.sem, n * self.per + (self.per if k is None else k) + self.credit)

    def inc(self, ins):
        return ins.then_inc(self.sem, 1)


class Line:

    def __init__(self, nc, eng, name):
        self.eng, self.sem, self.n = eng, nc.alloc_semaphore(name), 0
        self.seen = {}

    def after(self, *tokens):
        for sem, value in tokens:
            if self.seen.get(sem.name, 0) < value:
                self.eng.wait_ge(sem, value)
                self.seen[sem.name] = value

    def done(self, ins):
        self.n += 1
        ins.then_inc(self.sem, 1)
        return (self.sem, self.n)

    def last(self):
        return (self.sem, self.n)


class Load:

    def __init__(self, nc, name):
        self.sem, self.n = nc.alloc_semaphore(name), 0

    def add(self, ins):
        self.n += 16
        ins.then_inc(self.sem, 16)

    def token(self):
        return (self.sem, self.n)




def constants():
    w = 2 * np.pi * (np.arange(S)[None, :] + 0.5) * np.arange(S)[:, None] / (2 * S)
    dft = np.stack([np.cos(w), np.sin(w), np.cos(w).T / S, np.sin(w).T / S]).astype(np.float32)
    heads, width, base_len = 8, 32, 512.0
    pos = np.arange(S, dtype=np.float64)[None, :]
    base = ((np.arange(0, width, 2) + 0.4 * width) / (1.4 * width))[:, None]
    scale = base ** (pos / base_len)
    angle = pos / 10000.0 ** (np.arange(width // 2) / (width // 2))[:, None]
    gamma = 1 - np.exp(np.linspace(math.log(1 / 32), math.log(1 / 512), heads))[:, None]
    sign = np.tile([-1.0, 1.0], width // 2)[:, None]
    tabs = []
    for power in (1, -1):
        for f, s in ((np.cos, 1.0), (np.sin, sign)):
            t = np.repeat(f(angle) * scale ** power, 2, axis=0) * s
            tabs.append((t[None] * (gamma ** (power * pos))[:, None, :]).reshape(heads * width, S))
    return {"dft": dft, "rotary": np.stack(tabs).astype(np.float32)}


def build(nc, ins, out):
    pe, act, dve, pool, sp = nc.tensor, nc.scalar, nc.vector, nc.gpsimd, nc.sync
    PE, AC, DV, PO = Line(nc, pe, "pe_line"), Line(nc, act, "act_line"), Line(nc, dve, "dve_line"), Line(nc, pool, "pool_line")

    scopes = []

    def sb(name, shape, dt=F32):
        return scopes[-1].enter_context(nc.sbuf_tensor(name, shape, dt))

    def phase_begins():
        scopes.append(ExitStack())

    def phase_ends():
        nc.all_engine_barrier()
        scopes.pop().close()

    phase_begins()

    def load(name, pairs, eng=sp):
        ld = Load(nc, name)
        with nc.allow_non_contiguous_dma(reason="some are short vectors"):
            for dst, src in pairs:
                ld.add(eng.dma_start(dst, src))
        return ld.token()

    def row(name):
        return ins[name].rearrange("(a n) -> a n", a=1)

    bank = nc.alloc_psum_tensor("bank", [P, 8, 512], F32)

    ident = sb("ident", [P, P])
    identb = sb("identb", [P, P], BF16)
    ones = sb("ones", [P, 512])
    x = sb("x", [P, NT, D])
    xn = sb("xn", [P, NT, D])
    xT = sb("xT", [P, 2, T])
    stats = sb("stats", [P, NT, 6])
    mv = sb("mv", [P, NT, 2])
    rstd = sb("rstd", [P, NT])

    t_x = load("ld_x", [(x[:, :, :], ins["x"].rearrange("b (t p) d -> p (b t) d", p=P))])
    zeros = sb("zeros", [P, 512])
    t_zeros = DV.done(dve.memset(zeros[:, :], 0.0))
    t_ones = DV.done(dve.memset(ones[:, :], 1.0))
    t = PO.done(pool.memset(ident[:, :], 0.0))
    PO.after(t)
    t_ident = PO.done(pool.affine_select(out=ident[:, :], in_=ident[:, :], compare_op=ALU.not_equal, fill=1.0,
                                         base=0, pattern=[[-1, P]], channel_multiplier=1))
    DV.after(t_ident)
    t_identb = DV.done(dve.tensor_copy(identb[:, :], ident[:, :]))

    spare = nc.alloc_semaphore("spare")

    def hold(eng):
        eng.sem_inc(spare, 1)

    def layer_norm(dst, src, after, n_tiles=NT):
        DV.after(*after)
        for i in range(n_tiles):
            t = DV.done(dve.bn_stats(stats[:, i, :], src[:, i, :]))
        DV.after(t)
        for i in range(n_tiles):
            t = DV.done(dve.bn_aggr(mv[:, i, :], stats[:, i, :]))
        DV.after(t)
        t = DV.done(dve.tensor_scalar(rstd[:, 0:n_tiles], mv[:, 0:n_tiles, 1], EPS, None, ALU.add))
        AC.after(t)
        t = AC.done(act.sqrt(rstd[:, 0:n_tiles], rstd[:, 0:n_tiles]))
        DV.after(t)
        t = DV.done(dve.reciprocal(rstd[:, 0:n_tiles], rstd[:, 0:n_tiles]))
        DV.after(t)
        for i in range(n_tiles):
            t = DV.done(dve.tensor_scalar(dst[:, i, :], src[:, i, :], mv[:, i, 0:1], rstd[:, i:i + 1],
                                          ALU.subtract, ALU.mult))
        return t

    def features_on_partitions(dst, src, after, free, banks=(0, 1)):
        PE.after(*after, *free, t_ident)
        toks = []
        for kt in range(D // P):
            for i in range(NT):
                t = PE.done(pe.transpose(bank[:, banks[kt], i * P:(i + 1) * P], src(i, kt), ident[:, :]))
            AC.after(t, *free)
            toks.append(AC.done(act.copy(dst[:, kt, :], bank[:, banks[kt], :])))
        return toks[-1]

    NSTATE, LA, LB = 64, 32, 8
    Ap = [sb(f"Ap{c}", [P, 4, LA, 32]) for c in "ri"]
    Bp = [sb(f"Bp{c}", [P, 4, LB, 32]) for c in "ri"]
    phase_begins()
    W2 = 2 * NSTATE
    ldt = sb("ldt", [P, 2])
    dt_n = sb("dt_n", [P, 2])
    dt_r = sb("dt_r", [P, 2])
    dt_p = sb("dt_p", [P, 2])
    dt_i = sb("dt_i", [P, 2], I32)
    are, aim, cre, cim = (sb(n, [P, 2, NSTATE]) for n in ("are", "aim", "cre", "cim"))
    t_s4 = load("ld_s4", [(tile[:, :, :], ins["L1_xattn_" + n].rearrange("(t p) n -> p t n", p=P))
                          for tile, n in ((are, "A_re"), (aim, "A_im"), (cre, "C_re"), (cim, "C_im"))]
                + [(ldt[:, :], ins["L1_xattn_log_dt"].rearrange("(t p) -> p t", p=P))], eng=act)

    def ts(dst, src, a, b=None, op0=ALU.mult, op1=None, line=None):
        line = line or DV
        line.after(line.last())
        return line.done(line.eng.tensor_scalar(dst, src, a, b, op0, op1) if op1 is not None
                         else line.eng.tensor_scalar(dst, src, a, b, op0))

    def tt(dst, a, b, op, line=None):
        line = line or DV
        line.after(line.last())
        return line.done(line.eng.tensor_tensor(dst, a, b, op))

    BIG = 1.5 * 2.0 ** 23
    LN2_HI = 0.693359375
    DV.after(t_s4)
    ts(dt_n[:, :], ldt[:, :], 1.0 / math.log(2.0), BIG, ALU.mult, ALU.add)
    ts(dt_n[:, :], dt_n[:, :], BIG, None, ALU.subtract)
    ts(dt_r[:, :], dt_n[:, :], -LN2_HI)
    tt(dt_r[:, :], ldt[:, :], dt_r[:, :], ALU.add)
    ts(dt_p[:, :], dt_n[:, :], -(math.log(2.0) - LN2_HI))
    tt(dt_r[:, :], dt_r[:, :], dt_p[:, :], ALU.add)
    ts(dt_p[:, :], dt_r[:, :], 1.0 / math.factorial(8), 1.0 / math.factorial(7), ALU.mult, ALU.add)
    for k in range(6, -1, -1):
        tt(dt_p[:, :], dt_p[:, :], dt_r[:, :], ALU.mult)
        ts(dt_p[:, :], dt_p[:, :], 1.0 / math.factorial(k), None, ALU.add)
    ts(dt_i[:, :], dt_n[:, :], 127.0, 2.0 ** 23, ALU.add, ALU.mult)
    t_dt = tt(dt_p[:, :], dt_p[:, :], dt_i[:, :].bitcast(F32), ALU.mult)

    HALVINGS = 10
    wch = [sb(f"wch{c}", [P, 2, NSTATE]) for c in "ri"]
    for dst, src in zip(wch, (are, aim)):
        for t_ in range(2):
            t = ts(dst[:, t_, :], src[:, t_, :], dt_p[:, t_:t_ + 1], 2.0 ** -HALVINGS, ALU.mult, ALU.mult)
    wr, wi, AR_, AI_, CR_, CI_, er, ei, fr, fi, g1, g2 = (sb(n, [P, W2]) for n in (
        "wr", "wi", "A_r", "A_i", "C_r", "C_i", "er", "ei", "fr", "fi", "g1", "g2"))
    PE.after(t, t_ident, t_s4)
    for k, src in enumerate((*wch, are, aim, cre, cim)):
        t = PE.done(pe.transpose(bank[:, 6 + k // 4, k % 4 * P:(k % 4 + 1) * P], src[:, :, :].rearrange("p t n -> p (t n)"), ident[:, :]))
    AC.after(t)
    for k, dst in enumerate((wr, wi, AR_, AI_, CR_, CI_)):
        t_s4T = AC.done(act.copy(dst[:, :], bank[:, 6 + k // 4, k % 4 * P:(k % 4 + 1) * P]))
    DV.after(t_s4T)
    tt(g1[:, :], AR_[:, :], AR_[:, :], ALU.mult)
    tt(g2[:, :], AI_[:, :], AI_[:, :], ALU.mult)
    tt(g1[:, :], g1[:, :], g2[:, :], ALU.add)
    DV.after(DV.last())
    rabs = sb("rabs", [P, W2])
    t_rabs = DV.done(dve.reciprocal(rabs[:, :], g1[:, :]))

    phase_begins()
    V = sb("V", [P, NB * NCH, H0, VW])
    phase_begins()
    wkv1 = sb("wkv1", [P, 2 * D + P])
    wkv2 = sb("wkv2", [DC - P + 1, 2 * D + P])
    wk_all = [("L0_xattn_Wk", 0, D), ("L0_xattn_Wv", D, D), ("L1_xattn_Wk", 2 * D, P)]
    pairs = []
    for name, at, n in wk_all:
        pairs += [(wkv1[:, at:at + n], ins[name][0:P, :]), (wkv2[0:DC - P, at:at + n], ins[name][P:DC, :])]
    pairs += [(wkv2[DC - P:DC - P + 1, 0:D], row("L0_xattn_bk")), (wkv2[DC - P:DC - P + 1, D:2 * D], row("L0_xattn_bv"))]
    t_m = DV.done(dve.memset(wkv2[DC - P:DC - P + 1, :], 0.0))
    act.wait_ge(*t_m)
    t_wkv = load("ld_wkv", pairs, eng=act)

    cx = [sb(f"cx{j}", [P, BLK // P, DC]) for j in range(2)]
    ctx_d = ins["ctx_768"].rearrange("b (n c p) d -> (b n) p c d", p=P, c=BLK // P)
    ctx_loaded = [Count(nc, f"ctx_loaded{j}", 16) for j in range(2)]
    ctx_turned = Count(nc, "ctx_turned", 1, 2)
    ctx_turned.give(pe)

    def load_ctx(n, j):
        ctx_turned.wait(sp, n - 2)
        sp.dma_start(cx[j][:, :, :], ctx_d[bass.ds(n, 1), :, :, :].rearrange("a p c d -> (a p) c d"))\
            .then_inc(ctx_loaded[j].sem, 16)

    for j in range(2):
        load_ctx(j, j)
    t_xn = layer_norm(xn, x, [t_x])
    t_xT = features_on_partitions(xT, lambda i, kt: xn[:, i, kt * P:(kt + 1) * P], [t_xn], [])
    wq = sb("wq", [P, 2, D])
    bq = sb("bq", [1, D])
    t_wq = load("ld_wq", [(wq[:, :, :], ins["L0_xattn_Wq"].rearrange("(k p) n -> p k n", p=P)),
                          (bq[:, :], row("L0_xattn_bq"))])
    qf = sb("qf", [P, T])
    qr = sb("qr", [P, T])
    qparts = sb("qparts", [P, 2, 3, T], BF16)
    q_stack_d = nc.dram_tensor("q_stack_d", [NH, NSTK, D0, S], BF16).ap()
    k_parts_d = nc.dram_tensor("k_parts_d", [NB * D, 3, S2], BF16).ap()
    k1_parts_d = nc.dram_tensor("k1_parts_d", [NB * P, 3, S2], BF16).ap()

    def three_parts(parts, full, rest, after):
        DV.after(*after)
        t = DV.done(dve.tensor_copy(parts(0), full))
        DV.after(t)
        t = DV.done(dve.tensor_tensor(rest, full, parts(0), ALU.subtract))
        DV.after(t)
        t = DV.done(dve.tensor_copy(parts(1), rest))
        DV.after(t)
        return DV.done(dve.tensor_tensor(parts(2), rest, parts(1), ALU.subtract))

    ld_q = Load(nc, "st_qparts")
    PE.after(t_wq, t_xT, t_ones)
    for mt in range(2):
        for kt in range(2):
            pe.matmul(bank[:, 2 + mt, :], wq[:, kt, mt * P:(mt + 1) * P], xT[:, kt, :], start=(kt == 0), stop=False)
        t_q = PE.done(pe.matmul(bank[:, 2 + mt, :], bq[0:1, mt * P:(mt + 1) * P], ones[0:1, :], start=False, stop=True))
        DV.after(t_q)
        t = DV.done(dve.tensor_scalar(qf[:, :], bank[:, 2 + mt, :], float(D0) ** -0.5, None, ALU.mult))
        t = three_parts(lambda k: qparts[:, mt, k, :], qf[:, :], qr[:, :], [t])
        act.wait_ge(*t)
        for b in range(NB):
            h0 = b * H0 + mt * (P // D0)
            for s, (kp, qp) in enumerate(STACK):
                ld_q.add(act.dma_start(q_stack_d[h0:h0 + P // D0, s, :, :], qparts[:, mt, qp, b * S:(b + 1) * S]))

    cT1 = [sb(f"cT1_{j}", [P, BLK]) for j in range(2)]
    cT2 = [sb(f"cT2_{j}", [DC - P + 1, BLK]) for j in range(2)]
    kf = sb("kf", [P, 3, BLK])
    kr = sb("kr", [P, 3, BLK])
    kparts = [sb(f"kparts{j}", [P, 3, 3, BLK], BF16) for j in range(2)]
    for j in range(2):
        t_c = DV.done(dve.memset(cT2[j][DC - P:DC - P + 1, :], 1.0))
    t_v1 = PO.done(pool.memset(V[:, :, :, D0:VW], 1.0))

    cT_copied = Count(nc, "cT_copied", 2, 1)
    k_made = Count(nc, "k_made", 3)
    v_made = Count(nc, "v_made", 2, 2)
    kf_copied = Count(nc, "kf_copied", 3, 1)
    v_copied = Count(nc, "v_copied", 2, 1)
    kh_done = Count(nc, "kh_done", 6, 1)
    kl_done = Count(nc, "kl_done", 6, 1)
    kparts_out = [Count(nc, f"kparts_out{j}", 48, 1) for j in range(2)]
    for c, e in ((cT_copied, act), (v_made, pe), (kf_copied, act), (v_copied, act),
                 (kh_done, dve), (kl_done, pool), (kparts_out[0], sp), (kparts_out[1], sp)):
        c.give(e)

    PE.after(t_wkv, t_c, t_q, t_xT)
    AC.after(t_v1, t_xT)
    PO.after(t_ones)
    DV.after(t_q)

    def turn(batch, bpair, j):
        pair, n = bpair + batch * (NBB // 2), bpair * 2 + j + batch * NBB
        ctx_loaded[j].wait(pe, pair)
        cT_copied.wait(pe, n - 1)
        for c in range(BLK // P):
            pe.transpose(bank[:, 0, c * P:(c + 1) * P], cx[j][:, c, 0:P], ident[:, :])
            ins_ = pe.transpose(bank[0:DC - P, 1, c * P:(c + 1) * P], cx[j][:, c, P:DC], ident[:, :])
        ctx_turned.inc(ins_)
        ctx_turned.wait(act, n)
        v_made.wait(act, n - 2)
        cT_copied.inc(act.copy(cT1[j][:, :], bank[:, 0, :]))
        cT_copied.inc(act.copy(cT2[j][0:DC - P, :], bank[0:DC - P, 1, :]))

    def project(batch, bpair, j):
        blk = bpair * 2 + j
        pair, n = bpair + batch * (NBB // 2), blk + batch * NBB
        cT_copied.wait(pe, n)
        for m, at in enumerate((0, P, 2 * D)):
            kf_copied.wait(pe, n - 1, m + 1)
            pe.matmul(bank[:, 2 + m, :], wkv1[:, at:at + P], cT1[j][:, :], start=True, stop=False)
            k_made.inc(pe.matmul(bank[:, 2 + m, :], wkv2[:, at:at + P], cT2[j][:, :], start=False, stop=True))
        for c in range(BLK // P):
            if c % 2 == 0:
                v_copied.wait(pe, n - 1, c // 2 + 1)
            o = bank[:, 5 + c // 2, (c % 2) * D:(c % 2 + 1) * D]
            pe.matmul(o, cT1[j][:, c * P:(c + 1) * P], wkv1[:, D:2 * D], start=True, stop=False)
            ins_ = pe.matmul(o, cT2[j][:, c * P:(c + 1) * P], wkv2[:, D:2 * D], start=False, stop=True)
            if c % 2 == 1:
                v_made.inc(ins_)
        for m in range(3):
            k_made.wait(act, n, m + 1)
            kl_done.wait(act, n - 1, 2 * m + 1)
            kh_done.wait(act, n - 1, 2 * m + 2)
            kf_copied.inc(act.copy(kf[:, m, :], bank[:, 2 + m, :]))
            kf_copied.wait(dve, n, m + 1)
            kparts_out[j].wait(dve, pair - 1)
            kh_done.inc(dve.tensor_scalar(kparts[j][:, m, 0, :], kf[:, m, :], 1.0, None, ALU.mult))
            kh_done.wait(dve, n, 2 * m + 1)
            kl_done.wait(dve, n - 1, 2 * m + 2)
            kh_done.inc(dve.tensor_tensor(kr[:, m, :], kf[:, m, :], kparts[j][:, m, 0, :], ALU.subtract))
            kh_done.wait(pool, n, 2 * m + 2)
            kparts_out[j].wait(pool, pair - 1)
            kl_done.inc(pool.tensor_tensor(kparts[j][:, m, 1, :], kr[:, m, :], zeros[:, :], ALU.add))
            kl_done.wait(pool, n, 2 * m + 1)
            kl_done.inc(pool.tensor_tensor(kparts[j][:, m, 2, :], kr[:, m, :], kparts[j][:, m, 1, :], ALU.subtract))
            kl_done.wait(sp, n, 2 * m + 2)
            dst, row0 = (k_parts_d, batch * D + m * P) if m < 2 else (k1_parts_d, batch * P)
            sp.dma_start(dst[row0:row0 + P, :, bass.ds(blk * BLK, BLK)],
                         kparts[j][:, m, :, :]).then_inc(kparts_out[j].sem, 16)
        for h in range(2):
            v_made.wait(act, n, h + 1)
            v_copied.inc(act.copy(V[:, bass.ds(n * 4 + 2 * h, 2), :, 0:D0],
                                  bank[:, 5 + h, :].rearrange("p (c h d) -> p c h d", c=2, h=H0)))

    for batch in range(NB):
        n0 = batch * NBB
        turn(batch, 0, 0)
        with nc.Fori(0, NBB // 2 - 1, 1) as bpair:
            load_ctx(bpair * 2 + 2 + n0, 0)
            turn(batch, bpair, 1)
            project(batch, bpair, 0)
            load_ctx(bpair * 2 + 3 + n0, 1)
            turn(batch, bpair + 1, 0)
            project(batch, bpair, 1)
        if batch < NB - 1:
            load_ctx(n0 + NBB, 0)
        turn(batch, NBB // 2 - 1, 1)
        project(batch, NBB // 2 - 1, 0)
        if batch < NB - 1:
            load_ctx(n0 + NBB + 1, 1)
        project(batch, NBB // 2 - 1, 1)
    for j in range(2):
        kparts_out[j].wait(sp, NBLK // 2 - 1)
    sp.wait_ge(*ld_q.token())
    phase_ends()
    PO.after(t_rabs, t_s4T)

    def cmul(outr, outi, ar, ai, br, bi, s1, s2):
        tt(s1, ar, br, ALU.mult, PO)
        tt(s2, ai, bi, ALU.mult, PO)
        tt(outr, s1, s2, ALU.subtract, PO)
        tt(s1, ar, bi, ALU.mult, PO)
        tt(s2, ai, br, ALU.mult, PO)
        return tt(outi, s1, s2, ALU.add, PO)

    f, G1, G2 = slice(None), g1[:, :], g2[:, :]
    ts(er[:, :], wr[:, :], 1.0 / 5.0, 1.0, ALU.mult, ALU.add, line=PO)
    ts(ei[:, :], wi[:, :], 1.0 / 5.0, 0.0, ALU.mult, ALU.add, line=PO)
    for k in (4, 3, 2):
        cmul(fr[:, :], fi[:, :], er[:, :], ei[:, :], wr[:, :], wi[:, :], G1, G2)
        ts(er[:, :], fr[:, :], 1.0 / k, 1.0, ALU.mult, ALU.add, line=PO)
        ts(ei[:, :], fi[:, :], 1.0 / k, 0.0, ALU.mult, ALU.add, line=PO)
    cmul(fr[:, :], fi[:, :], er[:, :], ei[:, :], wr[:, :], wi[:, :], G1, G2)
    a, b = (fr, fi), (er, ei)
    for k in range(HALVINGS):
        ts(wr[:, :], a[0][:, :], 1.0, 2.0, ALU.mult, ALU.add, line=PO)
        cmul(b[0][:, :], b[1][:, :], a[0][:, :], a[1][:, :], wr[:, :], a[1][:, :], G1, G2)
        a, b = b, a
    AR, AI, CR, CI = (q[:, :] for q in (AR_, AI_, CR_, CI_))
    ts(wi[:, :], rabs[:, :], 2.0, 0.0, ALU.mult, ALU.add, line=PO)
    tt(AR, AR, wi[:, :], ALU.mult, PO)
    tt(AI, AI, wi[:, :], ALU.mult, PO)
    ts(AI, AI, -1.0, 0.0, ALU.mult, ALU.add, line=PO)
    cmul(b[0][:, :], b[1][:, :], AR, AI, CR, CI, G1, G2)
    cmul(AR, AI, b[0][:, :], b[1][:, :], a[0][:, :], a[1][:, :], G1, G2)
    t_z = ts(a[0][:, :], a[0][:, :], 1.0, 1.0, ALU.mult, ALU.add, line=PO)
    zz = [[a[0], a[1]], [b[0], b[1]]]

    def keep(dst, src):
        PO.after(PO.last())
        return PO.done(pool.tensor_tensor(dst, src.rearrange("p (q g) -> p q g", q=4),
                                          zeros[:, 0:P].rearrange("p (q g) -> p q g", q=4), ALU.add))

    keep(Ap[0][:, :, 0, :], AR)
    keep(Ap[1][:, :, 0, :], AI)
    keep(Bp[0][:, :, 1, :], a[0][:, :])
    keep(Bp[1][:, :, 1, :], a[1][:, :])
    s1, s2 = sb("s1", [P, 4, LA // 2, 32]), sb("s2", [P, 4, LA // 2, 32])
    PO.done(pool.memset(Bp[0][:, :, 0, :], 1.0))
    PO.done(pool.memset(Bp[1][:, :, 0, :], 0.0))
    cur = 0

    def square(cur):
        z, y = zz[cur], zz[1 - cur]
        cmul(y[0][:, :], y[1][:, :], z[0][:, :], z[1][:, :], z[0][:, :], z[1][:, :],
             *(q[:, 0, 0:4, :].rearrange("p a g -> p (a g)") for q in (s1, s2)))
        return 1 - cur

    def extend(pw, m, cur):
        zb = [q[:, :].rearrange("p (q a g) -> p q a g", q=4, a=1).to_broadcast([P, 4, m, 32]) for q in zz[cur]]
        return cmul(pw[0][:, :, m:2 * m, :], pw[1][:, :, m:2 * m, :], pw[0][:, :, 0:m, :], pw[1][:, :, 0:m, :],
                    zb[0], zb[1], s1[:, :, 0:m, :], s2[:, :, 0:m, :])

    for m in (2, 4):
        cur = square(cur)
        extend(Bp, m, cur)
    for m in (1, 2, 4, 8, 16):
        cur = square(cur)
        extend(Ap, m, cur)
    t_pow = ts(Bp[1][:, :, :, :], Bp[1][:, :, :, :], -1.0, 0.0, ALU.mult, ALU.add, line=PO)

    NS = NSTK * D0
    HK = S2 // 2
    ks = [sb(f"ks{i}", [NS + 3, S2], BF16) for i in range(4)]
    qs = [sb(f"qs{j}", [NS + 3, S], BF16) for j in range(4)]
    vs = [sb(f"vs{j}", [P, NCH, 32]) for j in range(2)]
    pT = [sb(f"pT{j}", [P, 4 * S]) for j in range(2)]
    rmax = [sb(f"rmax{j}", [P, 2, 8]) for j in range(2)]
    nmax = sb("nmax", [P, 2])
    nres = sb("nres", [P, 2])
    mparts = sb("mparts", [P, 2, 3], BF16)
    ao = sb("ao", [P, NH, 2, D0])
    oT = sb("oT", [P, S])
    fold = sb("fold", [P, VW])
    rden = sb("rden", [P, 2])
    DV.done(dve.memset(ks[0][NS:NS + 3, :], 1.0))
    for i in range(1, 4):
        t_kones = AC.done(act.copy(ks[i][NS:NS + 3, :].rearrange("p (a n) -> p a n", a=S2 // BLK),
                                   ones[NS:NS + 3, :].rearrange("p (a n) -> p a n", a=1).to_broadcast([3, S2 // BLK, BLK])))
    for j in range(2):
        t_vz = DV.done(dve.memset(vs[j][:, :, :], 0.0))
    AC.after(t_vz)
    t_f = DV.done(dve.tensor_copy(fold[0:32, :], ident[0:32, 0:VW]))
    for q in range(1, 4):
        t_f = DV.done(dve.tensor_copy(fold[32 * q:32 * q + 32, :], ident[0:32, 0:VW]))
    PE.after(t_f)

    key_in = [Count(nc, f"key_in{i}", 16 * NSTK) for i in range(4)]
    query_in = [Count(nc, f"query_in{j}", 16) for j in range(4)]
    max_made = Count(nc, "max_made", 16)
    max_read = Count(nc, "max_read", 16, 1)
    rows_made = Count(nc, "rows_made", 1)
    rows_read = Count(nc, "rows_read", 1, 1)
    max_step = Count(nc, "max_step", 6)
    st_made = Count(nc, "st_made", 8, 4)
    p_made = Count(nc, "p_made", 8, 1)
    pv_made = Count(nc, "pv_made", 8, 4)
    vs_copied = Count(nc, "vs_copied", 1)
    oT_copied = Count(nc, "oT_copied", 1, 1)
    o_made = Count(nc, "o_made", 1, 1)
    o_done = Count(nc, "o_done", 2, 2)
    for c, e in ((max_read, dve), (rows_read, act), (st_made, pe), (p_made, act), (pv_made, pe), (oT_copied, act), (o_made, pe), (o_done, dve)):
        c.give(e)

    def load_queries(four, i):
        n = four * 4 + i
        st_made.wait(sp, n - 4)
        sp.dma_start(qs[i][0:NS, :], q_stack_d[bass.ds(n, 1), :, :, :].rearrange("a s d q -> (a s d) q"))\
            .then_inc(query_in[i].sem, 16)

    def load_keys(four, i):
        n = four * 4 + i
        st_made.wait(sp, n - 4)
        kd = k_parts_d[bass.ds(n * D0, D0), :, :]
        for s, (kp, qp) in enumerate(STACK):
            sp.dma_start(ks[i][s * D0:(s + 1) * D0, :], kd[:, kp, :]).then_inc(key_in[i].sem, 16)

    def values(four, i):
        n, j = four * 4 + i, i % 2
        pv_made.wait(act, n - 2)
        hold(act)
        vs_copied.inc(act.copy(vs[j][:, :, 0:VW], V[:, bass.ds((n // H0) * NCH, NCH), bass.ds(n % H0, 1), :]
                               .rearrange("p c a d -> p c (a d)")))

    def max_chunk(four, i, u):
        n, qt, c, b = four * 4 + i, u // 8, u % 8, u % 2
        if u == 0:
            query_in[i].wait(pe, four)
            key_in[i].wait(pe, four)
        if u < 2:
            max_read.wait(pe, n - 1, u + 15)
        else:
            max_read.wait(pe, n, u - 1)
        max_made.inc(pe.matmul(bank[:, b, :], qs[i][0:NS, qt * P:(qt + 1) * P], ks[i][0:NS, c * 512:(c + 1) * 512],
                               start=True, stop=True))
        max_made.wait(dve, n, u + 1)
        max_read.inc(dve.tensor_reduce(rmax[i % 2][:, qt, c:c + 1], bank[:, b, :], AX.X, ALU.max))

    def max_rows_step(four, i, k):
        n, part = four * 4 + i, (k - 1) // 2
        if k == 0:
            max_read.wait(dve, n, 16)
            max_step.inc(dve.tensor_reduce(nmax[:, :], rmax[i % 2][:, :, :], AX.X, ALU.max, negate=True))
            return
        max_step.wait(dve, n, k)
        src = nmax if part == 0 else nres
        if k % 2:
            max_step.inc(dve.tensor_copy(mparts[:, :, part], src[:, :]))
        else:
            max_step.inc(dve.tensor_tensor(nres[:, :], src[:, :], mparts[:, :, part], ALU.subtract))

    def max_rows(four, i):
        n = four * 4 + i
        max_step.wait(pe, n)
        o_done.wait(pe, n - 2)
        for qt in range(2):
            ins_ = pe.matmul(bank[NS:NS + 3, 7, qt * P:(qt + 1) * P], mparts[:, qt, :], identb[:, :],
                             start=True, stop=True)
        rows_made.inc(ins_)
        rows_made.wait(act, n)
        rows_read.inc(act.copy(qs[i][NS:NS + 3, :], bank[NS:NS + 3, 7, 0:S]))

    def scores(four, i, g):
        n, j, b0 = four * 4 + i, i % 2, 2 + 2 * (g % 2)
        p_made.wait(pe, n if g >= 2 else n - 1, g - 1 if g >= 2 else 7 + g)
        if g == 0:
            rows_read.wait(pe, n)
        for c in range(4):
            k0 = (4 * g + c) * P
            ins_ = pe.matmul(bank[:, b0 + c // 2, (c % 2) * S:(c % 2 + 1) * S], ks[i][:, k0:k0 + P], qs[i][:, :],
                             start=True, stop=True)
        st_made.inc(ins_)
        st_made.wait(act, n, g + 1)
        pv_made.wait(act, n if g >= 2 else n - 1, g - 1 if g >= 2 else 7 + g)
        p_made.inc(act.activation(pT[g % 2][:, :], bank[:, b0:b0 + 2, :].rearrange("p a k -> p (a k)"), ACT.Exp))

    def weigh(four, i, g):
        n, j = four * 4 + i, i % 2
        p_made.wait(pe, n, g + 1)
        if g == 0:
            vs_copied.wait(pe, n)
            oT_copied.wait(pe, n - 1)
        for c in range(4):
            ins_ = pe.matmul(bank[32 * c:32 * c + 32, 6, 0:S], vs[j][:, 4 * g + c, :], pT[g % 2][:, c * S:(c + 1) * S],
                             start=(g == 0), stop=(g == 7))
        pv_made.inc(ins_)

    def sum_out(four, i):
        n = four * 4 + i
        pv_made.wait(act, n)
        o_made.wait(act, n - 1)
        oT_copied.inc(act.copy(oT[:, :], bank[:, 6, 0:S]))

    def add_quarters(four, i):
        n = four * 4 + i
        oT_copied.wait(pe, n)
        o_done.wait(pe, n - 1)
        for qt in range(2):
            ins_ = pe.matmul(bank[:, 7, qt * 32:qt * 32 + VW], oT[:, qt * P:(qt + 1) * P], fold[:, :], start=True, stop=True)
        o_made.inc(ins_)

    def divide(four, i):
        n = four * 4 + i
        o_made.wait(dve, n)
        o_done.inc(dve.reciprocal(rden[:, :], bank[:, 7, 0:64].rearrange("p (a k) -> p a k", a=2)[:, :, D0]))
        o_done.wait(dve, n, 1)
        for qt in range(2):
            ins_ = dve.tensor_scalar(ao[:, bass.ds(n, 1), qt, :].rearrange("p a d -> p (a d)"),
                                     bank[:, 7, qt * 32:qt * 32 + D0], rden[:, qt:qt + 1], None, ALU.mult)
        o_done.inc(ins_)

    LEAD = 2

    def attend(four, i, before, nxt, after_nxt):
        for g in range(8):
            slots = []
            for u in (2 * g, 2 * g + 1):
                m = nxt if u + 2 * LEAD < 16 else after_nxt
                slots.append((*m, (u + 2 * LEAD) % 16) if m else None)
            if g == 8 - LEAD and nxt:
                max_rows_step(*nxt, 0)
            if slots[0]:
                max_chunk(*slots[0])
            if g == 7 and nxt:
                max_rows(*nxt)
            if g == 8 - LEAD and nxt:
                max_rows_step(*nxt, 1)
                max_rows_step(*nxt, 2)
            scores(four, i, g)
            if g == 1 and before:
                add_quarters(*before)
            if slots[1]:
                max_chunk(*slots[1])
            if g == 8 - LEAD and nxt:
                max_rows_step(*nxt, 3)
                max_rows_step(*nxt, 4)
                max_rows_step(*nxt, 5)
            if g == 0 and before:
                weigh(*before, 7)
                sum_out(*before)
            if g == 1 and before:
                divide(*before)
            if g == 1 and nxt:
                values(*nxt)
            if g:
                weigh(four, i, g - 1)

    for i in range(4):
        load_queries(0, i)
        load_keys(0, i)
        if i < 1:
            values(0, i)
    for u in range(16):
        max_chunk(0, 0, u)
    for k in range(6):
        max_rows_step(0, 0, k)
    max_rows(0, 0)
    for u in range(2 * LEAD):
        max_chunk(0, 1, u)

    def place(four, i):
        return (four + i // 4, i % 4)

    def steps_of(four, first=False):
        for i in range(4):
            last = four == NH // 4 - 1 if isinstance(four, int) else False
            attend(four, i, place(four, i - 1) if not (first and i == 0) else None,
                   place(four, i + 1) if not (last and i > 2) else None,
                   place(four, i + 2) if not (last and i > 1) else None)
            if not last and i:
                load_queries(four + 1, i - 1)
                load_keys(four + 1, i - 1)

    PE.after(t_kones)
    steps_of(0, first=True)
    with nc.Fori(1, NH // 4 - 1, 1) as four:
        load_queries(four, 3)
        load_keys(four, 3)
        steps_of(four)
    four = NH // 4 - 1
    load_queries(four, 3)
    load_keys(four, 3)
    steps_of(four)
    weigh(four, 3, 7)
    sum_out(four, 3)
    add_quarters(four, 3)
    divide(four, 3)
    o_done.wait(pe, NH - 1)
    o_done.wait(dve, NH - 1)

    wo = pT[1][:, 0:2 * D].rearrange("p (k n) -> p k n", k=2)
    bo = pT[1][0:1, 2 * D:3 * D]
    pv_made.wait(sp, NH - 1)
    t_wo = load("ld_wo", [(wo, ins["L0_xattn_Wo"].rearrange("(k p) n -> p k n", p=P)), (bo, row("L0_xattn_bo"))])
    aoc = pT[0][:, :].rearrange("p (t d) -> p t d", t=NT)
    for i in range(NT):
        b, qt = i // 2, i % 2
        t = DV.done(dve.tensor_copy(aoc[:, i, :].rearrange("p (h d) -> p h d", h=H0), ao[:, b * H0:(b + 1) * H0, qt, :]))
    t_aoT = features_on_partitions(xT, lambda i, kt: aoc[:, i, kt * P:(kt + 1) * P], [t], [])

    def project_tokens(srcT, w, bias, after, first_bank=2, width=D):
        PE.after(*after)
        toks = []
        for i in range(NT):
            for kt in range(2):
                t = pe.matmul(bank[:, first_bank + i, 0:width], srcT[:, kt, i * P:(i + 1) * P], w[:, kt, :],
                              start=(kt == 0), stop=(kt == 1 and bias is None))
            if bias is not None:
                t = pe.matmul(bank[:, first_bank + i, 0:width], ones[0:1, 0:P], bias, start=False, stop=True)
            toks.append(PE.done(t))
        return toks

    def add_to_x(toks, first_bank=2):
        for i in range(NT):
            DV.after(toks[i])
            t = DV.done(dve.tensor_tensor(x[:, i, :], bank[:, first_bank + i, 0:D], x[:, i, :], ALU.add))
        return t

    t_x1 = add_to_x(project_tokens(xT, wo, bo, [t_wo, t_aoT]))
    phase_ends()
    phase_ends()

    HA, DA = 8, 32
    phase_begins()
    t_xn = layer_norm(xn, x, [t_x1])
    t_xT = features_on_partitions(xT, lambda i, kt: xn[:, i, kt * P:(kt + 1) * P], [t_xn], [])
    lowV = {c: sb(f"lowV{c}", [P, 2, P]) for c in "qkv"}
    lowU = {c: sb(f"lowU{c}", [P, 2, P]) for c in "qkv"}
    lowb = sb("lowb", [P, 3, 2])
    lowbv = sb("lowbv", [1, D])
    raw = sb("raw", [P, 2, 2, P])
    pairs = [(lowbv[:, :], ins["L0_attn_bv"].rearrange("h d -> (h d)").rearrange("(a n) -> a n", a=1))]
    for k, c in enumerate("qkv"):
        t = PO.done(pool.memset(lowV[c][:, :, :], 0.0))
        t = PO.done(pool.memset(lowU[c][:, :, :], 0.0))
    sp.wait_ge(*t)
    ld = Load(nc, "ld_lowrank")
    with nc.allow_non_contiguous_dma(reason="small transposed weights"):
        for dst, src in pairs:
            ld.add(sp.dma_start(dst, src))
        for k, c in enumerate("qkv"):
            for h in range(HA):
                r = slice((h % 4) * DA, (h % 4 + 1) * DA)
                ld.add(sp.dma_start(lowV[c][r, h // 4, r], ins["L0_attn_V" + c][h, :, :].rearrange("r d -> d r")))
                ld.add(sp.dma_start(lowU[c][r, h // 4, r], ins["L0_attn_U" + c][h, :, :].rearrange("d r -> r d")))
            for m in range(2):
                ld.add(sp.dma_start(lowb[:, k, m:m + 1], ins["L0_attn_b" + c][4 * m:4 * m + 4, :].rearrange("h (d a) -> (h d) a", a=1)))
    t_low = ld.token()
    lowT = sb("lowT", [P, 2, T])
    qk = {c: sb(f"low_{c}", [P, 2, T]) for c in "qk"}
    vA = sb("vA", [P, NT, HA, DA + 1])
    t_vo = PO.done(pool.memset(vA[:, :, :, DA:DA + 1], 1.0))
    free = [t_xT, t_x1]
    for k, c in enumerate("qkv"):
        for m in range(2):
            PE.after(t_low, t_xT, *free)
            t = PE.done(pe.matmul(bank[:, 2 + m, :], lowV[c][:, m, :], xT[:, m, :], start=True, stop=True))
            AC.after(t, *free)
            t_l = AC.done(act.copy(lowT[:, m, :], bank[:, 2 + m, :]))
            PE.after(t_l)
            if c != "v":
                t = PE.done(pe.matmul(bank[:, 4 + m, :], lowU[c][:, m, :], lowT[:, m, :], start=True, stop=True))
                DV.after(t)
                t = DV.done(dve.tensor_scalar(qk[c][:, m, :], bank[:, 4 + m, :], lowb[:, k, m:m + 1],
                                              float(DA) ** -0.5 if c == "q" else 1.0, ALU.add, ALU.mult))
                free = [t]
        if c == "v":
            for i in range(NT):
                b, h = 6 + i // 2, (i % 2) * D
                for m in range(2):
                    o = bank[:, b, h + m * P:h + (m + 1) * P]
                    pe.matmul(o, lowT[:, m, i * P:(i + 1) * P], lowU[c][:, m, :], start=True, stop=False)
                    t = PE.done(pe.matmul(o, ones[0:1, 0:P], lowbv[:, m * P:(m + 1) * P], start=False, stop=True))
            AC.after(t, t_vo)
            for i in range(NT):
                b, h = 6 + i // 2, (i % 2) * D
                t_v = AC.done(act.copy(vA[:, i, :, 0:DA], bank[:, b, h:h + D].rearrange("p (h d) -> p h d", h=HA)))
    sA = sb("sA", [P, HA, S])
    sAT = sb("sAT", [P, HA, 2, P])
    mA = sb("mA", [P, HA])
    oA = sb("oA", [P, NT, HA, DA])
    rA = sb("rA", [P, HA])

    def low_scores(i, after):
        PE.after(*after)
        for h in range(HA):
            r = slice((h % 4) * DA, (h % 4 + 1) * DA)
            t = pe.matmul(bank[:, h % 4, (h // 4) * S:(h // 4 + 1) * S], qk["q"][r, h // 4, i * P:(i + 1) * P],
                          qk["k"][r, h // 4, i // 2 * S:(i // 2 + 1) * S], start=True, stop=True)
        return PE.done(t)

    def low_exps(t, turned):
        DV.after(t, *turned)
        t = DV.done(dve.tensor_reduce(mA[:, :], bank[:, 0:4, :].rearrange("p c (a k) -> p a c k", a=2), AX.X, ALU.max, negate=True))
        AC.after(t, *turned)
        for h in range(HA):
            t = AC.done(act.activation(sA[:, h, :], bank[:, h % 4, (h // 4) * S:(h // 4 + 1) * S], ACT.Exp, bias=mA[:, h:h + 1]))
        return t

    t_done = t_v
    t_exp = low_exps(low_scores(0, [free[0], t_v]), [])
    for i in range(NT):
        b = i // 2
        PE.after(t_exp, t_done)
        for h in range(HA):
            for k in range(2):
                t = pe.transpose(bank[:, 4 + h // 2, (h % 2) * S + k * P:(h % 2) * S + (k + 1) * P], sA[:, h, k * P:(k + 1) * P], ident[:, :])
        t = t_turned = PE.done(t)
        if i + 1 < NT:
            t_s = low_scores(i + 1, [])
        DV.after(t)
        t = DV.done(dve.tensor_copy(sAT[:, :, :, :].rearrange("p h k q -> p (h k q)"), bank[:, 4:8, :].rearrange("p a n -> p (a n)")))
        if i + 1 < NT:
            t_exp = low_exps(t_s, [t_turned, t_exp])
        PE.after(t)
        for h in range(HA):
            for k in range(2):
                t = pe.matmul(bank[:, 4, h * 64:h * 64 + DA + 1], sAT[:, h, k, :], vA[:, b * 2 + k, h, :], start=(k == 0), stop=(k == 1))
        t = PE.done(t)
        o = bank[:, 4, :].rearrange("p (h d) -> p h d", h=HA)
        DV.after(t)
        t = DV.done(dve.reciprocal(rA[:, :], o[:, :, DA]))
        DV.after(t)
        for h in range(HA):
            t_done = DV.done(dve.tensor_scalar(oA[:, i, h, :], o[:, h, 0:DA], rA[:, h:h + 1], None, ALU.mult))
        DV.after(t_done)
        t_x2 = DV.done(dve.tensor_tensor(x[:, i, :], x[:, i, :], oA[:, i, :, :].rearrange("p h d -> p (h d)"), ALU.add))
    phase_ends()

    NE, FI, TOP = 16, 128, 4
    phase_begins()
    w13 = [sb(f"w13_{i}", [P, 2, 2, FI]) for i in range(4)]
    w2e = [sb(f"w2e_{i}", [P, D]) for i in range(4)]
    w_in = [Count(nc, f"w_in{i}", 48) for i in range(4)]
    y_made = Count(nc, "y_made", 1, 4)
    y_made.give(pe)
    w1_d, w3_d, w2_d = ins["L0_ffn_w1"], ins["L0_ffn_w3"], ins["L0_ffn_w2"]
    gwr = sb("gwr", [NE, D])
    gwT = sb("gwT", [P, 2, NE])
    t_g = load("ld_gate", [(gwr[:, :], ins["L0_ffn_gate_w"])])

    def load_expert(four, i):
        e = four * 4 + i
        y_made.wait(sp, e - 4)
        for k, w in enumerate((w1_d, w3_d)):
            sp.dma_start(w13[i][:, k, :, :], w[bass.ds(e, 1), :, :].rearrange("a (k p) i -> p (a k) i", p=P)).then_inc(w_in[i].sem, 16)
        sp.dma_start(w2e[i][:, :], w2_d[bass.ds(e, 1), :, :].rearrange("a i h -> (a i) h")).then_inc(w_in[i].sem, 16)

    for i in range(4):
        load_expert(0, i)
    t_xn = layer_norm(xn, x, [t_x2])
    t_xT = features_on_partitions(xT, lambda i, kt: xn[:, i, kt * P:(kt + 1) * P], [t_xn], [])
    PE.after(t_g, t_xT)
    for kt in range(2):
        t = PE.done(pe.transpose(bank[:, 2, kt * NE:(kt + 1) * NE], gwr[:, kt * P:(kt + 1) * P], ident[0:NE, 0:NE]))
    DV.after(t)
    t = DV.done(dve.tensor_copy(gwT[:, :, :].rearrange("p a b -> p (a b)"), bank[:, 2, 0:2 * NE]))
    PE.after(t)
    for i in range(NT):
        for kt in range(2):
            t = pe.matmul(bank[:, 3, i * NE:(i + 1) * NE], xT[:, kt, i * P:(i + 1) * P], gwT[:, kt, :], start=(kt == 0), stop=(kt == 1))
    t = PE.done(t)
    PAD = 4
    lg = sb("lg", [P, NT, NE])
    best = sb("best", [P, NT, 8])
    prob = sb("prob", [P, NT, NE + PAD])
    rest = sb("rest", [P, NT, NE + PAD])
    score = sb("score", [P, NT, NE])
    nm = sb("nm", [P, NT])
    den = sb("den", [P, NT])
    DV.after(t)
    t = DV.done(dve.tensor_copy(lg[:, :, :].rearrange("p a b -> p (a b)"), bank[:, 3, 0:NT * NE]))
    DV.after(t)
    t = DV.done(dve.tensor_reduce(nm[:, :], lg[:, :, :], AX.X, ALU.max, negate=True))
    AC.after(t)
    for i in range(NT):
        t = AC.done(act.activation(prob[:, i, 0:NE], lg[:, i, :], ACT.Exp, bias=nm[:, i:i + 1], accum_out=den[:, i:i + 1]))
    DV.after(t)
    for k in range(PAD):
        t = DV.done(dve.memset(prob[:, :, NE + k:NE + k + 1], -1.0 - k))
    t = DV.done(dve.reciprocal(den[:, :], den[:, :]))
    DV.after(t)
    for i in range(NT):
        t = DV.done(dve.tensor_scalar(prob[:, i, 0:NE], prob[:, i, 0:NE], den[:, i:i + 1], None, ALU.mult))
    DV.after(t)
    for i in range(NT):
        t = DV.done(dve.max(best[:, i, :], prob[:, i, :]))
    DV.after(t)
    for k in range(PAD):
        t = DV.done(dve.memset(best[:, :, TOP + k:TOP + k + 1], -1.0 - k))
    DV.after(t)
    for i in range(NT):
        t = DV.done(dve.match_replace(rest[:, i, :], best[:, i, :], prob[:, i, :], 0.0))
    t = DV.done(dve.tensor_reduce(den[:, :], best[:, :, 0:TOP], AX.X, ALU.add))
    DV.after(t)
    t = DV.done(dve.reciprocal(den[:, :], den[:, :]))
    t = DV.done(dve.tensor_tensor(score[:, :, :], prob[:, :, 0:NE], rest[:, :, 0:NE], ALU.subtract))
    DV.after(t)
    for i in range(NT):
        t_score = DV.done(dve.tensor_scalar(score[:, i, :], score[:, i, :], den[:, i:i + 1], None, ALU.mult))

    gate = [sb(f"gate{j}", [P, T]) for j in range(2)]
    hid = [sb(f"hid{j}", [P, T]) for j in range(2)]
    sce = [sb(f"sce{j}", [P, NT]) for j in range(2)]
    gu_made = Count(nc, "gu_made", 1)
    gate_done = Count(nc, "gate_done", 1)
    hid_done = Count(nc, "hid_done", 2, 2)
    y_added = Count(nc, "y_added", NT, 2)
    for c, e in ((hid_done, dve), (y_added, dve)):
        c.give(e)
    PE.after(t_xT, t_score)
    DV.after(t_score)
    def expert_up(four, i):
        e, j = four * 4 + i, i % 2
        w_in[i].wait(pe, four)
        hid_done.wait(pe, e - 2, 1)
        for k in range(2):
            for kt in range(2):
                ins_ = pe.matmul(bank[:, 2 * j + k, :], w13[i][:, k, kt, :], xT[:, kt, :], start=(kt == 0), stop=(kt == 1))
        gu_made.inc(ins_)
        gu_made.wait(act, e)
        gate_done.inc(act.activation(gate[j][:, :], bank[:, 2 * j, :], ACT.Silu))
        gate_done.wait(dve, e)
        y_made.wait(dve, e - 2)
        hid_done.inc(dve.tensor_tensor(hid[j][:, :], bank[:, 2 * j + 1, :], gate[j][:, :], ALU.mult))
        y_added.wait(dve, e - 2)
        hid_done.inc(dve.tensor_scalar(sce[j][:, :], score[:, :, bass.ds(e, 1)].rearrange("p t a -> p (t a)"), 1.0, None, ALU.mult))

    def expert_down(four, i):
        e, j = four * 4 + i, i % 2
        hid_done.wait(pe, e)
        y_added.wait(pe, e - 2)
        for t_ in range(NT):
            ins_ = pe.matmul(bank[:, 4 + 2 * j + t_ // 2, (t_ % 2) * D:(t_ % 2 + 1) * D], hid[j][:, t_ * P:(t_ + 1) * P], w2e[i][:, :],
                             start=True, stop=True)
        y_made.inc(ins_)
        y_made.wait(dve, e)
        y_added.wait(dve, e - 1)
        for i in range(NT):
            y_added.inc(dve.scalar_tensor_tensor(x[:, i, :], bank[:, 4 + 2 * j + i // 2, (i % 2) * D:(i % 2 + 1) * D],
                                                 sce[j][:, i:i + 1], x[:, i, :], ALU.mult, ALU.add))

    expert_up(0, 0)
    with nc.Fori(0, NE // 4 - 1, 1) as four:
        for i in range(4):
            expert_up(four + (i + 1) // 4, (i + 1) % 4)
            expert_down(four, i)
            load_expert(four + 1, i)
    for i in range(4):
        if i < 3:
            expert_up(NE // 4 - 1, i + 1)
        expert_down(NE // 4 - 1, i)
    y_added.wait(dve, NE - 1)
    y_added.wait(act, NE - 1)
    y_added.wait(pe, NE - 1)
    t_x3 = DV.done(dve.tensor_copy(nm[:, 0:1], nm[:, 0:1]))
    phase_ends()

    H1, D1, KTOP = 4, 32, 32
    DCM = DC - P
    phase_begins()
    xt = sb("xt", [P, NT, D])
    xh = sb("xh", [P, NT, D])
    c0T = [sb("c0T1", [P, T]), sb("c0T2", [DCM, T])]
    tabs = sb("tabs", [P, 4, 2, S])
    KT = sb("KT", [P, 2, D])
    Kf = sb("Kf", [P, 2, 2, D])
    phase_begins()
    wq1 = sb("wq1", [P, 2, P])
    m8 = sb("m8", [NB, S2], mybir.dt.uint8)
    t_w = load("ld_wq1", [(wq1[:, :, :], ins["L1_xattn_Wq"].rearrange("(k p) n -> p k n", p=P))])
    t_m = load("ld_mask", [(m8[:, :], ins["mask_BxS2_bf1"])])
    t_tab = load("ld_tab", [(tabs[:, k, :, :], ins["dft"][k].rearrange("(t p) n -> p t n", p=P)) for k in range(4)])
    t_xt = layer_norm(xt, x, [t_x3])
    t_xT = features_on_partitions(xT, lambda i, kt: xt[:, i, kt * P:(kt + 1) * P], [t_xt], [])
    layer_norm(xh, xt, [t_xt])

    q1f, q1r, q1p = sb("q1f", [P, T]), sb("q1r", [P, T]), sb("q1p", [P, 3, T], BF16)
    q1_parts_d = nc.dram_tensor("q1_parts_d", [NB * P, 3, S], BF16).ap()
    PE.after(t_w, t_xT)
    for kt in range(2):
        t = pe.matmul(bank[:, 2, :], wq1[:, kt, :], xT[:, kt, :], start=(kt == 0), stop=(kt == 1))
    t = PE.done(t)
    DV.after(t)
    t = DV.done(dve.tensor_scalar(q1f[:, :], bank[:, 2, :], 1.0 / math.sqrt(D1), None, ALU.mult))
    t = three_parts(lambda k: q1p[:, k, :], q1f[:, :], q1r[:, :], [t])
    sp.wait_ge(*t)
    ld_q1 = Load(nc, "st_q1")
    for b in range(NB):
        ld_q1.add(sp.dma_start(q1_parts_d[b * P:(b + 1) * P, :, :], q1p[:, :, b * S:(b + 1) * S]))
    mrow = sb("mrow", [NB, S2], BF16)
    mask_d = nc.dram_tensor("mask_d", [NB, S2], BF16).ap()
    DV.after(t_m)
    t = DV.done(dve.tensor_scalar(mrow[:, :], m8[:, :], 1e30, -1e30, ALU.mult, ALU.add))
    sp.wait_ge(*t)
    ld_q1.add(sp.dma_start(mask_d, mrow[:, :]))
    kst = sb("kst", [P, LA, 2, 32])
    PE.after(t_pow, t_xT)
    for t_ in range(2):
        hs = slice(t_ * NSTATE, (t_ + 1) * NSTATE)
        for g in range(32):
            c0 = (t_ * 32 + g) * LA
            for c in range(2):
                for q in range(4):
                    t = pe.matmul(bank[32 * q:32 * q + LB, 4 + c0 // 512, c0 % 512:c0 % 512 + LA],
                                  Bp[c][hs, q, :, g], Ap[c][hs, q, :, g], start=(c == 0), stop=(c == 1))
    t = PE.done(t)
    AC.after(t)
    DV.after(t)
    kp = bank[:, 4:8, :].rearrange("p c n -> p (c n)").rearrange("p (t g a) -> p t g a", t=2, g=32)
    for q in range(4):
        rows = slice(32 * q, 32 * q + LB)
        for t_ in range(2):
            dst, src = kst[rows, :, t_, :].rearrange("p a g -> p g a"), kp[rows, t_, :, :]
            if t_:
                t2 = DV.done(dve.tensor_copy(dst, src))
            else:
                t = AC.done(act.copy(dst, src))
    sp.wait_ge(*ld_q1.token())
    K_d = nc.dram_tensor("K_d", [S, D], F32).ap()
    sp.wait_ge(*t)
    sp.wait_ge(*t2)
    ld = Load(nc, "st_K")
    for q in range(4):
        for t_ in range(2):
            at = t_ * P + q * 32
            ld.add(sp.dma_start(K_d.rearrange("(a b) d -> b a d", b=LB)[:, :, at:at + 32], kst[32 * q:32 * q + LB, :, t_, :]))
    sp.wait_ge(*ld.token())
    t_KT = load("ld_KT", [(KT[:, :, :], K_d.rearrange("(t p) d -> p t d", p=P))])

    PE.after(t_KT, t_tab)
    for c in range(2):
        for ft in range(2):
            for lt in range(2):
                t = pe.matmul(bank[:, 4 + c, ft * D:(ft + 1) * D], tabs[:, c, lt, ft * P:(ft + 1) * P], KT[:, lt, :],
                              start=(lt == 0), stop=(lt == 1))
        t = PE.done(t)
        AC.after(t)
        t_Kf = AC.done(act.copy(Kf[:, c, :, :].rearrange("p f d -> p (f d)"), bank[:, 4 + c, :]))
    phase_ends()

    phase_begins()
    NS1 = 3 * D1
    NM = NB * H1
    k1s = [sb(f"k1s{g}", [NS1 + 1, S2], BF16) for g in range(2)]
    q1s = [sb(f"q1s{g}", [NS1 + 1, S], BF16) for g in range(2)]
    GC = 128
    NG = S2 // GC
    Sc = [sb(f"Sc{j}", [P, S2]) for j in range(2)]
    Ex = [sb(f"Ex{j}", [P, S2]) for j in range(2)]
    amean = sb("amean", [P, 2, S2])
    cand = sb("cand", [P, NG, 8])
    cleft = sb("cleft", [P, NG * 8])
    top = [sb(f"top{j}", [P, KTOP]) for j in range(2)]
    rest8 = sb("rest8", [P, 8])
    worst = sb("worst", [P, 1])
    flag = sb("flag", [P, 1])
    flags = [sb(f"flags{j}", [1, 1], I32) for j in range(2)]
    thr = [sb(f"thr{j}", [P, 1]) for j in range(2)]
    ntop = [sb(f"ntop{j}", [P, 1]) for j in range(2)]
    etop = sb("etop", [P, KTOP])
    ssum = [sb(f"ssum{j}", [P, 1]) for j in range(2)]
    aT = [sb(f"aT{j}", [P, 4, P]) for j in range(2)]
    c0 = sb("c0", [P, NT, DC])
    for g in range(2):
        t_o = DV.done(dve.memset(q1s[g][NS1:NS1 + 1, :], 1.0 if g == 0 else 0.0))
        t_o = DV.done(dve.memset(k1s[g][NS1:NS1 + 1, :], 0.0))
    t_zero = PO.done(pool.memset(amean[:, :, :], 0.0))
    NSEL, NEX = 15, 10
    stack1_in = Count(nc, "stack1_in", 16 * 13)
    s_made = Count(nc, "s_made", 4)
    s_copied = Count(nc, "s_copied", 4, 1)
    ex_made = Count(nc, "ex_made", 1)
    sel = Count(nc, "sel", NSEL, 1)
    flag_summed = Count(nc, "flag_summed", 1)
    flag_in = Count(nc, "flag_in", 1, 1)
    exact = Count(nc, "exact", NEX)
    sum_made = Count(nc, "sum_made", 1)
    fin = Count(nc, "fin", 3, 2)
    scaled = Count(nc, "scaled", 1, 2)
    added = Count(nc, "added", 1, 2)
    for c, e in ((s_copied, act), (sel, dve), (flag_in, dve), (fin, dve), (scaled, act), (added, pool)):
        c.give(e)
    PE.after(t_Kf, t_o)
    PO.after(t_zero)
    sp.wait_ge(*t_o)
    GROUPS = (((0, 0), (0, 1), (1, 0)), ((0, 2), (2, 0), (1, 1)))

    def stack1(b, h):
        r = b * H1 * 2 + h * 2
        if not (b == 0 and isinstance(h, int) and h == 0):
            s_made.wait(sp, r - 1)
        kd = k1_parts_d[bass.ds(h * D1 + b * P, D1), :, :]
        qd = q1_parts_d[bass.ds(h * D1 + b * P, D1), :, :]
        for g in range(2):
            for s, (kp, qp) in enumerate(GROUPS[g]):
                sp.dma_start(k1s[g][s * D1:(s + 1) * D1, :], kd[:, kp, :]).then_inc(stack1_in.sem, 16)
                sp.dma_start(q1s[g][s * D1:(s + 1) * D1, :], qd[:, qp, :]).then_inc(stack1_in.sem, 16)
        sp.dma_start(k1s[0][NS1:NS1 + 1, :], mask_d[b:b + 1, :]).then_inc(stack1_in.sem, 16)

    def tile_no(b, h, qt):
        return (h + b * H1) * 2 + qt

    def score(b, h, qt):
        r, j = tile_no(b, h, qt), qt
        if qt == 0:
            stack1_in.wait(pe, h + b * H1)
        for k in range(4):
            s_copied.wait(pe, r if k >= 2 else r - 1, k - 1 if k >= 2 else k + 3)
            b0 = 2 * (k % 2)
            for c in range(2):
                k0 = (2 * k + c) * 512
                for g in range(2):
                    ins_ = pe.matmul(bank[:, b0 + c, :], q1s[g][:, qt * P:(qt + 1) * P], k1s[g][:, k0:k0 + 512],
                                     start=(g == 0), stop=(g == 1))
            s_made.inc(ins_)
            s_made.wait(act, r, k + 1)
            fin.wait(act, r - 2, 1)
            s_copied.inc(act.copy(Sc[j][:, k * 1024:(k + 1) * 1024], bank[:, b0:b0 + 2, :].rearrange("p c n -> p (c n)")))

    def take8(n, k, dst, src, left, count, wait0):
        count.wait(dve, n, wait0)
        hold(dve)
        count.inc(dve.max(dst, src))
        count.wait(dve, n, wait0 + 1)
        hold(dve)
        count.inc(dve.match_replace(left, dst, src, -3e38))

    def select(b, h, qt):
        r, j = tile_no(b, h, qt), qt
        flat = cand[:, :, :].rearrange("p g k -> p (g k)")
        sel.wait(dve, r - 1)
        fin.wait(dve, r - 2, 3)
        for k in range(4):
            s_copied.wait(dve, r, k + 1)
            hold(dve)
            for g in range(NG // 4 * k, NG // 4 * (k + 1)):
                ins_ = dve.max(cand[:, g, :], Sc[j][:, g * GC:(g + 1) * GC])
        sel.inc(ins_)
        take8(r, 0, top[j][:, 0:8], flat, cleft[:, :], sel, 1)
        sel.inc(dve.tensor_scalar(ntop[j][:, :], top[j][:, 0:1], -1.0, None, ALU.mult))
        sel.wait(act, r, 4)
        added.wait(act, r - 2)
        ex_made.inc(act.activation(Ex[j][:, :], Sc[j][:, :], ACT.Exp, bias=ntop[j][:, :]))

    def select_rest(b, h, qt):
        r, j = tile_no(b, h, qt), qt
        for k in range(1, KTOP // 8):
            take8(r, k, top[j][:, 8 * k:8 * k + 8], cleft[:, :], cleft[:, :], sel, 2 * k + 2)
        sel.inc(dve.tensor_reduce(worst[:, :], cand[:, :, 7], AX.X, ALU.max))
        sel.wait(dve, r, 11)
        hold(dve)
        sel.inc(dve.max(rest8[:, :], cleft[:, :]))
        sel.inc(dve.tensor_copy(thr[j][:, :], top[j][:, KTOP - 1:KTOP]))
        sel.wait(dve, r, 13)
        sel.inc(dve.tensor_tensor(worst[:, :], worst[:, :], rest8[:, 0:1], ALU.max))
        sel.wait(dve, r, 14)
        flag_in.wait(dve, r - 1)
        sel.inc(dve.tensor_scalar(flag[:, :], worst[:, :], thr[j][:, 0:1], None, ALU.is_ge))
        sel.wait(pe, r)
        flag_in.wait(pe, r - 1)
        flag_summed.inc(pe.matmul(bank[0:1, 6, 0:1], flag[:, :], ones[:, 0:1], start=True, stop=True))

    def flag_to_sbuf(b, h, qt):
        r = tile_no(b, h, qt)
        flag_summed.wait(dve, r)
        flag_in.inc(dve.tensor_copy(flags[qt][:, :], bank[0:1, 6, 0:1]))

    flagged = dve.alloc_register("flagged")

    def keep_best(b, h, qt):
        r, j = tile_no(b, h, qt), qt
        flag_in.wait(dve, r)
        ex_made.wait(dve, r)
        hold(dve)
        dve.reg_load(flagged, flags[j][0:1, 0:1])
        with dve.If_ne(flagged, 0):
            for k in range(KTOP // 8):
                take8(r, k, top[j][:, 8 * k:8 * k + 8], Sc[j][:, :], Sc[j][:, :], exact, 2 * k)
            exact.wait(dve, r, 8)
            exact.inc(dve.tensor_scalar(Sc[j][:, :], Sc[j][:, :], -3e38, 2.0, ALU.is_equal, ALU.mult))
            exact.inc(dve.memset(thr[j][:, :], 1.0))
        with dve.If_eq(flagged, 0):
            dve.sem_inc(exact.sem, NEX)
        exact.wait(dve, r)
        fin.inc(dve.scalar_tensor_tensor(Ex[j][:, :], Sc[j][:, :], thr[j][:, 0:1], Ex[j][:, :], ALU.is_ge, ALU.mult))
        exact.wait(act, r)
        scaled.wait(act, r - 2)
        fin.wait(act, r - 1, 2)
        sum_made.inc(act.activation(etop[:, :], top[j][:, :], ACT.Exp, bias=ntop[j][:, :], accum_out=ssum[j][:, :]))

    def share(b, h, qt):
        r, j = tile_no(b, h, qt), qt
        sum_made.wait(dve, r)
        fin.inc(dve.tensor_scalar(ssum[j][:, :], ssum[j][:, :], float(H1), None, ALU.mult))
        fin.wait(dve, r, 2)
        fin.inc(dve.reciprocal(ssum[j][:, :], ssum[j][:, :]))

    def add_to_mean(b, h, qt):
        r, j = tile_no(b, h, qt), qt
        fin.wait(act, r, 3)
        hold(act)
        scaled.inc(act.activation(Ex[j][:, :], Ex[j][:, :], ACT.Copy, scale=ssum[j][:, 0:1]))
        scaled.wait(pool, r)
        added.wait(pool, r - 1)
        hold(pool)
        added.inc(pool.tensor_tensor(amean[:, qt, :], amean[:, qt, :], Ex[j][:, :], ALU.add))

    def tile_step(b, h, qt, first=False, last=False):
        before = (b, h, 0) if qt else (b, h - 1, 1)
        select(b, h, qt)
        if not first:
            keep_best(*before)
        select_rest(b, h, qt)
        if not first:
            share(*before)
        flag_to_sbuf(b, h, qt)
        if not last:
            score(b, *((h + 1, 0) if qt else (h, 1)))
        if not first:
            add_to_mean(*before)

    used = [[], []]
    ctxn_d = ins["ctx_768"].rearrange("b (c p) d -> b p c d", p=P)
    for b in range(NB):
        ldc = [Load(nc, f"ld_cn{b}{j}") for j in range(2)]
        HC = NCH // 2
        cn = [Sc[j][:, 0:HC * DC].rearrange("p (c d) -> p c d", c=HC) for j in range(2)]

        def load_context(j):
            fin.wait(sp, 2 * H1 * b + 2 * H1 - 2 + j, 1)
            ldc[j].add(sp.dma_start(cn[j], ctxn_d[b][:, j * HC:(j + 1) * HC, :]))

        if b == 0:
            stack1(0, 0)
        score(b, 0, 0)
        tile_step(b, 0, 0, first=True)
        stack1(b, 1)
        tile_step(b, 0, 1)
        with nc.Fori(1, H1 - 1, 1) as h:
            tile_step(b, h, 0)
            stack1(b, h + 1)
            tile_step(b, h, 1)
        tile_step(b, H1 - 1, 0)
        tile_step(b, H1 - 1, 1, last=True)
        load_context(0)
        if b < NB - 1:
            stack1(b + 1, 0)
        keep_best(b, H1 - 1, 1)
        share(b, H1 - 1, 1)
        add_to_mean(b, H1 - 1, 1)
        load_context(1)
        added.wait(pe, 2 * H1 * (b + 1) - 1)
        added.wait(dve, 2 * H1 * (b + 1) - 1)
        NGR = NCH // 4

        def turn_group(n):
            qt, g, j = n // NGR, n % NGR, n % 2
            PE.after(*copied[j])
            for c in range(4):
                k0 = (4 * g + c) * P
                t = pe.transpose(bank[:, j, c * P:(c + 1) * P], amean[:, qt, k0:k0 + P], ident[:, :])
            AC.after(PE.done(t), *used[j])
            copied[j] = [AC.done(act.copy(aT[j][:, :, :].rearrange("p c q -> p (c q)"), bank[:, j, :]))]

        copied = [[], []]
        turn_group(0)
        for n in range(2 * NGR):
            qt, g, j = n // NGR, n % NGR, n % 2
            if n + 1 < 2 * NGR:
                turn_group(n + 1)
            PE.after(*copied[j], ldc[4 * g // HC].token())
            for c in range(4):
                t = pe.matmul(bank[:, 2 + qt, 0:DC], aT[j][:, c, :], cn[4 * g // HC][:, (4 * g + c) % HC, :], start=(g == 0 and c == 0),
                              stop=(g == NGR - 1 and c == 3))
            used[j] = [PE.done(t)]
            if g == NGR - 1:
                DV.after(*used[j])
                t_c0 = DV.done(dve.tensor_copy(c0[:, b * 2 + qt, :], bank[:, 2 + qt, 0:DC]))
        DV.after(*used[0], *used[1])
        PE.after(DV.last())
        act.wait_ge(*DV.last())
        if b < NB - 1:
            PO.after(PE.last(), DV.last())
            t_zero = PO.done(pool.memset(amean[:, :, :], 0.0))
            PO.after(t_zero)
        act.wait_ge(*PE.last())
    tm8 = sb("tm8", [P, NT], mybir.dt.uint8)
    tmask = sb("tmask", [P, NT])
    with nc.allow_non_contiguous_dma(reason="512 mask bytes"):
        t_tm = load("ld_tm", [(tm8[:, :], ins["mask_BxS_bf1"].rearrange("b (t p) -> p (b t)", p=P))])
    DV.after(t_tm, t_c0)
    t = DV.done(dve.tensor_copy(tmask[:, :], tm8[:, :]))
    DV.after(t)
    for i in range(NT):
        t = DV.done(dve.tensor_scalar(c0[:, i, :], c0[:, i, :], tmask[:, i:i + 1], None, ALU.mult))
    PE.after(t)
    for k, (lo, n) in enumerate(((0, P), (P, DCM))):
        for i in range(NT):
            t = PE.done(pe.transpose(bank[0:n, 4 + k, i * P:(i + 1) * P], c0[:, i, lo:lo + n], ident[:, :]))
        AC.after(t)
        t_c0T = AC.done(act.copy(c0T[k][:, :], bank[0:n, 4 + k, :]))
    phase_ends()

    phase_begins()
    wv1, wv2 = sb("wv1", [P, D]), sb("wv2", [DCM, D])
    film = sb("film", [P, 2, 2, 2 * D])
    bfilm = sb("bfilm", [1, 2, 2 * D])
    vecs = sb("vecs", [P, 7, D])
    mgate = sb("mgate", [P, 1])
    NAMES = ("g_norm_in", "b_norm_in", "g_norm_out", "b_norm_out", "g_ffn", "b_ffn", "D_skip")
    pairs = [(wv1[:, :], ins["L1_xattn_Wv"][0:P, :]), (wv2[:, :], ins["L1_xattn_Wv"][P:DC, :]),
             (mgate[:, :], ins["L1_xattn_mod_gate"].rearrange("(a n) -> a n", a=1).to_broadcast([P, 1]))]
    for k, n in enumerate(("in", "out")):
        pairs += [(film[:, k, :, :], ins["L1_xattn_W_film_" + n].rearrange("(k p) n -> p k n", p=P)),
                  (bfilm[:, k, :], row("L1_xattn_b_film_" + n))]
    t_w = load("ld_film", pairs)
    t_vec = load("ld_vecs", [(vecs[:, k, :], row("L1_xattn_" + n).to_broadcast([P, D])) for k, n in enumerate(NAMES)])
    HID = 4 * D
    MT = HID // P
    W1 = sb("W1", [P, 2, HID])
    W2 = sb("W2", [P, MT, D])
    b1 = sb("b1", [P, MT])
    b2 = sb("b2", [1, D])
    pairs = [(W1[:, :, :], ins["L1_xattn_W1"].rearrange("(k p) n -> p k n", p=P)),
              (W2[:, :, :], ins["L1_xattn_W2"].rearrange("(k p) n -> p k n", p=P)), (b2[:, :], row("L1_xattn_b2"))]
    with nc.allow_non_contiguous_dma(reason="1024 bias values"):
        t_ffw = load("ld_ffw", pairs + [(b1[:, :], ins["L1_xattn_b1"].rearrange("(k p) -> p k", p=P))])
    VEC = {n: vecs[:, k, :] for k, n in enumerate(NAMES)}

    def seq(*fns):
        for fn in fns:
            DV.after(DV.last())
            t = DV.done(fn())
        return t

    ctT = sb("ctT", [P, 2, T])
    mod = sb("mod", [P, 2, NT, 2 * D])
    PE.after(t_w, t_c0T)
    for m in range(2):
        pe.matmul(bank[:, m, :], wv1[:, m * P:(m + 1) * P], c0T[0][:, :], start=True, stop=False)
        t = PE.done(pe.matmul(bank[:, m, :], wv2[:, m * P:(m + 1) * P], c0T[1][:, :], start=False, stop=True))
        AC.after(t)
        t_ct = AC.done(act.copy(ctT[:, m, :], bank[:, m, :]))
    AC.after(t_w)
    for k in range(2):
        toks = []
        PE.after(t_ct)
        for i in range(NT):
            if k and i == 0:
                PE.after(t_mod)
            for kt in range(2):
                pe.matmul(bank[:, 4 + i, :], ctT[:, kt, i * P:(i + 1) * P], film[:, k, kt, :], start=(kt == 0), stop=False)
            t = PE.done(pe.matmul(bank[:, 4 + i, :], ones[0:1, 0:P], bfilm[0:1, k, :], start=False, stop=True))
            AC.after(t)
            t_mod = AC.done(act.activation(mod[:, k, i, :], bank[:, 4 + i, :], ACT.Copy, scale=mgate[:, 0:1]))

    def affine(dst, src, g, b, i):
        seq(lambda: dve.tensor_tensor(dst[:, i, :], src[:, i, :], VEC[g], ALU.mult),
            lambda: dve.tensor_tensor(dst[:, i, :], dst[:, i, :], VEC[b], ALU.add))

    def modulate(dst, k, i):
        seq(lambda: dve.scalar_tensor_tensor(dst[:, i, :], mod[:, k, i, 0:D], 1.0, dst[:, i, :], ALU.add, ALU.mult),
            lambda: dve.tensor_tensor(dst[:, i, :], dst[:, i, :], mod[:, k, i, D:2 * D], ALU.add))

    DV.after(t_mod, t_vec)
    for i in range(NT):
        affine(xh, xh, "g_norm_in", "b_norm_in", i)
        modulate(xh, 0, i)
    t_xh = DV.last()
    Xf = sb("Xf", [P, 2, 2, NB, D])
    Yf = sb("Yf", [P, 2, 2, NB, D])
    tmpf = sb("tmpf", [P, NB, D])
    xhv = xh[:, :, :].rearrange("p (b t) d -> p t b d", b=NB)
    PE.after(t_xh, t_tab, t_ct)
    for c in range(2):
        for ft in range(2):
            o = bank[:, c * 2 + ft, :]
            for lt in range(2):
                t = pe.matmul(o, tabs[:, c, lt, ft * P:(ft + 1) * P], xhv[:, lt, :, :], start=(lt == 0), stop=(lt == 1))
            t = PE.done(t)
            AC.after(t)
            t_Xf = AC.done(act.copy(Xf[:, c, ft, :, :].rearrange("p b d -> p (b d)"), o))
    DV.after(t_Xf, t_Kf)
    for ft in range(2):
        kb = [Kf[:, c, ft:ft + 1, :].to_broadcast([P, NB, D]) for c in range(2)]
        Xc, Xs = (Xf[:, c, ft, :, :] for c in range(2))
        for c, (a0, a1, op) in enumerate(((kb[0], kb[1], ALU.subtract), (kb[1], kb[0], ALU.add))):
            seq(lambda: dve.tensor_tensor(Yf[:, c, ft, :, :], Xc, a0, ALU.mult),
                lambda: dve.tensor_tensor(tmpf[:, :, :], Xs, a1, ALU.mult),
                lambda: dve.tensor_tensor(Yf[:, c, ft, :, :], Yf[:, c, ft, :, :], tmpf[:, :, :], op))
    PE.after(DV.last())
    for nt in range(2):
        for n_, (c, ft) in enumerate(((0, 0), (0, 1), (1, 0), (1, 1))):
            t = pe.matmul(bank[:, nt, :], tabs[:, 2 + c, ft, nt * P:(nt + 1) * P], Yf[:, c, ft, :, :].rearrange("p b d -> p (b d)"),
                          start=(n_ == 0), stop=(n_ == 3))
        t = PE.done(t)
    DV.after(t)
    xt2 = sb("xt2", [P, NT, D])
    for i in range(NT):
        b, nt = i // 2, i % 2
        seq(lambda: dve.tensor_tensor(xh[:, i, :], xh[:, i, :], VEC["D_skip"], ALU.mult),
            lambda: dve.tensor_tensor(xh[:, i, :], bank[:, nt, b * D:(b + 1) * D], xh[:, i, :], ALU.add))
        modulate(xh, 1, i)
        seq(lambda: dve.tensor_tensor(xt2[:, i, :], xh[:, i, :], xt[:, i, :], ALU.add))
    layer_norm(xh, xt2, [DV.last()])
    for i in range(NT):
        affine(xh, xh, "g_ffn", "b_ffn", i)
    t_hT = features_on_partitions(xT, lambda i, kt: xh[:, i, kt * P:(kt + 1) * P], [DV.last()], [], banks=(2, 3))
    ffh = sb("ffh", [P, MT, T])
    PE.after(t_hT, t_ffw)
    AC.after(t_ffw)
    used = [None] * 2
    for m in range(MT):
        j = m % 2
        if used[j]:
            PE.after(used[j])
        for kt in range(2):
            t = pe.matmul(bank[:, 2 + j, :], W1[:, kt, m * P:(m + 1) * P], xT[:, kt, :], start=(kt == 0), stop=(kt == 1))
        t = PE.done(t)
        AC.after(t)
        used[j] = t_h = AC.done(act.activation(ffh[:, m, :], bank[:, 2 + j, :], ACT.Gelu, bias=b1[:, m:m + 1]))
    PE.after(t_h)
    for i in range(NT):
        for m in range(MT):
            pe.matmul(bank[:, 4 + i, 0:D], ffh[:, m, i * P:(i + 1) * P], W2[:, m, :], start=(m == 0), stop=False)
        t = PE.done(pe.matmul(bank[:, 4 + i, 0:D], ones[0:1, 0:P], b2[0:1, :], start=False, stop=True))
        DV.after(t)
        t = DV.done(dve.tensor_tensor(xt2[:, i, :], bank[:, 4 + i, 0:D], xt2[:, i, :], ALU.add))
    layer_norm(xh, xt2, [t])
    for i in range(NT):
        affine(xh, xh, "g_norm_out", "b_norm_out", i)
        seq(lambda: dve.tensor_tensor(x[:, i, :], x[:, i, :], xh[:, i, :], ALU.add))
    t_x4 = DV.last()
    phase_ends()
    phase_ends()

    HR, DR = 8, 32
    phase_begins()
    xr = xn
    t_xn = layer_norm(xr, x, [t_x4])
    t_xT = features_on_partitions(xT, lambda i, kt: xr[:, i, kt * P:(kt + 1) * P], [t_xn], [])
    wr_ = {c: sb(f"wr_{c}", [P, 2, D]) for c in "QKVGO"}
    wsw = {c: sb(f"wsw_{c}", [P, 2, D]) for c in "QK"}
    rtab = sb("rtab", [P, 4, 2, S])
    rmask = sb("rmask", [P, 3, P])
    gnv = sb("gnv", [P, 2, D])
    pairs = [(wr_[c][:, k, :].rearrange("p (h e) -> p h e", h=HR), ins["L1_attn_W_" + c][:, k * P:(k + 1) * P, :].rearrange("h p e -> p h e"))
             for c in "QKV" for k in range(2)]
    pairs += [(wr_[c][:, :, :], ins["L1_attn_W_" + c].rearrange("(k p) n -> p k n", p=P)) for c in "GO"]
    pairs += [(rtab[:, k, :, :], ins["rotary"][k].rearrange("(t p) n -> p t n", p=P)) for k in range(4)]
    pairs += [(gnv[:, k, :], row("L1_attn_gn_" + n).to_broadcast([P, D])) for k, n in enumerate(("weight", "bias"))]
    t_w = load("ld_ret", pairs)
    t = PO.done(pool.memset(rmask[:, :, :], 1.0))
    PO.after(t)
    for k in (0, 2):
        t_rm = PO.done(pool.affine_select(out=rmask[:, k, :], in_=rmask[:, k, :], compare_op=ALU.is_ge, fill=0.0, base=0,
                                          pattern=[[1, P]], channel_multiplier=-1))
    DV.after(t_w)
    for c in "QK":
        for par in range(2):
            t_sw = DV.done(dve.tensor_copy(wsw[c][:, :, :].rearrange("p k (e two) -> p (k e) two", two=2)[:, :, par],
                                           wr_[c][:, :, :].rearrange("p k (e two) -> p (k e) two", two=2)[:, :, 1 - par]))
    qkr = {c: sb(f"qkr_{c}", [P, 2, T]) for c in "QK"}
    rtmp = sb("rtmp", [P, T])
    PE.after(t_w, t_sw, t_xT)
    last_rot = {}
    for n_, c in enumerate("QK"):
        for m in range(2):
            b0 = 2 * m
            if n_:
                PE.after(last_rot[m])
            for k, w in enumerate((wr_[c], wsw[c])):
                for kt in range(2):
                    t = pe.matmul(bank[:, b0 + k, :], w[:, kt, m * P:(m + 1) * P], xT[:, kt, :], start=(kt == 0), stop=(kt == 1))
            t = PE.done(t)
            DV.after(t)
            ctab, stab = (rtab[:, 2 * n_ + k, m:m + 1, :].to_broadcast([P, NB, S]) for k in range(2))
            v3 = lambda a: a.rearrange("p (b s) -> p b s", b=NB)
            last_rot[m] = seq(lambda: dve.tensor_tensor(v3(qkr[c][:, m, :]), v3(bank[:, b0, :]), ctab, ALU.mult),
                              lambda: dve.tensor_tensor(v3(rtmp[:, :]), v3(bank[:, b0 + 1, :]), stab, ALU.mult),
                              lambda: dve.tensor_tensor(qkr[c][:, m, :], qkr[c][:, m, :], rtmp[:, :], ALU.add))
    t_rot = DV.last()
    vr = sb("vr", [P, NT, D])
    gr = sb("gr", [P, NT, D])
    for i in range(NT):
        for k, w in enumerate((wr_["V"], wr_["G"])):
            for kt in range(2):
                t = pe.matmul(bank[:, 4 + i, k * D:(k + 1) * D], xT[:, kt, i * P:(i + 1) * P], w[:, kt, :], start=(kt == 0), stop=(kt == 1))
        t = PE.done(t)
        AC.after(t)
        AC.done(act.copy(vr[:, i, :], bank[:, 4 + i, 0:D]))
        t_v = AC.done(act.activation(gr[:, i, :], bank[:, 4 + i, D:2 * D], ACT.Silu))
    sR = [sb(f"sR{j}", [P, 3, P]) for j in range(2)]
    yr = sb("yr", [P, NT, HR, DR])
    PE.after(t_rot, t_v)
    DV.after(t_rm)
    masked, used, y_read = {}, {}, {}
    for b in range(NB):
        for h in range(HR):
            j = h % 2
            if j in masked:
                PE.after(masked[j])
            rs = slice((h % 4) * DR, (h % 4 + 1) * DR)
            kq = lambda c, lo, n: qkr[c][rs, h // 4, b * S + lo:b * S + lo + n]
            pe.matmul(bank[:, j, 0:2 * P], kq("K", 0, P), kq("Q", 0, 2 * P), start=True, stop=True)
            t = PE.done(pe.matmul(bank[:, j, 2 * P:3 * P], kq("K", P, P), kq("Q", P, P), start=True, stop=True))
            DV.after(t)
            if j in used:
                DV.after(used[j])
            masked[j] = DV.done(dve.tensor_tensor(sR[j][:, :, :].rearrange("p c q -> p (c q)"), bank[:, j, 0:3 * P],
                                                  rmask[:, :, :].rearrange("p c q -> p (c q)"), ALU.mult))
            PE.after(masked[j])
            if b and h == 0:
                PE.after(y_read[0], y_read[1])
            vv = lambda kt: vr[:, b * 2 + kt, h * DR:(h + 1) * DR]
            o = [bank[:, 2 + qt, h * DR:(h + 1) * DR] for qt in range(2)]
            pe.matmul(o[0], sR[j][:, 0, :], vv(0), start=True, stop=True)
            pe.matmul(o[1], sR[j][:, 1, :], vv(0), start=True, stop=False)
            used[j] = PE.done(pe.matmul(o[1], sR[j][:, 2, :], vv(1), start=False, stop=True))
        for qt in range(2):
            AC.after(used[1])
            y_read[qt] = AC.done(act.copy(yr[:, b * 2 + qt, :, :].rearrange("p h d -> p (h d)"), bank[:, 2 + qt, 0:D]))
    gm, gv = sb("gm", [P, NT * HR]), sb("gv", [P, NT * HR])
    ysq = sb("ysq", [P, NT * HR, DR])
    y3 = yr[:, :, :, :].rearrange("p t h d -> p (t h) d")
    gb = lambda a: a[:, :].rearrange("p (n a) -> p n a", a=1).to_broadcast([P, NT * HR, DR])
    DV.after(y_read[0], y_read[1])
    t = seq(lambda: dve.tensor_reduce(gm[:, :], y3, AX.X, ALU.add),
            lambda: dve.tensor_scalar(gm[:, :], gm[:, :], 1.0 / DR, None, ALU.mult),
            lambda: dve.tensor_tensor(y3, y3, gb(gm), ALU.subtract),
            lambda: dve.tensor_tensor(ysq[:, :, :], y3, y3, ALU.mult),
            lambda: dve.tensor_reduce(gv[:, :], ysq[:, :, :], AX.X, ALU.add),
            lambda: dve.tensor_scalar(gv[:, :], gv[:, :], 1.0 / DR, EPS, ALU.mult, ALU.add))
    AC.after(t)
    t = AC.done(act.sqrt(gv[:, :], gv[:, :]))
    DV.after(t)
    seq(lambda: dve.reciprocal(gv[:, :], gv[:, :]),
        lambda: dve.tensor_tensor(y3, y3, gb(gv), ALU.mult))
    for i in range(NT):
        yi = yr[:, i, :, :].rearrange("p h d -> p (h d)")
        seq(lambda: dve.tensor_tensor(yi, yi, gnv[:, 0, :], ALU.mult),
            lambda: dve.tensor_tensor(yi, yi, gnv[:, 1, :], ALU.add),
            lambda: dve.tensor_tensor(yi, yi, gr[:, i, :], ALU.mult))
    t_yT = features_on_partitions(xT, lambda i, kt: yr[:, i, :, :].rearrange("p h d -> p (h d)")[:, kt * P:(kt + 1) * P],
                                  [DV.last()], [t_rot])
    t_x5 = add_to_x(project_tokens(xT, wr_["O"], None, [t_yT, t_v], first_bank=4), first_bank=4)
    phase_ends()

    KA = 8
    phase_begins()
    ids = sb("ids", [1, KA], I32)
    wts = sb("wts", [P, KA])
    wsel = sb("wsel", [P, KA, 2, D])
    bsel = sb("bsel", [1, KA, D])
    wmix = sb("wmix", [P, 2, D])
    wmT = sb("wmT", [P, 2, D])
    bmix = sb("bmix", [1, D])
    t_ids = load("ld_ids", [(ids[:, :], row("L1_ffn_ids")), (wts[:, :], row("L1_ffn_weights").to_broadcast([P, KA]))])
    sp.wait_ge(*t_ids)
    ld = Load(nc, "ld_sel")
    for k in range(KA):
        a = sp.value_load(ids[0:1, k:k + 1], min_val=0, max_val=31)
        ld.add(sp.dma_start(wsel[:, k, :, :], ins["L1_ffn_W"][bass.ds(a, 1), :, :].rearrange("a (t p) d -> p (a t) d", p=P)))
        ld.add(sp.dma_start(bsel[:, k, :], ins["L1_ffn_b"][bass.ds(a, 1), :]))
    t_xn = layer_norm(xn, x, [t_x5])
    t_xT = features_on_partitions(xT, lambda i, kt: xn[:, i, kt * P:(kt + 1) * P], [t_xn], [])
    DV.after(ld.token(), t_ids)
    flat = lambda t: t.rearrange("p t d -> p (t d)")
    seq(lambda: dve.tensor_scalar(flat(wmix[:, :, :]), flat(wsel[:, 0, :, :]), wts[:, 0:1], None, ALU.mult))
    seq(lambda: dve.tensor_scalar(bmix[:, :], bsel[:, 0, :], wts[0:1, 0:1], None, ALU.mult))
    for k in range(1, KA):
        seq(lambda: dve.scalar_tensor_tensor(flat(wmix[:, :, :]), flat(wsel[:, k, :, :]), wts[:, k:k + 1], flat(wmix[:, :, :]), ALU.mult, ALU.add))
        seq(lambda: dve.scalar_tensor_tensor(bmix[:, :], bsel[:, k, :], wts[0:1, k:k + 1], bmix[:, :], ALU.mult, ALU.add))
    PE.after(DV.last())
    for kt in range(2):
        for ot in range(2):
            t = PE.done(pe.transpose(bank[:, 2 + kt, ot * P:(ot + 1) * P], wmix[:, ot, kt * P:(kt + 1) * P], ident[:, :]))
        AC.after(t)
        t_wm = AC.done(act.copy(wmT[:, kt, :], bank[:, 2 + kt, 0:D]))
    t_x6 = add_to_x(project_tokens(xT, wmT, bmix[0:1, :], [t_wm, t_xT], first_bank=4), first_bank=4)

    sp.wait_ge(*t_x6)
    done = Load(nc, "stored")
    done.add(sp.dma_start(out.rearrange("b (t p) d -> p (b t) d", p=P), x[:, :, :]))
    sp.wait_ge(*done.token())


def kernel(**inputs):
    import numpy as _np
    import concourse.bacc as _bacc
    from concourse.bass_utils import run_bass_kernel_spmd as _run

    nc = _bacc.Bacc("TRN2", target_bir_lowering=False, num_devices=1)
    arrays, aps = {}, {}
    for name in inputs:
        a = _np.ascontiguousarray(inputs[name])
        if a.shape == ():
            a = a.reshape(1)
        if a.dtype == _np.bool_:
            a = a.view(_np.uint8)
        arrays["in_" + name] = a
        aps[name] = nc.dram_tensor("in_" + name, a.shape, mybir.dt.from_np(a.dtype), kind="ExternalInput").ap()
    for name, a in constants().items():
        arrays["in_" + name] = a
        aps[name] = nc.dram_tensor("in_" + name, a.shape, mybir.dt.from_np(a.dtype), kind="ExternalInput").ap()
    out = nc.dram_tensor("out_x", (NB, S, D), F32, kind="ExternalOutput").ap()
    build(nc, aps, out)
    r = _run(nc, [arrays], core_ids=[0])
    return r.results[0]["out_x"]
```
